# Optimizing a Trainium2 kernel written in Bass

```python
import numpy as np
import jax
import jax.numpy as jnp

def _softmax(x, axis=-1):
    return jax.nn.softmax(x, axis=axis)

def _gelu(x):
    return jax.nn.gelu(x, approximate=True)

def _silu(x):
    return jax.nn.silu(x)

def _sigmoid(x):
    return jax.nn.sigmoid(x)

def _layernorm(x, axis=-1, eps=1e-05):
    m = jnp.mean(x, axis=axis, keepdims=True)
    v = jnp.var(x, axis=axis, keepdims=True)
    return (x - m) / jnp.sqrt(v + eps)

def _scatter_add(tgt, idx, src, axis=0):
    return tgt.at[idx].add(src)

def _segment_sum(src, seg, n):
    return jax.ops.segment_sum(src, seg, n)
kernel_name = 'mk_adj_resnorm_d4_adj_r2_d854c2'

def setup_inputs(seed: int=0):
    np.random.seed(seed)
    _w = jnp.asarray

    def _rec_inputs():
        import jax
        import jax.numpy as jnp
        _gk = jax.random.key(seed)
        x = 7.22e-05 + 1 * jax.random.normal(jax.random.fold_in(_gk, 1), (64, 128, 256), jnp.float32)
        _a = jax.random.bernoulli(jax.random.fold_in(_gk, 2), 0.125, (128, 128))
        _a = jnp.logical_or(_a, jnp.swapaxes(_a, -1, -2))
        _a = jnp.logical_or(_a, jnp.eye(128, dtype=bool))
        adj = _a.astype(jnp.int32)
        return (x, adj)
    x, adj = _rec_inputs()

    def _L0_gnn_setup():
        import jax, jax.numpy as jnp
        import numpy as np
        B, N, D = (8, 1024, 256)
        NEG_SLOPE = 0.2
        key = jax.random.key(seed)
        k1, k2, k3, k4, k5 = jax.random.split(key, 5)
        x = jax.random.normal(k1, (B, N, D), dtype=jnp.float32)
        adj = jax.random.randint(k2, (N, N), 0, 2, dtype=jnp.int32)
        adj = jnp.maximum(adj, jnp.eye(N, dtype=jnp.int32))
        W = jax.random.normal(k3, (D, D), dtype=jnp.float32) * (1.0 / np.sqrt(D))
        a_src = jax.random.normal(k4, (D,), dtype=jnp.float32) * (1.0 / np.sqrt(D))
        a_dst = jax.random.normal(k5, (D,), dtype=jnp.float32) * (1.0 / np.sqrt(D))
        return {'x': x, 'adj': adj, 'W': W, 'a_src': a_src, 'a_dst': a_dst}
    _L0_gnn_all = _L0_gnn_setup()
    _L0_gnn_in = {k: v for k, v in _L0_gnn_all.items() if k in ('W', 'a_src', 'a_dst')}
    del _L0_gnn_all

    def _L1_gnn_setup():
        import jax, jax.numpy as jnp
        import numpy as np
        D_MODEL = 256
        NUM_HEADS = 8
        D_HEAD = D_MODEL // NUM_HEADS
        B, N = (4, 1024)
        key = jax.random.key(seed)
        ks = jax.random.split(key, 10)
        s = 1.0 / np.sqrt(D_MODEL)
        inp = {'h': jax.random.normal(ks[0], (B, N, D_MODEL), dtype=jnp.float32), 'adj': jax.random.randint(ks[1], (N, N), 0, 2, dtype=jnp.int32), 'Wq': jax.random.uniform(ks[2], (D_MODEL, D_MODEL), jnp.float32, -s, s), 'bq': jax.random.uniform(ks[3], (D_MODEL,), jnp.float32, -s, s), 'Wk': jax.random.uniform(ks[4], (D_MODEL, D_MODEL), jnp.float32, -s, s), 'bk': jax.random.uniform(ks[5], (D_MODEL,), jnp.float32, -s, s), 'Wv': jax.random.uniform(ks[6], (D_MODEL, D_MODEL), jnp.float32, -s, s), 'bv': jax.random.uniform(ks[7], (D_MODEL,), jnp.float32, -s, s), 'Wo': jax.random.uniform(ks[8], (D_MODEL, D_MODEL), jnp.float32, -s, s), 'bo': jax.random.uniform(ks[9], (D_MODEL,), jnp.float32, -s, s)}
        return inp
    _L1_gnn_all = _L1_gnn_setup()
    _L1_gnn_in = {k: v for k, v in _L1_gnn_all.items() if k in ('Wq', 'bq', 'Wk', 'bk', 'Wv', 'bv', 'Wo', 'bo')}
    del _L1_gnn_all

    def _L2_gnn_setup():
        import jax, jax.numpy as jnp
        import numpy as np
        LEAKY_ALPHA = 0.01
        NEG_INF = -1000000000.0
        LN_EPS = 1e-05

        def _gat_heads(x, adj, W, a):
            O = W.shape[-1]
            Wh = jnp.einsum('bnf,hfo->bhno', x, W)
            f1 = jnp.einsum('bhno,ho->bhn', Wh, a[:, :O])
            f2 = jnp.einsum('bhno,ho->bhn', Wh, a[:, O:])
            e = f1[:, :, :, None] + f2[:, :, None, :]
            e = jnp.where(e > 0, e, LEAKY_ALPHA * e)
            e = jnp.where(adj[None, None] > 0, e, NEG_INF)
            attn = jax.nn.softmax(e, axis=-1)
            return jnp.einsum('bhnm,bhmo->bhno', attn, Wh)
        key = jax.random.key(seed)
        ks = jax.random.split(key, 10)
        B, N, F_in, F_hid, H, F_out, D_ff = (8, 1024, 256, 256, 4, 256, 256)
        s = 0.05
        return {'enc_inputs': jax.random.normal(ks[0], (B, N, F_in), jnp.float32), 'adj': jax.random.randint(ks[1], (N, N), 0, 2, jnp.int32), 'W_heads': jax.random.normal(ks[2], (H, F_in, F_hid), jnp.float32) * s, 'a_heads': jax.random.normal(ks[3], (H, 2 * F_hid), jnp.float32) * s, 'W_out': jax.random.normal(ks[4], (H * F_hid, F_out), jnp.float32) * s, 'a_out': jax.random.normal(ks[5], (2 * F_out,), jnp.float32) * s, 'w1': jax.random.normal(ks[6], (F_out, D_ff), jnp.float32) * s, 'b1': jnp.zeros((D_ff,), jnp.float32), 'w2': jax.random.normal(ks[7], (D_ff, F_out), jnp.float32) * s, 'b2': jnp.zeros((F_out,), jnp.float32), 'ln_gamma': jnp.ones((F_out,), jnp.float32), 'ln_beta': jnp.zeros((F_out,), jnp.float32)}
    _L2_gnn_all = _L2_gnn_setup()
    _L2_gnn_in = {k: v for k, v in _L2_gnn_all.items() if k in ('W_heads', 'a_heads', 'W_out', 'a_out', 'w1', 'b1', 'w2', 'b2', 'ln_gamma', 'ln_beta')}
    del _L2_gnn_all

    def _L3_gnn_setup():
        import jax, jax.numpy as jnp
        import numpy as np
        B, K, DIN, DOUT = (32, 64, 256, 256)
        key = jax.random.key(seed)
        k1, k2, k3, k4 = jax.random.split(key, 4)
        x = jax.random.normal(k1, (B, K, DIN), dtype=jnp.float32)
        adj = jax.random.randint(k2, (K, K), 0, 2, dtype=jnp.int32)
        W = jax.random.normal(k3, (DOUT, 2 * DIN), dtype=jnp.float32) * 0.02
        b = jax.random.normal(k4, (DOUT,), dtype=jnp.float32) * 0.02
        return {'x': x, 'adj': adj, 'W': W, 'b': b}
    _L3_gnn_all = _L3_gnn_setup()
    _L3_gnn_in = {k: v for k, v in _L3_gnn_all.items() if k in ('W', 'b')}
    del _L3_gnn_all
    return {'x': x, 'adj': adj, 'L0_gnn_W': _L0_gnn_in['W'], 'L0_gnn_a_src': _L0_gnn_in['a_src'], 'L0_gnn_a_dst': _L0_gnn_in['a_dst'], 'L1_gnn_Wq': _L1_gnn_in['Wq'], 'L1_gnn_bq': _L1_gnn_in['bq'], 'L1_gnn_Wk': _L1_gnn_in['Wk'], 'L1_gnn_bk': _L1_gnn_in['bk'], 'L1_gnn_Wv': _L1_gnn_in['Wv'], 'L1_gnn_bv': _L1_gnn_in['bv'], 'L1_gnn_Wo': _L1_gnn_in['Wo'], 'L1_gnn_bo': _L1_gnn_in['bo'], 'L2_gnn_W_heads': _L2_gnn_in['W_heads'], 'L2_gnn_a_heads': _L2_gnn_in['a_heads'], 'L2_gnn_W_out': _L2_gnn_in['W_out'], 'L2_gnn_a_out': _L2_gnn_in['a_out'], 'L2_gnn_w1': _L2_gnn_in['w1'], 'L2_gnn_b1': _L2_gnn_in['b1'], 'L2_gnn_w2': _L2_gnn_in['w2'], 'L2_gnn_b2': _L2_gnn_in['b2'], 'L2_gnn_ln_gamma': _L2_gnn_in['ln_gamma'], 'L2_gnn_ln_beta': _L2_gnn_in['ln_beta'], 'L3_gnn_W': _L3_gnn_in['W'], 'L3_gnn_b': _L3_gnn_in['b']}

def reference(x, adj, L0_gnn_W, L0_gnn_a_src, L0_gnn_a_dst, L1_gnn_Wq, L1_gnn_bq, L1_gnn_Wk, L1_gnn_bk, L1_gnn_Wv, L1_gnn_bv, L1_gnn_Wo, L1_gnn_bo, L2_gnn_W_heads, L2_gnn_a_heads, L2_gnn_W_out, L2_gnn_a_out, L2_gnn_w1, L2_gnn_b1, L2_gnn_w2, L2_gnn_b2, L2_gnn_ln_gamma, L2_gnn_ln_beta, L3_gnn_W, L3_gnn_b):
    import jax
    import jax.numpy as jnp

    def _L0_gnn_ref(x, adj, W, a_src, a_dst):
        import jax, jax.numpy as jnp
        import numpy as np
        B, N, D = (8, 1024, 256)
        NEG_SLOPE = 0.2
        Wh = jnp.einsum('bnd,de->bne', x, W)
        e_src = jnp.einsum('bnd,d->bn', Wh, a_src)
        e_dst = jnp.einsum('bnd,d->bn', Wh, a_dst)
        logits = e_src[:, :, None] + e_dst[:, None, :]
        logits = jnp.where(logits >= 0, logits, NEG_SLOPE * logits)
        mask = (adj == 0)[None, :, :]
        logits = jnp.where(mask, -jnp.inf, logits)
        attn = jax.nn.softmax(logits, axis=-1)
        attn = jnp.nan_to_num(attn, nan=0.0)
        out = jnp.einsum('bnm,bmd->bnd', attn, Wh)
        return out

    def _L1_gnn_ref(h, adj, Wq, bq, Wk, bk, Wv, bv, Wo, bo):
        import jax, jax.numpy as jnp
        import numpy as np
        D_MODEL = 256
        NUM_HEADS = 8
        D_HEAD = D_MODEL // NUM_HEADS
        B, N = (4, 1024)
        b, n, _ = h.shape

        def split_heads(x):
            return x.reshape(b, n, NUM_HEADS, D_HEAD).transpose(0, 2, 1, 3)
        q = split_heads(h @ Wq.T + bq)
        k = split_heads(h @ Wk.T + bk)
        v = split_heads(h @ Wv.T + bv)
        scale = 1.0 / np.sqrt(D_HEAD)
        scores = jnp.einsum('bhqd,bhkd->bhqk', q, k) * scale
        mask = (adj == 0)[None, None, :, :]
        scores = jnp.where(mask, -jnp.inf, scores)
        attn = jax.nn.softmax(scores, axis=-1)
        out = jnp.einsum('bhqk,bhkd->bhqd', attn, v)
        out = out.transpose(0, 2, 1, 3).reshape(b, n, D_MODEL)
        return out @ Wo.T + bo

    def _L2_gnn_ref(enc_inputs, adj, W_heads, a_heads, W_out, a_out, w1, b1, w2, b2, ln_gamma, ln_beta):
        import jax, jax.numpy as jnp
        import numpy as np
        LEAKY_ALPHA = 0.01
        NEG_INF = -1000000000.0
        LN_EPS = 1e-05

        def _gat_heads(x, adj, W, a):
            O = W.shape[-1]
            Wh = jnp.einsum('bnf,hfo->bhno', x, W)
            f1 = jnp.einsum('bhno,ho->bhn', Wh, a[:, :O])
            f2 = jnp.einsum('bhno,ho->bhn', Wh, a[:, O:])
            e = f1[:, :, :, None] + f2[:, :, None, :]
            e = jnp.where(e > 0, e, LEAKY_ALPHA * e)
            e = jnp.where(adj[None, None] > 0, e, NEG_INF)
            attn = jax.nn.softmax(e, axis=-1)
            return jnp.einsum('bhnm,bhmo->bhno', attn, Wh)
        B, N, _ = enc_inputs.shape
        h = jax.nn.elu(_gat_heads(enc_inputs, adj, W_heads, a_heads))
        h = jnp.transpose(h, (0, 2, 1, 3)).reshape(B, N, -1)
        out = _gat_heads(h, adj, W_out[None], a_out[None])[:, 0]
        out = jax.nn.elu(out)
        ffn = jnp.maximum(out @ w1 + b1, 0.0) @ w2 + b2
        y = ffn + out
        mu = jnp.mean(y, axis=-1, keepdims=True)
        var = jnp.var(y, axis=-1, keepdims=True)
        return (y - mu) / jnp.sqrt(var + LN_EPS) * ln_gamma + ln_beta

    def _L3_gnn_ref(x, adj, W, b):
        import jax, jax.numpy as jnp
        import numpy as np
        B, K, DIN, DOUT = (32, 64, 256, 256)
        Din = x.shape[-1]
        Wi, Wj = (W[:, :Din], W[:, Din:])
        mi = jnp.einsum('bkd,od->bko', x, Wi)
        mj = jnp.einsum('bkd,od->bko', x, Wj)
        a = adj.astype(x.dtype)
        deg = a.sum(axis=1)
        out = deg[None, :, None] * (mi + b) + jnp.einsum('ij,bjo->bio', a, mj)
        return out
    x = _layernorm(x + _L0_gnn_ref(x, adj, L0_gnn_W, L0_gnn_a_src, L0_gnn_a_dst), axis=-1)
    x = _layernorm(x + _L1_gnn_ref(x, adj, L1_gnn_Wq, L1_gnn_bq, L1_gnn_Wk, L1_gnn_bk, L1_gnn_Wv, L1_gnn_bv, L1_gnn_Wo, L1_gnn_bo), axis=-1)
    x = _layernorm(x + _L2_gnn_ref(x, adj, L2_gnn_W_heads, L2_gnn_a_heads, L2_gnn_W_out, L2_gnn_a_out, L2_gnn_w1, L2_gnn_b1, L2_gnn_w2, L2_gnn_b2, L2_gnn_ln_gamma, L2_gnn_ln_beta), axis=-1)
    x = _layernorm(x + _L3_gnn_ref(x, adj, L3_gnn_W, L3_gnn_b), axis=-1)
    return x

_drawn_inputs = setup_inputs


def setup_inputs(seed=0):
    import zlib

    import numpy as np

    out = dict(_drawn_inputs(seed))
    spreads = {'L2_gnn_b1': (0.0, 0.1),
     'L2_gnn_b2': (0.0, 0.1),
     'L2_gnn_ln_gamma': (1.0, 0.2),
     'L2_gnn_ln_beta': (0.0, 0.1)}
    factors = {'L1_gnn_Wq': 3.321,
     'L1_gnn_bq': 8.0,
     'L1_gnn_Wk': 3.115,
     'L1_gnn_bk': 8.0,
     'L2_gnn_a_out': 3.37}
    for name, (base, spread) in spreads.items():
        noise = np.random.default_rng([zlib.crc32(name.encode()), seed]).standard_normal(out[name].shape)
        drawn = base * np.exp(spread * noise) if base else spread * noise
        out[name] = jnp.asarray(drawn.astype(out[name].dtype))
    for name, factor in factors.items():
        out[name] = (out[name] * factor).astype(out[name].dtype)
    return out
```

```python
from contextlib import ExitStack

import numpy as np

import concourse.bass as bass
from concourse import mybir

F32 = mybir.dt.float32
F32R = mybir.dt.float32r
I32 = mybir.dt.int32
ALU = mybir.AluOpType
ACT = mybir.ActivationFunctionType
AX = mybir.AxisListType.X

P = 128
D = 256
C = D // P
G = 2
H1 = 8
DH = D // H1
R = P // DH
H2 = 4
MASK = -1.0e9
EPS = 1e-5
SLOPE0, SLOPE2 = 0.2, 0.01
SCALE = 1.0 / float(np.sqrt(DH))

_COLS = [("W0", C * (D + 2)), ("Wq", C * D), ("Wk", C * D), ("Wv", C * D), ("Wo", C * D),
         ("Wh", H2 * C * D), ("Wout", H2 * C * (D + 2)), ("w1", C * D), ("w2", C * D),
         ("W3", C * 2 * D), ("Wa", C * P), ("adjT", P)]
OFF = {}
WTOT = 0
for _n, _w in _COLS:
    OFF[_n] = (WTOT, WTOT + _w)
    WTOT += _w
_ROWS = ["bo", "b2", "gamma", "beta", "b3"]


def build(nc, x_n, x_t, weights, adj, adj_t, att_rows, rows, cols, out):
    B = x_n.shape[0]
    NG = B // G
    xn_v = x_n.rearrange("(g b) n d -> g n b d", b=G)
    out_v = out.rearrange("(g b) n d -> g n b d", b=G)

    with ExitStack() as ctx:
        def sb(name, shape, dt=F32):
            return ctx.enter_context(nc.sbuf_tensor(name, shape, dt))

        def sem(name):
            return ctx.enter_context(nc.semaphore(name))

        ps = ctx.enter_context(nc.psum_tensor("ps", [P, 8, 512], F32))

        w_hi = sb("w_hi", [P, WTOT], F32R)
        w_lo = sb("w_lo", [P, WTOT], F32R)
        rowsb = sb("rowsb", [P, len(_ROWS), D])
        colsb = sb("colsb", [P, 4, C])
        ident = sb("ident", [P, P])
        mask = sb("mask", [P, P])
        mask2 = sb("mask2", [P, P])
        adj_i = sb("adj_i", [P, P], I32)
        adjt_i = sb("adjt_i", [P, P], I32)
        adj_f = sb("adj_f", [P, P])
        deg = sb("deg", [P, 1])
        valid = sb("valid", [P, 3])
        eps_t = sb("eps_t", [P, G])
        pow_t = sb("pow_t", [P, G])

        def view(t, name, *dims):
            a, b = OFF[name]
            v = t[:, a:b]
            if len(dims) == 2:
                return v.rearrange("p (a b) -> p a b", a=dims[0])
            if len(dims) == 3:
                return v.rearrange("p (a b c) -> p a b c", a=dims[0], b=dims[1])
            return v

        def both(name, *dims):
            return view(w_hi, name, *dims), view(w_lo, name, *dims)

        W0, Wq, Wk, Wv, Wo = both("W0", C, D + 2), both("Wq", C, D), both("Wk", C, D), both("Wv", C, D), both("Wo", C, D)
        WH, WOUT = both("Wh", H2, C, D), both("Wout", H2 * C, D + 2)
        W1, W2, W3, WA = both("w1", C, D), both("w2", C, D), both("W3", C, 2 * D), both("Wa", C, P)
        ADJT = view(w_hi, "adjT")
        row = {n: rowsb[:, k, :].unsqueeze(1).to_broadcast([P, G, D]) for k, n in enumerate(_ROWS)}
        BQ, BK, BV, B1 = range(4)

        xn = sb("xn", [P, G, D])
        xt = sb("xt", [P, C, G * P])
        m2, t2 = sb("m2", [P, G, H2, P]), sb("t2", [P, G, H2, P])
        he, hf = sb("he", [P, 2, C * G * P]), sb("hf", [P, 2, C * G * P])
        f_small, b_small, c_small = sb("f_small", [P, 8, G]), sb("b_small", [P, 8, G, H2]), sb("c_small", [P, 8, G])

        with nc.sbuf_tensor("w_raw", [P, WTOT], F32) as w_raw:
            pass

        xr = sb("xr", [P, G, D])
        xT = sb("xT_hi", [P, C, G * P], F32R), sb("xT_lo", [P, C, G * P], F32R)
        wh = sb("wh_hi", [P, G, D], F32R), sb("wh_lo", [P, G, D], F32R)
        val = wh
        qq = sb("q_hi", [P, C, G * P], F32R), sb("q_lo", [P, C, G * P], F32R)
        kk = sb("k_hi", [P, C, G * P], F32R), sb("k_lo", [P, C, G * P], F32R)
        qs = sb("q_stack", [3 * DH, R, C, G * P], F32R)
        ks = sb("k_stack", [3 * DH, R, C, G * P], F32R)
        oT = sb("oT_hi", [P, C, G * P], F32R), sb("oT_lo", [P, C, G * P], F32R)
        sm = sb("sm", [P, 2, R, P])
        pT = sb("pT_hi", [P, 2, R * P], F32R), sb("pT_lo", [P, 2, R * P], F32R)
        m0, t0 = sm[:, 0, 0:G], sm[:, 1, 0:G]
        p0 = tuple(t[:, 0, 0:G * P].rearrange("p (g n) -> p g n", g=G) for t in pT)
        ec0 = sb("ec0", [P, G, 2])
        s1max, s1neg, s1sum, s1rec = (sb("s1" + n, [P, 2, R]) for n in ("max", "neg", "sum", "rec"))
        f_bn, f_mv, f_rs = sb("f_bn", [P, 2, G, 6]), sb("f_mv", [P, 2, G, 2]), sb("f_rs", [P, 2, G])
        f_ve = sb("f_ve", [P, 2, G])

        xb = sb("xb", [P, G, D])
        x2 = sb("x2_hi", [P, G, D], F32R), sb("x2_lo", [P, G, D], F32R)
        bT = sb("bT_hi", [P, C, G * P], F32R), sb("bT_lo", [P, C, G * P], F32R)
        eT = sb("eT", [2 * H2, G * P])
        ec2 = sb("ec2", [P, G, 2 * H2])
        p2 = sb("p2_hi", [P, G, H2 * P], F32R), sb("p2_lo", [P, G, H2 * P], F32R)
        hT = sb("hT_hi", [P, H2, C, G * P], F32R), sb("hT_lo", [P, H2, C, G * P], F32R)
        wh3 = x2
        ec3 = sb("ec3", [P, G, 2])
        m3, t3 = m2[:, 0, 0:G], t2[:, 0, 0:G]
        p3 = tuple(t[:, 0, 0:G * P].rearrange("p (g n) -> p g n", g=G) for t in p2)
        ob = sb("ob", [P, G, D])
        oe = hf[:, 0].rearrange("p (g d) -> p g d", g=G)
        hid = sb("hid_hi", [P, C, G * P], F32R), sb("hid_lo", [P, C, G * P], F32R)
        hidf = he[:, 0].rearrange("p (c n) -> p c n", c=C)
        x3d = sb("x3d", [P, G, D])
        mj = tuple(t[:].rearrange("p c n -> p (c n)").rearrange("p (g d) -> p g d", g=G) for t in hid)
        b_bn, b_mv, b_rs = sb("b_bn", [P, 3, G, 6]), sb("b_mv", [P, 3, G, 2]), sb("b_rs", [P, 3, G])
        b_ve = sb("b_ve", [P, 3, G])

        names = """prep_dma prep prep_w prep_id x_in xt_in xt_hi xt_lo wh_ps wh_hi wh_lo ec0
            z0_ps g0_m g0_d g0_t g0_w g0_p g0_r p0_ps p0_hi p0_lo av0_ps
            y0 n0_st n0_mv n0_ve n0_rs x1 x1T_ps x1T_hi x1T_lo xr q_ps q_hi q_lo k_ps k_hi k_lo v_ps v_hi v_lo
            q_stack k_stack s_ps sm smax sneg s_p s_rec0 s_rec s_pn p1_ps p1_hi p1_lo o_ps o_hi o_lo wo_ps
            y1 n1_st n1_mv n1_ve n1_rs x2
            x2T_ps x2T_hi x2T_lo x2_hi x2_lo xb er_ps eT ec_ps ec2 z2_ps g2_m g2_d g2_t g2_w g2_p g2_r g2_pn
            p2_ps p2_hi p2_lo g_ps g_hi g_lo h_ps h_e h_e1 h_f h_hi h_lo wh3_ps wh3_hi wh3_lo ec3
            z3_ps g3_m g3_d g3_t g3_w g3_p g3_r p3_ps p3_hi p3_lo av3_ps o3_e o3_e1 o3_z o3
            oT_ps oT_hi oT_lo ob f1_ps hid_hi hid_f hid_lo f2_ps y2 n2_st n2_mv n2_ve n2_rs n2 n2g y3
            n3_st n3_mv n3_ve n3_rs x3 x3T_ps x3T_hi x3T_lo x3d mm_ps x3m mj_hi mj_lo am_ps
            y4 n4_st n4_mv n4_ve n4_rs x4 out""".split()
        S = {n: sem("s_" + n) for n in names}

        def three(pe, dst, a, b, start, stop):
            nc.tensor.matmul(dst, a[0], b[1], start=start, stop=False)
            nc.tensor.matmul(dst, a[1], b[0], start=False, stop=False)
            return nc.tensor.matmul(dst, a[0], b[0], start=False, stop=stop)

        def part(pair, *idx):
            return pair[0][idx], pair[1][idx]

        def f(ap):
            return ap.bitcast(F32)

        ALL = slice(None)

        def node(b):
            return slice(b * P, (b + 1) * P)

        def steps(front, back):
            f_names = ["x0", "wh", "g0a", "g0b", "g0c", "pt0", "av0", "n0", "x1T", "qk", "v",
                       "sA", "sB", "pA", "pB", "oA", "sC", "sD", "pC", "pD", "oB", "wo", "n1"]
            b_names = ["x2T", "er", "g2a", "g2b", "g2c", "g2d", "gx", "hT0", "hT1", "hT2", "hT3", "wh3",
                       "g3a", "g3b", "g3c", "pt3", "av3", "oT", "f1", "f2", "n2", "n3", "x3T", "mm", "am", "n4"]
            return ([("f", n) for n in f_names] if front else []) + ([("b", n) for n in b_names] if back else [])

        def run(table, i_front, i_back):
            for side, n in steps(i_front is not None, i_back is not None):
                if n in table:
                    table[n](i_front if side == "f" else i_back)

        block = ctx.enter_context(nc.Block())

        @block.sync
        def _(sp):
            for src, dst in ((weights, w_raw), (rows, rowsb), (cols, colsb), (adj, adj_i), (adj_t, adjt_i)):
                sp.dma_start(dst[:], src).then_inc(S["prep_dma"], 16)
            sp.dma_start(m2[:].rearrange("p g h n -> p (g h n)"), att_rows[:, 0:G * H2 * P]).then_inc(S["prep_dma"], 16)
            sp.dma_start(t2[:].rearrange("p g h n -> p (g h n)"), att_rows[:, G * H2 * P:2 * G * H2 * P]).then_inc(S["prep_dma"], 16)
            sp.dma_start(he[:].rearrange("p g n -> p (g n)"), att_rows[:, 2 * G * H2 * P:]).then_inc(S["prep_dma"], 16)

            def x0(i):
                sp.dma_start(xt[:].rearrange("p c n -> p (c n)"), x_t[i]).then_inc(S["xt_in"], 16)
                sp.dma_start(xn[:], xn_v[i]).then_inc(S["x_in"], 16)

            def x0_next(i):
                sp.wait_ge(S["xt_hi"], i + 1)
                sp.wait_ge(S["xt_lo"], i + 1)
                sp.dma_start(xt[:].rearrange("p c n -> p (c n)"), x_t[i + 1]).then_inc(S["xt_in"], 16)
                sp.wait_ge(S["x2T_ps"], i + 1)
                sp.wait_ge(S["x2_hi"], i + 1)
                sp.wait_ge(S["x2_lo"], i + 1)
                sp.wait_ge(S["xb"], i + 1)
                sp.dma_start(xn[:], xn_v[i + 1]).then_inc(S["x_in"], 16)

            def stack(i):
                for name, pair, dst, order in (("q", qq, qs, (0, 0, 1)), ("k", kk, ks, (0, 1, 0))):
                    sp.wait_ge(S[name + "_hi"], C * (i + 1))
                    sp.wait_ge(S[name + "_lo"], C * (i + 1))
                    for j, which in enumerate(order):
                        for r in range(R):
                            sp.dma_start(f(dst[DH * j:DH * (j + 1), r]), f(pair[which][DH * r:DH * (r + 1)])) \
                              .then_inc(S[name + "_stack"], 16)

            def store(i):
                sp.wait_ge(S["x4"], G * (i + 1))
                sp.dma_start(out_v[i], ob[:]).then_inc(S["out"], 16)

            x0(0)
            with_loop(nc, sp, NG, {"qk": stack, "n4": store}, run, after_load=x0_next)
            sp.wait_ge(S["out"], 16 * NG)

        @block.gpsimd
        def _(pool):
            nc.gpsimd.memset(ident[:], 0.0).then_inc(S["prep_id"], 1)
            nc.gpsimd.memset(eps_t[:], EPS).then_inc(S["prep_id"], 1)
            nc.gpsimd.memset(pow_t[:], -0.5).then_inc(S["prep_id"], 1)
            pool.wait_ge(S["prep_id"], 3)
            nc.gpsimd.affine_select(out=ident[:], in_=ident[:], compare_op=ALU.not_equal, fill=1.0, base=0,
                                    pattern=[[-1, P]], channel_multiplier=1).then_inc(S["prep_id"], 1)
            pool.wait_ge(S["prep"], 1)

            def rsqrt(i, n, mv, ve, rs):
                pool.wait_ge(S[n + "_mv"], G * (i + 1))
                nc.gpsimd.tensor_tensor(ve, mv[:, :, 1], eps_t[:], ALU.add).then_inc(S[n + "_ve"], 1)
                pool.wait_ge(S[n + "_ve"], i + 1)
                nc.gpsimd.tensor_tensor(rs, ve, pow_t[:], ALU.pow).then_inc(S[n + "_rs"], 1)

            def x0(i):
                pool.wait_ge(S["xt_hi"], i + 1)
                nc.gpsimd.tensor_tensor(xT[1][:], xt[:], f(xT[0][:]), ALU.subtract).then_inc(S["xt_lo"], 1)

            def n0(i):
                rsqrt(i, "n0", f_mv[:, 0], f_ve[:, 0], f_rs[:, 0])

            def x1T(i):
                pool.wait_ge(S["x1"], G * (i + 1))
                nc.gpsimd.tensor_tensor(xr[:], xn[:], row["bo"], ALU.add).then_inc(S["xr"], 1)

            def norm_probs(u):
                def fn(i):
                    pool.wait_ge(S["s_p"], R * (4 * i + u + 1))
                    pool.wait_ge(S["s_rec"], 4 * i + u + 1)
                    nc.gpsimd.tensor_tensor(sm[:, u % 2], sm[:, u % 2], s1rec[:, u % 2].unsqueeze(2).to_broadcast([P, R, P]),
                                            ALU.mult).then_inc(S["s_pn"], 1)
                return fn

            def n1(i):
                rsqrt(i, "n1", f_mv[:, 1], f_ve[:, 1], f_rs[:, 1])

            def x2T(i):
                pool.wait_ge(S["x2"], G * (i + 1))
                nc.gpsimd.tensor_tensor(xb[:], xn[:], row["beta"], ALU.add).then_inc(S["xb"], 1)
                pool.wait_ge(S["x2_hi"], i + 1)
                nc.gpsimd.tensor_tensor(x2[1][:], xn[:], f(x2[0][:]), ALU.subtract).then_inc(S["x2_lo"], 1)

            def g2c(i):
                for b in range(G):
                    pool.wait_ge(S["g2_p"], H2 * (G * i + b + 1))
                    pool.wait_ge(S["g2_r"], G * i + b + 1)
                    nc.gpsimd.tensor_tensor(t2[:, b], t2[:, b], b_small[:, 7, b].unsqueeze(2).to_broadcast([P, H2, P]),
                                            ALU.mult).then_inc(S["g2_pn"], 1)

            def h_low(h):
                def fn(i):
                    pool.wait_ge(S["h_hi"], H2 * i + h + 1)
                    nc.gpsimd.tensor_tensor(hT[1][:, h], hf[:, h % 2].rearrange("p (c n) -> p c n", c=C), f(hT[0][:, h]),
                                            ALU.subtract).then_inc(S["h_lo"], 1)
                return fn

            def oT_(i):
                pool.wait_ge(S["oT_ps"], i + 1)
                nc.gpsimd.tensor_tensor(ob[:], ob[:], row["b2"], ALU.add).then_inc(S["ob"], 1)

            def n2(i):
                rsqrt(i, "n2", b_mv[:, 0], b_ve[:, 0], b_rs[:, 0])
                pool.wait_ge(S["n2"], G * (i + 1))
                nc.gpsimd.tensor_tensor(ob[:], ob[:], row["gamma"], ALU.mult).then_inc(S["n2g"], 1)
                pool.wait_ge(S["n2g"], i + 1)
                nc.gpsimd.tensor_tensor(ob[:], ob[:], xb[:], ALU.add).then_inc(S["y3"], 1)

            def n3(i):
                rsqrt(i, "n3", b_mv[:, 1], b_ve[:, 1], b_rs[:, 1])

            def x3T(i):
                pool.wait_ge(S["x3"], G * (i + 1))
                nc.gpsimd.tensor_tensor(x3d[:], ob[:], row["b3"], ALU.add).then_inc(S["x3d"], 1)

            def n4(i):
                rsqrt(i, "n4", b_mv[:, 2], b_ve[:, 2], b_rs[:, 2])

            with_loop(nc, pool, NG, {
                "x0": x0, "n0": n0, "x1T": x1T, "pA": norm_probs(0), "pB": norm_probs(1), "pC": norm_probs(2),
                "pD": norm_probs(3), "n1": n1, "x2T": x2T, "g2c": g2c, "hT0": h_low(0), "hT1": h_low(1),
                "hT2": h_low(2), "hT3": h_low(3), "oT": oT_, "n2": n2, "n3": n3, "x3T": x3T, "n4": n4}, run)

        @block.scalar
        def _(act):
            act.wait_ge(S["prep"], 1)

            def high(name, count, dst, src, ready, func=ACT.Identity, **kw):
                act.wait_ge(S[ready], count)
                nc.scalar.activation(dst, src, func, **kw).then_inc(S[name], 1)

            def whh(i, n, pair, bank0):
                for b in range(G):
                    high(n + "_hi", G * i + b + 1, pair[0][:, b], ps[:, bank0 + b, 0:D], n + "_ps")

            def scaled(i, n, small, m, t, slope, T, b=0, G_=1):
                act.wait_ge(S[n + "_d"], 6 * (G_ * i + b + 1))
                for k in range(T):
                    nc.scalar.activation(t[:, k], m[:, k], ACT.Identity, bias=small(5)[:, k:k + 1], scale=slope) \
                      .then_inc(S[n + "_t"], 1)

            def exps(i, n, small, m, t, T, b=0, G_=1):
                for k in range(T):
                    act.wait_ge(S[n + "_w"], T * (G_ * i + b) + k + 1)
                    nc.scalar.activation(t[:, k], m[:, k], ACT.Exp, accum_out=small(6)[:, k:k + 1]) \
                      .then_inc(S[n + "_p"], 1)

            s0 = lambda j: f_small[:, j]
            s3 = lambda j: c_small[:, j]

            def wh_(i):
                whh(i, "wh", wh, 0)

            def g0b(i):
                scaled(i, "g0", s0, m0, t0, SLOPE0, G)

            def g0c(i):
                exps(i, "g0", s0, m0, t0, G)

            def pt0(i):
                high("p0_hi", i + 1, p0[0][:].rearrange("p g n -> p (g n)"), ps[:, 3, 0:G * P], "p0_ps")

            def x1T(i):
                high("x1T_hi", i + 1, xT[0][:].rearrange("p c n -> p (c n)"), ps[:, 2, :], "x1T_ps")

            def qk(i):
                for n, pair, bank, bias in (("q", qq, 3, BQ), ("k", kk, 0, BK)):
                    for t in range(C):
                        high(n + "_hi", C * (i + 1), pair[0][:, t], ps[:, bank, t * G * P:(t + 1) * G * P], n + "_ps",
                             bias=colsb[:, bias, t:t + 1])

            def v(i):
                high("v_hi", G * (i + 1), val[0][:].rearrange("p g d -> p (g d)"), ps[:, 1, :], "v_ps")

            def probs(u):
                def fn(i):
                    act.wait_ge(S["sneg"], 4 * i + u + 1)
                    for r in range(R):
                        nc.scalar.activation(sm[:, u % 2, r], sm[:, u % 2, r], ACT.Exp, bias=s1neg[:, u % 2, r:r + 1],
                                             scale=SCALE, accum_out=s1sum[:, u % 2, r:r + 1]).then_inc(S["s_p"], 1)
                return fn

            def probsT(u):
                def fn(i):
                    high("p1_hi", 4 * i + u + 1, pT[0][:, u % 2], ps[:, u % 2, :], "p1_ps")
                return fn

            def heads_out(t):
                def fn(i):
                    act.wait_ge(S["o_ps"], 4 * i + G * (t + 1))
                    for r in range(R):
                        q = slice(DH * r, DH * (r + 1))
                        nc.scalar.activation(oT[0][q, t].rearrange("p (g n) -> p g n", g=G), ps[q, 0:G, r * P:(r + 1) * P],
                                             ACT.Identity, bias=colsb[q, BV, t:t + 1]).then_inc(S["o_hi"], 1)
                return fn

            def both_(*fns):
                def fn(i):
                    for g in fns:
                        g(i)
                return fn

            def x2T(i):
                act.wait_ge(S["x2"], G * (i + 1))
                nc.scalar.activation(x2[0][:], xn[:], ACT.Identity).then_inc(S["x2_hi"], 1)
                high("x2T_hi", i + 1, bT[0][:].rearrange("p c n -> p (c n)"), ps[:, 4, :], "x2T_ps")

            def g2b(i):
                for b in range(G):
                    scaled(i, "g2", lambda j: b_small[:, j, b], m2[:, b], t2[:, b], SLOPE2, H2, b, G)

            def g2c(i):
                for b in range(G):
                    exps(i, "g2", lambda j: b_small[:, j, b], m2[:, b], t2[:, b], H2, b, G)

            def g2d(i):
                for b in range(G):
                    high("p2_hi", G * i + b + 1, p2[0][:, b], ps[:, 6 + b, :], "p2_ps")

            def gx(i):
                for b in range(G):
                    for c in range(C):
                        high("g_hi", C * (G * i + b) + c + 1, hT[0][:, :, c, node(b)],
                             ps[:, 4 + 2 * b + c, :].rearrange("p (h n) -> p h n", h=H2), "g_ps")

            def hT_(h):
                def fn(i):
                    high("h_e", H2 * i + h + 1, he[:, h % 2], ps[:, 4 + h, :], "h_ps", ACT.Exp)
                    act.wait_ge(S["h_f"], H2 * i + h + 1)
                    nc.scalar.activation(hT[0][:, h].rearrange("p c n -> p (c n)"), hf[:, h % 2], ACT.Identity) \
                      .then_inc(S["h_hi"], 1)
                return fn

            def wh3_(i):
                whh(i, "wh3", wh3, 4)

            def g3b(i):
                scaled(i, "g3", s3, m3, t3, SLOPE2, G)

            def g3c(i):
                exps(i, "g3", s3, m3, t3, G)

            def pt3(i):
                high("p3_hi", i + 1, p3[0][:].rearrange("p g n -> p (g n)"), ps[:, 7, 0:G * P], "p3_ps")

            def av3(i):
                act.wait_ge(S["g3_r"], i + 1)
                for b in range(G):
                    high("o3_e", G * (i + 1), oe[:, b], ps[:, 4, b * D:(b + 1) * D], "av3_ps", ACT.Exp,
                         scale=c_small[:, 7, b:b + 1])

            def oT_(i):
                high("oT_hi", i + 1, bT[0][:].rearrange("p c n -> p (c n)"), ps[:, 5, :], "oT_ps")

            def f1(i):
                for t in range(C):
                    high("hid_hi", C * (i + 1), hid[0][:, t], ps[:, 6, t * G * P:(t + 1) * G * P], "f1_ps", ACT.Relu,
                         bias=colsb[:, B1, t:t + 1])

            def x3T(i):
                high("x3T_hi", i + 1, bT[0][:].rearrange("p c n -> p (c n)"), ps[:, 4, :], "x3T_ps")

            def mm(i):
                for b in range(G):
                    high("mj_hi", G * i + b + 1, mj[0][:, b], ps[:, 5 + b, D:2 * D], "mm_ps")

            with_loop(nc, act, NG, {
                "wh": wh_, "g0b": g0b, "g0c": g0c, "pt0": pt0, "x1T": x1T, "qk": qk, "v": v,
                "sA": probs(0), "sB": probs(1), "sC": probs(2), "sD": probs(3),
                "pA": probsT(0), "pB": probsT(1), "pC": probsT(2), "pD": probsT(3),
                "oA": heads_out(0), "oB": heads_out(1),
                "x2T": x2T, "g2b": g2b, "g2c": g2c, "g2d": g2d, "gx": gx, "hT0": hT_(0), "hT1": hT_(1),
                "hT2": hT_(2), "hT3": hT_(3), "wh3": wh3_, "g3b": g3b, "g3c": g3c, "pt3": pt3, "av3": av3,
                "oT": oT_, "f1": f1, "x3T": x3T, "mm": mm}, run)

        @block.vector
        def _(dve):
            V = nc.vector
            dve.wait_ge(S["prep_dma"], 16 * 8)
            chain = [0]

            def link(ins):
                chain[0] += 1
                ins.then_inc(S["prep_w"], 1)
                dve.wait_ge(S["prep_w"], chain[0])

            rows0 = m2[:].rearrange("p g h n -> p (g h n)"), t2[:].rearrange("p g h n -> p (g h n)"), he[:].rearrange("p g n -> p (g n)")

            def att(k):
                per = G * H2 * P // D
                return rows0[k // per][:, (k % per) * D:(k % per + 1) * D]

            scr = hf[:, 0, 0:D]
            raw0, rawo = view(w_raw, "W0", C, D + 2), view(w_raw, "Wout", H2 * C, D + 2)
            rawh, rawa = view(w_raw, "Wh", H2, C, D), view(w_raw, "Wa", C, P)

            def product(weight, k, dst):
                link(V.tensor_tensor_reduce(out=scr, in0=weight, in1=att(k), scale=1.0, scalar=0.0, op0=ALU.mult,
                                            op1=ALU.add, accum_out=dst))

            for s in range(2):
                for c in range(C):
                    product(raw0[:, c, 0:D], s, raw0[:, c, D + s:D + s + 1])
                for c in range(H2 * C):
                    product(rawo[:, c, 0:D], 2 + s, rawo[:, c, D + s:D + s + 1])
                for h in range(H2):
                    for c in range(C):
                        product(rawh[:, h, c], 4 + 2 * h + s, rawa[:, c, s * H2 + h:s * H2 + h + 1])
            link(V.tensor_copy(view(w_raw, "adjT"), adjt_i[:]))
            link(V.tensor_copy(adj_f[:], adj_i[:]))
            link(V.tensor_scalar(mask[:], adj_f[:], 0.0, MASK, ALU.is_equal, ALU.mult))
            link(V.tensor_scalar(mask2[:], adj_f[:], 0.0, MASK, ALU.is_le, ALU.mult))
            link(V.reduce_sum(deg[:], adj_f[:], axis=AX))
            link(V.tensor_reduce(valid[:, 0:1], mask[:], AX, ALU.max))
            link(V.tensor_scalar(valid[:, 1:2], valid[:, 0:1], 0.0, None, ALU.is_equal))
            link(V.reciprocal(valid[:, 0:1], valid[:, 1:2]))
            link(V.tensor_tensor(valid[:, 2:3], valid[:, 0:1], valid[:, 1:2], ALU.mult))
            link(V.tensor_scalar(rowsb[:, 4], rowsb[:, 4], deg[:], None, ALU.mult))
            link(V.tensor_copy(w_hi[:], w_raw[:]))
            link(V.tensor_tensor(w_lo[:], w_raw[:], f(w_hi[:]), ALU.subtract))
            dve.wait_ge(S["prep_id"], 4)
            V.memset(c_small[:], 0.0).then_inc(S["prep"], 1)

            def low(name, count, dst, src, high_, ready, hi_count=None):
                dve.wait_ge(S[ready], count if hi_count is None else hi_count)
                V.tensor_tensor(dst, src, f(high_), ALU.subtract).then_inc(S[name], 1)

            def edge_columns(i, n, ec, pair, bank0, e_name):
                for b in range(G):
                    dve.wait_ge(S[n + "_hi"], G * i + b + 1)
                    V.tensor_copy(ec[:, b], ps[:, bank0 + b, D:D + 2]).then_inc(S[e_name], 1)
                for b in range(G):
                    low(n + "_lo", G * i + b + 1, pair[1][:, b], ps[:, bank0 + b, 0:D], pair[0][:, b], n + "_hi")

            def front_of_softmax(k, n, small, z, msk, m, es, slope, T):
                V.tensor_tensor(m, z, msk[:].unsqueeze(1).to_broadcast([P, T, P]), ALU.add).then_inc(S[n + "_m"], 1)
                dve.wait_ge(S[n + "_m"], k + 1)
                ops = [lambda: V.tensor_reduce(small(1), m, AX, ALU.max),
                       lambda: V.tensor_tensor(small(2), es, small(1), ALU.add),
                       lambda: V.scalar_tensor_tensor(small(3), small(2), slope, small(2), ALU.mult, ALU.max),
                       lambda: V.tensor_tensor(small(4), es, small(3), ALU.subtract),
                       lambda: V.scalar_tensor_tensor(small(5), es, slope, small(3), ALU.mult, ALU.subtract)]
                V.tensor_reduce(small(1), m, AX, ALU.max).then_inc(S[n + "_d"], 1)
                dve.wait_ge(S[n + "_d"], 6 * k + 1)
                V.tensor_tensor(small(2), es, small(1), ALU.add).then_inc(S[n + "_d"], 1)
                dve.wait_ge(S[n + "_d"], 6 * k + 2)
                V.scalar_tensor_tensor(small(3), small(2), slope, small(2), ALU.mult, ALU.max).then_inc(S[n + "_d"], 1)
                dve.wait_ge(S[n + "_d"], 6 * k + 3)
                V.tensor_tensor(small(4), es, small(3), ALU.subtract).then_inc(S[n + "_d"], 1)
                V.scalar_tensor_tensor(small(5), es, slope, small(3), ALU.mult, ALU.subtract).then_inc(S[n + "_d"], 1)
                V.tensor_copy(small(0), small(3)).then_inc(S[n + "_d"], 1)

            def larger(k, n, small, m, t, T):
                dve.wait_ge(S[n + "_d"], 6 * k + 6)
                for j in range(T):
                    dve.wait_ge(S[n + "_t"], T * k + j + 1)
                    V.scalar_tensor_tensor(m[:, j], m[:, j], small(4)[:, j:j + 1], t[:, j], ALU.add, ALU.max) \
                     .then_inc(S[n + "_w"], 1)

            def stats(i, n, src, bn, mv):
                for b in range(G):
                    V.bn_stats(bn[:, b], src[:, b]).then_inc(S[n + "_st"], 1)
                for b in range(G):
                    dve.wait_ge(S["prep"], 1)
                    dve.wait_ge(S[n + "_st"], G * i + b + 1)
                    V.bn_aggr(mv[:, b], bn[:, b]).then_inc(S[n + "_mv"], 1)

            def normed(i, n, name, dst, mv, rs):
                dve.wait_ge(S[n + "_rs"], i + 1)
                dve.wait_ge(S[n + "_mv"], G * (i + 1))
                for b in range(G):
                    V.tensor_scalar(dst[:, b], dst[:, b], mv[:, b, 0:1], rs[:, b:b + 1], ALU.subtract, ALU.mult) \
                     .then_inc(S[name], 1)

            s0 = lambda j: f_small[:, j]
            s3 = lambda j: c_small[:, j]

            def x0(i):
                dve.wait_ge(S["xt_in"], 16 * (i + 1))
                V.tensor_copy(xT[0][:], xt[:]).then_inc(S["xt_hi"], 1)

            def wh_(i):
                edge_columns(i, "wh", ec0, wh, 0, "ec0")

            def g0a(i):
                dve.wait_ge(S["z0_ps"], i + 1)
                dve.wait_ge(S["ec0"], G * (i + 1))
                front_of_softmax(i, "g0", s0, ps[:, 2, 0:G * P].rearrange("p (g n) -> p g n", g=G), mask, m0[:],
                                 ec0[:, :, 0], SLOPE0, G)

            def g0b(i):
                larger(i, "g0", s0, m0, t0, G)

            def g0c(i):
                dve.wait_ge(S["g0_p"], G * (i + 1))
                V.reciprocal(s0(7), s0(6)).then_inc(S["g0_r"], 1)
                dve.wait_ge(S["g0_r"], 2 * i + 1)
                V.tensor_scalar(s0(7), s0(7), valid[:, 1:2], None, ALU.mult).then_inc(S["g0_r"], 1)

            def pt0(i):
                low("p0_lo", i + 1, p0[1][:].rearrange("p g n -> p (g n)"), ps[:, 3, 0:G * P],
                    p0[0][:].rearrange("p g n -> p (g n)"), "p0_hi")

            def av0(i):
                dve.wait_ge(S["x_in"], 16 * (i + 1))
                dve.wait_ge(S["g0_r"], 2 * (i + 1))
                for b in range(G):
                    dve.wait_ge(S["av0_ps"], G * i + b + 1)
                    V.scalar_tensor_tensor(xn[:, b], ps[:, b, 0:D], s0(7)[:, b:b + 1], xn[:, b], ALU.mult, ALU.add) \
                     .then_inc(S["y0"], 1)

            def n0(i):
                dve.wait_ge(S["y0"], G * (i + 1))
                stats(i, "n0", xn, f_bn[:, 0], f_mv[:, 0])
                normed(i, "n0", "x1", xn, f_mv[:, 0], f_rs[:, 0])

            def x1T(i):
                low("x1T_lo", i + 1, xT[1][:].rearrange("p c n -> p (c n)"), ps[:, 2, :],
                    xT[0][:].rearrange("p c n -> p (c n)"), "x1T_hi")

            def qk(i):
                for n, pair, bank, bias in (("q", qq, 3, BQ), ("k", kk, 0, BK)):
                    dve.wait_ge(S[n + "_hi"], C * (i + 1))
                    for t in range(C):
                        V.scalar_tensor_tensor(pair[1][:, t], ps[:, bank, t * G * P:(t + 1) * G * P],
                                               colsb[:, bias, t:t + 1], f(pair[0][:, t]), ALU.add, ALU.subtract) \
                         .then_inc(S[n + "_lo"], 1)

            def v(i):
                low("v_lo", i + 1, val[1][:].rearrange("p g d -> p (g d)"), ps[:, 1, :],
                    val[0][:].rearrange("p g d -> p (g d)"), "v_hi")

            def scores(u):
                def fn(i):
                    w = u % 2
                    dve.wait_ge(S["s_ps"], 4 * i + u + 1)
                    V.tensor_tensor(sm[:, w], ps[:, 2 + w, :].rearrange("p (r n) -> p r n", r=R),
                                    mask[:].unsqueeze(1).to_broadcast([P, R, P]), ALU.add).then_inc(S["sm"], 1)
                    dve.wait_ge(S["sm"], 4 * i + u + 1)
                    V.tensor_reduce(s1max[:, w], sm[:, w], AX, ALU.max).then_inc(S["smax"], 1)
                    dve.wait_ge(S["smax"], 4 * i + u + 1)
                    V.tensor_scalar(s1neg[:, w], s1max[:, w], -SCALE, None, ALU.mult).then_inc(S["sneg"], 1)
                return fn

            def sums(u):
                def fn(i):
                    w = u % 2
                    dve.wait_ge(S["s_p"], R * (4 * i + u + 1))
                    V.reciprocal(s1rec[:, w], s1sum[:, w]).then_inc(S["s_rec0"], 1)
                    dve.wait_ge(S["s_rec0"], 4 * i + u + 1)
                    V.tensor_scalar(s1rec[:, w], s1rec[:, w], valid[:, 2:3], None, ALU.mult).then_inc(S["s_rec"], 1)
                    low("p1_lo", 4 * i + u + 1, pT[1][:, w], ps[:, w, :], pT[0][:, w], "p1_hi")
                return fn

            def heads_out(t):
                def fn(i):
                    for r in range(R):
                        q = slice(DH * r, DH * (r + 1))
                        dve.wait_ge(S["o_hi"], C * R * i + R * t + r + 1)
                        V.scalar_tensor_tensor(oT[1][q, t].rearrange("p (g n) -> p g n", g=G), ps[q, 0:G, r * P:(r + 1) * P],
                                               colsb[q, BV, t:t + 1], f(oT[0][q, t].rearrange("p (g n) -> p g n", g=G)),
                                               ALU.add, ALU.subtract).then_inc(S["o_lo"], 1)
                return fn

            def wo(i):
                dve.wait_ge(S["wo_ps"], i + 1)
                dve.wait_ge(S["xr"], i + 1)
                V.tensor_tensor(xn[:].rearrange("p g d -> p (g d)"), ps[:, 2, :], xr[:].rearrange("p g d -> p (g d)"), ALU.add) \
                 .then_inc(S["y1"], 1)

            def n1(i):
                dve.wait_ge(S["y1"], i + 1)
                stats(i, "n1", xn, f_bn[:, 1], f_mv[:, 1])
                normed(i, "n1", "x2", xn, f_mv[:, 1], f_rs[:, 1])

            def x2T(i):
                low("x2T_lo", i + 1, bT[1][:].rearrange("p c n -> p (c n)"), ps[:, 4, :],
                    bT[0][:].rearrange("p c n -> p (c n)"), "x2T_hi")

            def er(i):
                dve.wait_ge(S["er_ps"], i + 1)
                V.tensor_copy(eT[:], ps[0:2 * H2, 5, 0:G * P]).then_inc(S["eT"], 1)
                dve.wait_ge(S["ec_ps"], i + 1)
                V.tensor_copy(ec2[:], ps[:, 6, 0:G * 2 * H2].rearrange("p (g e) -> p g e", g=G)).then_inc(S["ec2"], 1)

            def g2a(i):
                dve.wait_ge(S["ec2"], i + 1)
                for b in range(G):
                    dve.wait_ge(S["z2_ps"], G * i + b + 1)
                    front_of_softmax(G * i + b, "g2", lambda j: b_small[:, j, b],
                                     ps[:, 4 + b, :].rearrange("p (h n) -> p h n", h=H2), mask2, m2[:, b],
                                     ec2[:, b, 0:H2], SLOPE2, H2)

            def g2b(i):
                for b in range(G):
                    larger(G * i + b, "g2", lambda j: b_small[:, j, b], m2[:, b], t2[:, b], H2)

            def g2c(i):
                for b in range(G):
                    dve.wait_ge(S["g2_p"], H2 * (G * i + b + 1))
                    V.reciprocal(b_small[:, 7, b], b_small[:, 6, b]).then_inc(S["g2_r"], 1)

            def g2d(i):
                for b in range(G):
                    low("p2_lo", G * i + b + 1, p2[1][:, b], ps[:, 6 + b, :], p2[0][:, b], "p2_hi")

            def gx(i):
                for b in range(G):
                    for c in range(C):
                        low("g_lo", C * (G * i + b) + c + 1, hT[1][:, :, c, node(b)],
                            ps[:, 4 + 2 * b + c, :].rearrange("p (h n) -> p h n", h=H2), hT[0][:, :, c, node(b)], "g_hi")

            def hT_(h):
                def fn(i):
                    k = H2 * i + h + 1
                    dve.wait_ge(S["h_e"], k)
                    V.tensor_scalar(he[:, h % 2], he[:, h % 2], 1.0, -1.0, ALU.min, ALU.add).then_inc(S["h_e1"], 1)
                    dve.wait_ge(S["h_e1"], k)
                    if h >= 2:
                        dve.wait_ge(S["h_lo"], k - 2)
                    V.scalar_tensor_tensor(hf[:, h % 2], ps[:, 4 + h, :], 0.0, he[:, h % 2], ALU.max, ALU.add) \
                     .then_inc(S["h_f"], 1)
                return fn

            def wh3_(i):
                edge_columns(i, "wh3", ec3, wh3, 4, "ec3")

            def g3a(i):
                dve.wait_ge(S["z3_ps"], i + 1)
                dve.wait_ge(S["ec3"], G * (i + 1))
                front_of_softmax(i, "g3", s3, ps[:, 6, 0:G * P].rearrange("p (g n) -> p g n", g=G), mask2, m3[:],
                                 ec3[:, :, 0], SLOPE2, G)

            def g3b(i):
                larger(i, "g3", s3, m3, t3, G)

            def g3c(i):
                dve.wait_ge(S["g3_p"], G * (i + 1))
                V.reciprocal(s3(7), s3(6)).then_inc(S["g3_r"], 1)

            def pt3(i):
                low("p3_lo", i + 1, p3[1][:].rearrange("p g n -> p (g n)"), ps[:, 7, 0:G * P],
                    p3[0][:].rearrange("p g n -> p (g n)"), "p3_hi")

            def av3(i):
                dve.wait_ge(S["g3_r"], i + 1)
                dve.wait_ge(S["o3_e"], G * (i + 1))
                for b in range(G):
                    V.tensor_scalar(ob[:, b], ps[:, 4, b * D:(b + 1) * D], s3(7)[:, b:b + 1], 0.0, ALU.mult, ALU.max) \
                     .then_inc(S["o3_z"], 1)
                V.tensor_scalar(oe[:], oe[:], 1.0, -1.0, ALU.min, ALU.add).then_inc(S["o3_e1"], 1)
                dve.wait_ge(S["o3_e1"], i + 1)
                dve.wait_ge(S["o3_z"], G * (i + 1))
                V.tensor_tensor(ob[:], ob[:], oe[:], ALU.add).then_inc(S["o3"], 1)

            def oT_(i):
                low("oT_lo", i + 1, bT[1][:].rearrange("p c n -> p (c n)"), ps[:, 5, :],
                    bT[0][:].rearrange("p c n -> p (c n)"), "oT_hi")

            def f1(i):
                dve.wait_ge(S["hid_hi"], C * (i + 1))
                for t in range(C):
                    V.tensor_scalar(hidf[:, t], ps[:, 6, t * G * P:(t + 1) * G * P], colsb[:, B1, t:t + 1], 0.0,
                                    ALU.add, ALU.max).then_inc(S["hid_f"], 1)
                for t in range(C):
                    dve.wait_ge(S["hid_f"], C * i + t + 1)
                    low("hid_lo", C * i + t + 1, hid[1][:, t], hidf[:, t], hid[0][:, t], "hid_hi")

            def f2(i):
                dve.wait_ge(S["f2_ps"], i + 1)
                dve.wait_ge(S["ob"], i + 1)
                V.tensor_tensor(ob[:].rearrange("p g d -> p (g d)"), ps[:, 7, :], ob[:].rearrange("p g d -> p (g d)"), ALU.add) \
                 .then_inc(S["y2"], 1)

            def n2(i):
                dve.wait_ge(S["y2"], i + 1)
                stats(i, "n2", ob, b_bn[:, 0], b_mv[:, 0])
                normed(i, "n2", "n2", ob, b_mv[:, 0], b_rs[:, 0])

            def n3(i):
                dve.wait_ge(S["y3"], i + 1)
                stats(i, "n3", ob, b_bn[:, 1], b_mv[:, 1])
                normed(i, "n3", "x3", ob, b_mv[:, 1], b_rs[:, 1])

            def x3T(i):
                low("x3T_lo", i + 1, bT[1][:].rearrange("p c n -> p (c n)"), ps[:, 4, :],
                    bT[0][:].rearrange("p c n -> p (c n)"), "x3T_hi")

            def mm(i):
                dve.wait_ge(S["x3d"], i + 1)
                for b in range(G):
                    dve.wait_ge(S["mj_hi"], G * i + b + 1)
                    V.scalar_tensor_tensor(x3d[:, b], ps[:, 5 + b, 0:D], deg[:], x3d[:, b], ALU.mult, ALU.add) \
                     .then_inc(S["x3m"], 1)
                    low("mj_lo", G * i + b + 1, mj[1][:, b], ps[:, 5 + b, D:2 * D], mj[0][:, b], "mj_hi")

            def am(i):
                dve.wait_ge(S["x3m"], G * (i + 1))
                dve.wait_ge(S["am_ps"], i + 1)
                V.tensor_tensor(ob[:].rearrange("p g d -> p (g d)"), ps[:, 7, :], x3d[:].rearrange("p g d -> p (g d)"), ALU.add) \
                 .then_inc(S["y4"], 1)

            def n4(i):
                dve.wait_ge(S["y4"], i + 1)
                stats(i, "n4", ob, b_bn[:, 2], b_mv[:, 2])
                normed(i, "n4", "x4", ob, b_mv[:, 2], b_rs[:, 2])

            with_loop(nc, dve, NG, {
                "x0": x0, "wh": wh_, "g0a": g0a, "g0b": g0b, "g0c": g0c, "pt0": pt0, "av0": av0, "n0": n0, "x1T": x1T,
                "qk": qk, "v": v, "sA": scores(0), "sB": scores(1), "sC": scores(2), "sD": scores(3),
                "pA": sums(0), "pB": sums(1), "pC": sums(2), "pD": sums(3), "oA": heads_out(0), "oB": heads_out(1),
                "wo": wo, "n1": n1,
                "x2T": x2T, "er": er, "g2a": g2a, "g2b": g2b, "g2c": g2c, "g2d": g2d, "gx": gx,
                "hT0": hT_(0), "hT1": hT_(1), "hT2": hT_(2), "hT3": hT_(3), "wh3": wh3_,
                "g3a": g3a, "g3b": g3b, "g3c": g3c, "pt3": pt3, "av3": av3, "oT": oT_, "f1": f1, "f2": f2,
                "n2": n2, "n3": n3, "x3T": x3T, "mm": mm, "am": am, "n4": n4}, run, last_store=lambda i: None)

        @block.tensor
        def _(pe):
            T_ = nc.tensor
            pe.wait_ge(S["prep"], 1)

            def transposes(src, bank):
                for b in range(G):
                    for c in range(C):
                        last = T_.transpose(ps[:, bank, (c * G + b) * P:(c * G + b + 1) * P], src[:, b, c * P:(c + 1) * P], ident[:])
                return last

            def natural(bank, off, width, xt_, b, w, stop_chunks=C):
                for c in range(C):
                    last = three(pe, ps[:, bank, off:off + width], part(xt_, ALL, c, node(b)), part(w, ALL, c, slice(0, width)),
                                 c == 0, c == C - 1)
                return last

            def transposed(bank, t, w, xt_):
                for c in range(C):
                    last = three(pe, ps[:, bank, t * G * P:(t + 1) * G * P], part(w, ALL, c, slice(t * P, (t + 1) * P)),
                                 part(xt_, ALL, c), c == 0, c == C - 1)
                return last

            def spread(bank, off, col):
                return T_.transpose(ps[:, bank, off:off + P], col.to_broadcast([P, P]), ident[:])

            def wh_(i):
                pe.wait_ge(S["xt_lo"], i + 1)
                for b in range(G):
                    natural(b, 0, D + 2, xT, b, W0).then_inc(S["wh_ps"], 1)

            def g0a(i):
                pe.wait_ge(S["ec0"], G * (i + 1))
                for b in range(G):
                    last = spread(2, b * P, ec0[:, b, 1:2])
                last.then_inc(S["z0_ps"], 1)

            def pt0(i):
                pe.wait_ge(S["g0_p"], G * (i + 1))
                for b in range(G):
                    last = T_.transpose(ps[:, 3, b * P:(b + 1) * P], t0[:, b], ident[:])
                last.then_inc(S["p0_ps"], 1)

            def av0(i):
                pe.wait_ge(S["p0_lo"], i + 1)
                pe.wait_ge(S["wh_lo"], G * (i + 1))
                for b in range(G):
                    three(pe, ps[:, b, 0:D], part(p0, ALL, b), part(wh, ALL, b), True, True).then_inc(S["av0_ps"], 1)

            def x1T(i):
                pe.wait_ge(S["x1"], G * (i + 1))
                transposes(xn, 2).then_inc(S["x1T_ps"], 1)

            def qk(i):
                pe.wait_ge(S["x1T_lo"], i + 1)
                for n, w, bank in (("q", Wq, 3), ("k", Wk, 0)):
                    for t in range(C):
                        transposed(bank, t, w, xT).then_inc(S[n + "_ps"], 1)

            def v(i):
                for b in range(G):
                    natural(1, b * D, D, xT, b, Wv).then_inc(S["v_ps"], 1)

            def scores(u):
                t, b = divmod(u, G)

                def fn(i):
                    if u == 0:
                        pe.wait_ge(S["q_stack"], 16 * 3 * R * (i + 1))
                        pe.wait_ge(S["k_stack"], 16 * 3 * R * (i + 1))
                    else:
                        if u >= 2:
                            pe.wait_ge(S["sm"], 4 * i + u - 1)
                    for r in range(R):
                        last = T_.matmul(ps[:, 2 + u % 2, r * P:(r + 1) * P], qs[:, r, t, node(b)], ks[:, r, t, node(b)],
                                         start=True, stop=True)
                    last.then_inc(S["s_ps"], 1)
                return fn

            def probsT(u):
                t, b = divmod(u, G)

                def fn(i):
                    pe.wait_ge(S["s_pn"], 4 * i + u + 1)
                    if u == 1:
                        pe.wait_ge(S["v_lo"], i + 1)
                    if u >= 2:
                        pe.wait_ge(S["o_lo"], C * R * i + R * t)
                    for r in range(R):
                        last = T_.transpose(ps[:, b, r * P:(r + 1) * P], sm[:, u % 2, r], ident[:])
                    last.then_inc(S["p1_ps"], 1)
                return fn

            def heads(t):
                def fn(i):
                    pe.wait_ge(S["v_lo"], i + 1)
                    for b in range(G):
                        u = G * t + b
                        pe.wait_ge(S["p1_lo"], 4 * i + u + 1)
                        three(pe, ps[:, b, :], part(val, ALL, b, slice(t * P, (t + 1) * P)), part(pT, ALL, u % 2), True, True) \
                            .then_inc(S["o_ps"], 1)
                return fn

            def wo(i):
                pe.wait_ge(S["o_lo"], C * R * (i + 1))
                for b in range(G):
                    last = natural(2, b * D, D, oT, b, Wo)
                last.then_inc(S["wo_ps"], 1)

            def x2T(i):
                pe.wait_ge(S["x2"], G * (i + 1))
                transposes(xn, 4).then_inc(S["x2T_ps"], 1)

            def er(i):
                pe.wait_ge(S["x2T_lo"], i + 1)
                for c in range(C):
                    last = three(pe, ps[:, 5, 0:G * P], part(WA, ALL, c), part(bT, ALL, c), c == 0, c == C - 1)
                last.then_inc(S["er_ps"], 1)
                pe.wait_ge(S["prep"], 1)
                pe.wait_ge(S["eT"], i + 1)
                for b in range(G):
                    last = T_.transpose(ps[:, 6, b * 2 * H2:(b + 1) * 2 * H2], eT[:, node(b)], ident[0:2 * H2, 0:2 * H2])
                last.then_inc(S["ec_ps"], 1)

            def g2a(i):
                pe.wait_ge(S["ec2"], i + 1)
                for b in range(G):
                    for h in range(H2):
                        last = spread(4 + b, h * P, ec2[:, b, H2 + h:H2 + h + 1])
                    last.then_inc(S["z2_ps"], 1)

            def g2d(i):
                for b in range(G):
                    pe.wait_ge(S["g2_pn"], G * i + b + 1)
                    for h in range(H2):
                        last = T_.transpose(ps[:, 6 + b, h * P:(h + 1) * P], t2[:, b, h], ident[:])
                    last.then_inc(S["p2_ps"], 1)

            def gx(i):
                pe.wait_ge(S["x2_lo"], i + 1)
                pe.wait_ge(S["g2_m"], G * (i + 1))
                for b in range(G):
                    pe.wait_ge(S["p2_lo"], G * i + b + 1)
                    for c in range(C):
                        three(pe, ps[:, 4 + 2 * b + c, :], part(x2, ALL, b, slice(c * P, (c + 1) * P)), part(p2, ALL, b), True, True) \
                            .then_inc(S["g_ps"], 1)

            def hT_(h):
                def fn(i):
                    if h == 0:
                        pe.wait_ge(S["g_lo"], G * C * (i + 1))
                    for t in range(C):
                        for c in range(C):
                            last = three(pe, ps[:, 4 + h, t * G * P:(t + 1) * G * P], part(WH, ALL, h, c, slice(t * P, (t + 1) * P)),
                                         part(hT, ALL, h, c), c == 0, c == C - 1)
                    last.then_inc(S["h_ps"], 1)
                return fn

            def wh3_(i):
                pe.wait_ge(S["h_f"], H2 * i + 2)
                for b in range(G):
                    for k in range(H2 * C):
                        if b == 0 and k % C == 0:
                            pe.wait_ge(S["h_lo"], H2 * i + k // C + 1)
                        last = three(pe, ps[:, 4 + b, 0:D + 2], part(hT, ALL, k // C, k % C, node(b)), part(WOUT, ALL, k), k == 0,
                                     k == H2 * C - 1)
                    last.then_inc(S["wh3_ps"], 1)

            def g3a(i):
                pe.wait_ge(S["ec3"], G * (i + 1))
                for b in range(G):
                    last = spread(6, b * P, ec3[:, b, 1:2])
                last.then_inc(S["z3_ps"], 1)

            def pt3(i):
                pe.wait_ge(S["g3_p"], G * (i + 1))
                for b in range(G):
                    last = T_.transpose(ps[:, 7, b * P:(b + 1) * P], t3[:, b], ident[:])
                last.then_inc(S["p3_ps"], 1)

            def av3(i):
                pe.wait_ge(S["p3_lo"], i + 1)
                pe.wait_ge(S["wh3_lo"], G * (i + 1))
                for b in range(G):
                    three(pe, ps[:, 4, b * D:(b + 1) * D], part(p3, ALL, b), part(wh3, ALL, b), True, True).then_inc(S["av3_ps"], 1)

            def oT_(i):
                pe.wait_ge(S["o3"], i + 1)
                transposes(ob, 5).then_inc(S["oT_ps"], 1)

            def f1(i):
                pe.wait_ge(S["oT_lo"], i + 1)
                for t in range(C):
                    transposed(6, t, W1, bT).then_inc(S["f1_ps"], 1)

            def f2(i):
                pe.wait_ge(S["hid_lo"], C * (i + 1))
                for b in range(G):
                    last = natural(7, b * D, D, hid, b, W2)
                last.then_inc(S["f2_ps"], 1)

            def x3T(i):
                pe.wait_ge(S["x3"], G * (i + 1))
                transposes(ob, 4).then_inc(S["x3T_ps"], 1)

            def mm(i):
                pe.wait_ge(S["x3T_lo"], i + 1)
                for b in range(G):
                    natural(5 + b, 0, 2 * D, bT, b, W3).then_inc(S["mm_ps"], 1)

            def am(i):
                for b in range(G):
                    pe.wait_ge(S["mj_lo"], G * i + b + 1)
                    T_.matmul(ps[:, 7, b * D:(b + 1) * D], ADJT, mj[1][:, b], start=True, stop=False)
                    last = T_.matmul(ps[:, 7, b * D:(b + 1) * D], ADJT, mj[0][:, b], start=False, stop=True)
                last.then_inc(S["am_ps"], 1)

            with_loop(nc, pe, NG, {
                "wh": wh_, "g0a": g0a, "pt0": pt0, "av0": av0, "x1T": x1T, "qk": qk, "v": v,
                "sA": scores(0), "sB": scores(1), "sC": scores(2), "sD": scores(3),
                "pA": probsT(0), "pB": probsT(1), "pC": probsT(2), "pD": probsT(3), "oA": heads(0), "oB": heads(1), "wo": wo,
                "x2T": x2T, "er": er, "g2a": g2a, "g2d": g2d, "gx": gx, "hT0": hT_(0), "hT1": hT_(1), "hT2": hT_(2),
                "hT3": hT_(3), "wh3": wh3_, "g3a": g3a, "pt3": pt3, "av3": av3, "oT": oT_, "f1": f1, "f2": f2,
                "x3T": x3T, "mm": mm, "am": am}, run)


def with_loop(nc, eng, NG, table, run, after_load=None, last_store=None):
    with eng.Fori(0, NG - 1) as i:
        run(table, i, i)
        if after_load:
            after_load(i)
    run(table, NG - 1, NG - 1)


def kernel(**inputs):
    import concourse.bacc as bacc
    from concourse.bass_utils import run_bass_kernel_spmd

    a = {k: np.asarray(v) for k, v in inputs.items()}
    x = a["x"]
    B = x.shape[0]
    NG = B // G

    def chunks(w):
        return w.reshape(-1, P, w.shape[1]).transpose(1, 0, 2)

    def padded(w):
        v = np.zeros((P, w.shape[0] // P, D + 2), np.float32)
        v[:, :, 0:D] = chunks(w)
        return v

    heads = a["L2_gnn_W_heads"]
    w3 = np.concatenate([a["L3_gnn_W"][:, :D].T, a["L3_gnn_W"][:, D:].T], axis=1)
    parts = {"W0": padded(a["L0_gnn_W"]), "Wq": chunks(a["L1_gnn_Wq"].T), "Wk": chunks(a["L1_gnn_Wk"].T),
             "Wv": chunks(a["L1_gnn_Wv"].T), "Wo": chunks(a["L1_gnn_Wo"].T),
             "Wh": chunks(heads.reshape(H2 * D, D)), "Wout": padded(a["L2_gnn_W_out"]), "w1": chunks(a["L2_gnn_w1"]),
             "w2": chunks(a["L2_gnn_w2"]), "W3": chunks(w3), "Wa": np.zeros((P, C * P), np.float32),
             "adjT": np.zeros((P, P), np.float32)}
    weights = np.concatenate([parts[n].reshape(P, -1) for n, _ in _COLS], axis=1)
    att = np.concatenate([a["L0_gnn_a_src"], a["L0_gnn_a_dst"], a["L2_gnn_a_out"], a["L2_gnn_a_heads"].reshape(-1)])
    rows = np.stack([a["L1_gnn_bo"], a["L2_gnn_b2"], a["L2_gnn_ln_gamma"], a["L2_gnn_ln_beta"], a["L3_gnn_b"]])
    cols = np.stack([a[n].reshape(C, P).T for n in ("L1_gnn_bq", "L1_gnn_bk", "L1_gnn_bv", "L2_gnn_b1")], axis=1)
    arrays = {
        "x_n": x,
        "x_t": x.reshape(NG, G, P, C, P).transpose(0, 4, 3, 1, 2).reshape(NG, P, C * G * P),
        "weights": weights, "adj": a["adj"], "adj_t": a["adj"].T,
        "att_rows": np.broadcast_to(att, (P, att.size)), "rows": np.broadcast_to(rows, (P,) + rows.shape), "cols": cols,
    }
    nc = bacc.Bacc("TRN2", target_bir_lowering=False, num_devices=1)
    args, feed = [], {}
    for name, v in arrays.items():
        v = np.ascontiguousarray(v)
        feed[f"in_{name}"] = v
        args.append(nc.dram_tensor(f"in_{name}", v.shape, mybir.dt.from_np(v.dtype), kind="ExternalInput").ap())
    out = nc.dram_tensor("out_x", x.shape, F32, kind="ExternalOutput").ap()
    build(nc, *args, out)
    r = run_bass_kernel_spmd(nc, [feed], core_ids=[0])
    return r.results[0]["out_x"]
```

```python
from contextlib import ExitStack

import numpy as np

import concourse.bass as bass
from concourse import mybir

F32 = mybir.dt.float32
F32R = mybir.dt.float32r
I32 = mybir.dt.int32
BF16 = mybir.dt.bfloat16
ALU = mybir.AluOpType
ACT = mybir.ActivationFunctionType
AX = mybir.AxisListType.X

P = 128
D = 256
C = D // P
G = 2
H1 = 8
DH = D // H1
R = P // DH
H2 = 4
MASK = -1.0e9
EPS = 1e-5
SLOPE0, SLOPE2 = 0.2, 0.01
STACK = 16 * 3 * R
SCALE = 1.0 / float(np.sqrt(DH))

_COLS = [("W0", C * (D + 2)), ("Wq", C * D), ("Wk", C * D), ("Wv", C * D), ("Wo", C * D),
         ("Wh", H2 * C * D), ("Wout", H2 * C * (D + 2)), ("w1", C * D), ("w2", C * D),
         ("W3", C * 2 * D), ("Wa", C * P), ("adjT", P)]
OFF = {}
WTOT = 0
for _n, _w in _COLS:
    OFF[_n] = (WTOT, WTOT + _w)
    WTOT += _w

ORDER = [tuple(x.split(":")) for x in """
    F1:x0 B2:g3a F2:sA B1:x2T B2:g3b F1:wh F2:sB B1:er
    F2:eA F1:g0a B1:ec B2:g3c F2:eB B2:pt3 F1:g0b B1:g2a
    F1:g0c F1:pt0 B2:av3 F2:pA F2:pB B1:g2b B2:oT F1:av0
    B1:g2c F2:oA B2:f1 B1:g2d F1:n0 B2:f2 B2:n2 B1:gx0
    F2:sC F2:sD F1:n0b F1:x1T B2:n2b B2:n2c B1:gx1 F2:eC
    B2:n3 F2:eD F1:qk B1:hT0 B1:xb B2:n3b B1:hT1 B1:hh0
    F2:pC F2:pD B2:x3T B1:hh1 B1:hT2 B1:hT3 F2:oB B1:hh2
    B1:hh3 B2:mm F1:v F2:wo F2:n1 F2:n1b F1:xr B2:am
    B2:n4 B2:n4b B1:wh3_0 B1:wh3_1""".split()]
PARTS = ("F1", "F2", "B1", "B2")
_ROWS = ["bo", "b2", "gamma", "beta", "b3"]


def build(nc, x_n, x_t, weights, adj, adj_t, att_rows, rows, cols, out):
    B = x_n.shape[0]
    NG = B // G
    xn_v = x_n.rearrange("(g b) n d -> g n b d", b=G)
    out_v = out.rearrange("(g b) n d -> g n b d", b=G)

    with ExitStack() as ctx:
        def sb(name, shape, dt=F32):
            return ctx.enter_context(nc.sbuf_tensor(name, shape, dt))

        def sem(name):
            return ctx.enter_context(nc.semaphore(name))

        ps = ctx.enter_context(nc.psum_tensor("ps", [P, 8, 512], F32))

        w_hi = sb("w_hi", [P, WTOT], F32R)
        w_lo = sb("w_lo", [P, WTOT], F32R)
        rowsb = sb("rowsb", [P, len(_ROWS), D])
        colsb = sb("colsb", [P, 4, C])
        ident = sb("ident", [P, P])
        mask = sb("mask", [P, P])
        mask2 = sb("mask2", [P, P])
        mask_r = sb("mask_r", [P, R, P], BF16)
        tick = sb("tick", [P, 1])
        ident_b = sb("ident_b", [P, P], BF16)
        adj_i = sb("adj_i", [P, P], I32)
        adjt_i = sb("adjt_i", [P, P], I32)
        adj_f = sb("adj_f", [P, P])
        deg = sb("deg", [P, 1])
        valid = sb("valid", [P, 3])
        eps_t = sb("eps_t", [P, G])
        pow_t = sb("pow_t", [P, G])
        neg_t = sb("neg_t", [P, G])

        def view(t, name, *dims):
            a, b = OFF[name]
            v = t[:, a:b]
            if len(dims) == 2:
                return v.rearrange("p (a b) -> p a b", a=dims[0])
            if len(dims) == 3:
                return v.rearrange("p (a b c) -> p a b c", a=dims[0], b=dims[1])
            return v

        def both(name, *dims):
            return view(w_hi, name, *dims), view(w_lo, name, *dims)

        W0, Wq, Wk, Wv, Wo = both("W0", C, D + 2), both("Wq", C, D), both("Wk", C, D), both("Wv", C, D), both("Wo", C, D)
        WH, WOUT = both("Wh", H2, C, D), both("Wout", H2 * C, D + 2)
        W1, W2, W3, WA = both("w1", C, D), both("w2", C, D), both("W3", C, 2 * D), both("Wa", C, P)
        ADJT = view(w_hi, "adjT")
        row = {n: rowsb[:, k, :].unsqueeze(1).to_broadcast([P, G, D]) for k, n in enumerate(_ROWS)}
        BQ, BK, BV, B1 = range(4)

        xn = sb("xn", [P, G, D])
        xt = sb("xt", [P, C, G * P])
        m2, t2 = sb("m2", [P, G, H2, P]), sb("t2", [P, G, H2, P])
        he = sb("he", [P, 2, C * G * P])
        sm = sb("sm", [P, 2, R, P])
        f_small, b_small, c_small = sb("f_small", [P, 8, G]), sb("b_small", [P, 8, G, H2]), sb("c_small", [P, 8, G])

        with nc.sbuf_tensor("w_raw", [P, WTOT], F32) as w_raw:
            pass

        xr = sb("xr", [P, G, D])
        xT = sb("xT_hi", [P, C, G * P], F32R), sb("xT_lo", [P, C, G * P], F32R)
        wh = sb("wh_hi", [P, G, D], F32R), sb("wh_lo", [P, G, D], F32R)
        val = sb("val_hi", [P, G, D], F32R), sb("val_lo", [P, G, D], F32R)
        x1T_ = tuple(t[:].rearrange("p g d -> p (g d)").rearrange("p (c n) -> p c n", c=C) for t in wh)
        qq = xT
        kk = sb("k_hi", [P, C, G * P], F32R), sb("k_lo", [P, C, G * P], F32R)
        x2n = sb("x2n", [P, G, D])
        qs = sb("q_stack", [3 * DH, R, C, G * P], F32R)
        ks = sb("k_stack", [3 * DH, R, C, G * P], F32R)
        oT = sb("oT_hi", [P, C, G * P], F32R), sb("oT_lo", [P, C, G * P], F32R)
        pT = sb("pT_hi", [P, 2, R * P], F32R), sb("pT_lo", [P, 2, R * P], F32R)
        m0, t0 = (xt[:, k].rearrange("p (g n) -> p g n", g=G) for k in range(C))
        p0 = tuple(t[:, 0].rearrange("p (g n) -> p g n", g=G) for t in kk)
        ec0 = sb("ec0", [P, G, 2])
        s1max, s1neg, s1sum, s1rec = (sb("s1" + n, [P, 2, R]) for n in ("max", "neg", "sum", "rec"))
        f_bn, f_mv, f_rs = sb("f_bn", [P, 2, G, 6]), sb("f_mv", [P, 2, G, 2]), sb("f_rs", [P, 2, G])
        f_ve, f_sh = sb("f_ve", [P, 2, G]), sb("f_sh", [P, 2, G])

        xb = sb("xb", [P, G, D])
        x2 = sb("x2_hi", [P, G, D], F32R), sb("x2_lo", [P, G, D], F32R)
        bT = sb("bT_hi", [P, C, G * P], F32R), sb("bT_lo", [P, C, G * P], F32R)
        eT = sb("eT", [2 * H2, G * P])
        ec2 = sb("ec2", [P, G, 2 * H2])
        p2 = sb("p2_hi", [P, G, H2 * P], F32R), sb("p2_lo", [P, G, H2 * P], F32R)
        hT = sb("hT_hi", [P, H2, C, G * P], F32R), sb("hT_lo", [P, H2, C, G * P], F32R)
        wh3 = sb("wh3_hi", [P, G, D], F32R), sb("wh3_lo", [P, G, D], F32R)
        cT = sb("cT_hi", [P, C, G * P], F32R), sb("cT_lo", [P, C, G * P], F32R)
        ec3 = sb("ec3", [P, G, 2])
        ob = sb("ob", [P, G, D])
        hid = sb("hid_hi", [P, C, G * P], F32R), sb("hid_lo", [P, C, G * P], F32R)
        x3d = sb("x3d", [P, G, D])
        m3, t3 = x3d[:, :, 0:P], x3d[:, :, P:D]
        hidf = x3d[:].rearrange("p g d -> p (g d)").rearrange("p (c n) -> p c n", c=C)
        p3 = tuple(t[:, 0].rearrange("p (g n) -> p g n", g=G) for t in hid)
        mj = tuple(t[:].rearrange("p c n -> p (c n)").rearrange("p (g d) -> p g d", g=G) for t in hid)
        b_bn, b_mv, b_rs = sb("b_bn", [P, 3, G, 6]), sb("b_mv", [P, 3, G, 2]), sb("b_rs", [P, 3, G])
        b_ve, b_sh = sb("b_ve", [P, 3, G]), sb("b_sh", [P, 3, G])

        names = """prep_dma prep prep_w prep_id x_in xt_in xt_hi xt_lo wh_ps wh_hi wh_lo ec0
            z0_ps g0_m g0_d g0_t g0_w g0_p g0_r p0_ps p0_hi p0_lo av0_ps
            y0 n0_st n0_mv n0_rs x1 x1T_ps x1T_hi x1T_lo xr q_ps q_hi q_lo k_ps k_hi k_lo v_ps v_hi v_lo
            q_stack k_stack s_ps smax sneg s_p s_rec0 s_rec s_pn p1_ps p1_hi p1_lo o_ps o_hi o_lo wo_ps
            y1 n1_st n1_mv n1_rs x2
            x2T_ps x2T_hi x2T_lo x2_hi x2_lo xb er_ps eT ec_ps ec2 z2_ps g2_m g2_d g2_t g2_w g2_p g2_r g2_pn
            p2_ps p2_hi p2_lo g_ps g_hi g_lo h_ps h_e h_e1 h_f h_hi h_lo wh3_ps wh3_hi wh3_lo ec3
            z3_ps g3_m g3_d g3_t g3_w g3_p g3_r p3_ps p3_hi p3_lo av3_ps o3_e o3_e1 o3
            oT_ps oT_hi oT_lo ob f1_ps hid_hi hid_f hid_lo f2_ps y2 n2_st n2_mv n2_rs n2 n2g y3
            n3_st n3_mv n3_rs x3 x3T_ps x3T_hi x3T_lo x3d mm_ps x3m mj_hi mj_lo am_ps
            y4 n4_st n4_mv n4_rs x4 out""".split()
        S = {n: sem("s_" + n) for n in names}

        def three(pe, dst, a, b, start, stop):
            nc.tensor.matmul(dst, a[0], b[1], start=start, stop=False)
            nc.tensor.matmul(dst, a[1], b[0], start=False, stop=False)
            return nc.tensor.matmul(dst, a[0], b[0], start=False, stop=stop)

        def part(pair, *idx):
            return pair[0][idx], pair[1][idx]

        def f(ap):
            return ap.bitcast(F32)

        ALL = slice(None)

        def value(eng, count):
            return count if type(count) is int else eng.snap(count)

        def first(i):
            return type(i) is int and i == 0

        def node(b):
            return slice(b * P, (b + 1) * P)

        def run(table, i, parts=PARTS):
            for part_, stage in ORDER:
                if part_ in parts and stage in table:
                    table[stage](i - PARTS.index(part_))

        def rounds(eng, table):
            n = len(PARTS)
            for i in range(n):
                run(table, i, PARTS[:i + 1])
            with eng.Fori(n, NG) as i:
                run(table, i)
            for k in range(1, n):
                run(table, NG - 1 + k, PARTS[k:])

        block = ctx.enter_context(nc.Block())

        @block.sync
        def _(sp):
            for src, dst in ((weights, w_raw), (rows, rowsb), (cols, colsb), (adj, adj_i), (adj_t, adjt_i)):
                sp.dma_start(dst[:], src).then_inc(S["prep_dma"], 16)
            sp.dma_start(m2[:].rearrange("p g h n -> p (g h n)"), att_rows[:, 0:G * H2 * P]).then_inc(S["prep_dma"], 16)
            sp.dma_start(t2[:].rearrange("p g h n -> p (g h n)"), att_rows[:, G * H2 * P:2 * G * H2 * P]).then_inc(S["prep_dma"], 16)
            sp.dma_start(he[:].rearrange("p g n -> p (g n)"), att_rows[:, 2 * G * H2 * P:]).then_inc(S["prep_dma"], 16)

            def load_xt(i):
                if not first(i):
                    sp.wait_ge(S["p0_ps"], i)
                sp.dma_start(xt[:].rearrange("p c n -> p (c n)"), x_t[i]).then_inc(S["xt_in"], 16)

            def load_x(i):
                if not first(i):
                    sp.wait_ge(S["xr"], i)
                    sp.wait_ge(S["x1T_ps"], i)
                sp.dma_start(xn[:], xn_v[i]).then_inc(S["x_in"], 16)

            def stack(i):
                if not first(i):
                    sp.wait_ge(S["s_ps"], 4 * i)
                for name, pair, dst, order in (("q", qq, qs, (0, 0, 1)), ("k", kk, ks, (0, 1, 0))):
                    sp.wait_ge(S[name + "_hi"], C * (i + 1))
                    sp.wait_ge(S[name + "_lo"], C * (i + 1))
                    for j, which in enumerate(order):
                        for r in range(R):
                            sp.dma_start(f(dst[DH * j:DH * (j + 1), r]), f(pair[which][DH * r:DH * (r + 1)])) \
                              .then_inc(S[name + "_stack"], 16)

            def store(i):
                sp.wait_ge(S["x4"], G * (i + 1))
                sp.dma_start(out_v[i], ob[:]).then_inc(S["out"], 16)

            sp.sem_inc(S["out"], 16)
            late = len(PARTS)
            for i in range(late):
                load_xt(i)
                load_x(i)
                stack(i)
            with sp.Fori(late, NG) as i:
                load_xt(i)
                store(i - late)
                load_x(i)
                stack(i)
            for i in range(NG - late, NG):
                store(i)
            sp.wait_ge(S["out"], 16 * (NG + 1))

        @block.gpsimd
        def _(pool):
            nc.gpsimd.memset(ident[:], 0.0).then_inc(S["prep_id"], 1)
            nc.gpsimd.memset(eps_t[:], EPS).then_inc(S["prep_id"], 1)
            nc.gpsimd.memset(pow_t[:], -0.5).then_inc(S["prep_id"], 1)
            nc.gpsimd.memset(neg_t[:], -1.0).then_inc(S["prep_id"], 1)
            pool.wait_ge(S["prep_id"], 4)
            nc.gpsimd.affine_select(out=ident[:], in_=ident[:], compare_op=ALU.not_equal, fill=1.0, base=0,
                                    pattern=[[-1, P]], channel_multiplier=1).then_inc(S["prep_id"], 1)
            pool.wait_ge(S["prep"], 1)

            def rsqrt(i, n, mv, ve, rs, sh):
                pool.wait_ge(S[n + "_mv"], G * (i + 1))
                nc.gpsimd.tensor_tensor(ve, mv[:, :, 1], eps_t[:], ALU.add).then_inc(S[n + "_rs"], 1)
                nc.gpsimd.tensor_tensor(sh, mv[:, :, 0], neg_t[:], ALU.mult).then_inc(S[n + "_rs"], 1)
                pool.wait_ge(S[n + "_rs"], 4 * i + 2)
                nc.gpsimd.tensor_tensor(rs, ve, pow_t[:], ALU.pow).then_inc(S[n + "_rs"], 1)
                pool.wait_ge(S[n + "_rs"], 4 * i + 3)
                nc.gpsimd.tensor_tensor(sh, sh, rs, ALU.mult).then_inc(S[n + "_rs"], 1)

            def x0(i):
                pool.wait_ge(S["xt_hi"], i + 1)
                nc.gpsimd.tensor_tensor(xT[1][:], xt[:], f(xT[0][:]), ALU.subtract).then_inc(S["xt_lo"], 1)

            def n0(i):
                rsqrt(i, "n0", f_mv[:, 0], f_ve[:, 0], f_rs[:, 0], f_sh[:, 0])

            def x1_plus(i):
                pool.wait_ge(S["x1"], G * (i + 1))
                if not first(i):
                    pool.wait_ge(S["y1"], i)
                nc.gpsimd.tensor_tensor(xr[:], xn[:], row["bo"], ALU.add).then_inc(S["xr"], 1)

            def norm_probs(u):
                def fn(i):
                    pool.wait_ge(S["s_p"], R * (4 * i + u + 1))
                    pool.wait_ge(S["s_rec"], 4 * i + u + 1)
                    nc.gpsimd.tensor_tensor(sm[:, u % 2], sm[:, u % 2], s1rec[:, u % 2].unsqueeze(2).to_broadcast([P, R, P]),
                                            ALU.mult).then_inc(S["s_pn"], 1)
                return fn

            def n1(i):
                rsqrt(i, "n1", f_mv[:, 1], f_ve[:, 1], f_rs[:, 1], f_sh[:, 1])

            def x2_plus(i):
                nc.gpsimd.tensor_tensor(xb[:], x2n[:], row["beta"], ALU.add).then_inc(S["xb"], 1)

            def x2T(i):
                pool.wait_ge(S["x2_hi"], i + 1)
                nc.gpsimd.tensor_tensor(x2[1][:], x2n[:], f(x2[0][:]), ALU.subtract).then_inc(S["x2_lo"], 1)

            def g2c(i):
                for b in range(G):
                    pool.wait_ge(S["g2_p"], H2 * (G * i + b + 1))
                    pool.wait_ge(S["g2_r"], G * i + b + 1)
                    nc.gpsimd.tensor_tensor(t2[:, b], t2[:, b], b_small[:, 7, b].unsqueeze(2).to_broadcast([P, H2, P]),
                                            ALU.mult).then_inc(S["g2_pn"], 1)

            def h_low(h):
                def fn(i):
                    pool.wait_ge(S["h_hi"], H2 * i + h + 1)
                    nc.gpsimd.tensor_tensor(hT[1][:, h], he[:, h % 2].rearrange("p (c n) -> p c n", c=C), f(hT[0][:, h]),
                                            ALU.subtract).then_inc(S["h_lo"], 1)
                return fn

            def oT_(i):
                pool.wait_ge(S["oT_ps"], i + 1)
                nc.gpsimd.tensor_tensor(ob[:], ob[:], row["b2"], ALU.add).then_inc(S["ob"], 1)

            def n2(i):
                rsqrt(i, "n2", b_mv[:, 0], b_ve[:, 0], b_rs[:, 0], b_sh[:, 0])

            def n2c(i):
                pool.wait_ge(S["n2"], G * (i + 1))
                nc.gpsimd.tensor_tensor(ob[:], ob[:], row["gamma"], ALU.mult).then_inc(S["n2g"], 1)
                pool.wait_ge(S["n2g"], i + 1)
                nc.gpsimd.tensor_tensor(ob[:], ob[:], xb[:], ALU.add).then_inc(S["y3"], 1)

            def n3(i):
                rsqrt(i, "n3", b_mv[:, 1], b_ve[:, 1], b_rs[:, 1], b_sh[:, 1])

            def x3T(i):
                pool.wait_ge(S["x3"], G * (i + 1))
                nc.gpsimd.tensor_tensor(x3d[:], ob[:], row["b3"], ALU.add).then_inc(S["x3d"], 1)

            def n4(i):
                rsqrt(i, "n4", b_mv[:, 2], b_ve[:, 2], b_rs[:, 2], b_sh[:, 2])

            rounds(pool, {
                "x0": x0, "n0": n0, "xr": x1_plus, "xb": x2_plus, "eA": norm_probs(0), "eB": norm_probs(1), "eC": norm_probs(2),
                "eD": norm_probs(3), "n1": n1, "x2T": x2T, "g2c": g2c, "hh0": h_low(0), "hh1": h_low(1),
                "hh2": h_low(2), "hh3": h_low(3), "oT": oT_, "n2": n2, "n2c": n2c, "n3": n3, "x3T": x3T, "n4": n4})

        @block.scalar
        def _(act):
            act.wait_ge(S["prep"], 1)

            def high(name, count, dst, src, ready, func=ACT.Identity, **kw):
                act.wait_ge(S[ready], count)
                nc.scalar.activation(dst, src, func, **kw).then_inc(S[name], 1)

            def whh(i, n, pair, bank0, graphs=range(G)):
                for b in graphs:
                    high(n + "_hi", G * i + b + 1, pair[0][:, b], ps[:, bank0 + b, 0:D], n + "_ps")

            def scaled(i, n, small, m, t, slope, T, b=0, G_=1):
                act.wait_ge(S[n + "_d"], 5 * (G_ * i + b + 1))
                for k in range(T):
                    nc.scalar.activation(t[:, k], m[:, k], ACT.Identity, bias=small(5)[:, k:k + 1], scale=slope) \
                      .then_inc(S[n + "_t"], 1)

            def exps(i, n, small, m, t, T, b=0, G_=1):
                for k in range(T):
                    act.wait_ge(S[n + "_w"], T * (G_ * i + b) + k + 1)
                    nc.scalar.activation(t[:, k], m[:, k], ACT.Exp, accum_out=small(6)[:, k:k + 1]) \
                      .then_inc(S[n + "_p"], 1)

            s0 = lambda j: f_small[:, j]
            s3 = lambda j: c_small[:, j]

            def wh_(i):
                whh(i, "wh", wh, 0)

            def g0b(i):
                scaled(i, "g0", s0, m0, t0, SLOPE0, G)

            def g0c(i):
                exps(i, "g0", s0, m0, t0, G)

            def pt0(i):
                if not first(i):
                    act.wait_ge(S["k_stack"], STACK * i)
                high("p0_hi", i + 1, p0[0], ps[:, 1, 0:G * P].rearrange("p (g n) -> p g n", g=G), "p0_ps")

            def x1T(i):
                high("x1T_hi", i + 1, x1T_[0], ps[:, 1, :].rearrange("p (c n) -> p c n", c=C), "x1T_ps")

            def qk(i):
                for n, pair, bank, bias in (("q", qq, 0, BQ), ("k", kk, 1, BK)):
                    for t in range(C):
                        high(n + "_hi", C * (i + 1), pair[0][:, t], ps[:, bank, t * G * P:(t + 1) * G * P], n + "_ps",
                             bias=colsb[:, bias, t:t + 1])

            def v(i):
                high("v_hi", G * (i + 1), val[0][:].rearrange("p g d -> p (g d)"), ps[:, 0, :], "v_ps")

            def probs(u):
                def fn(i):
                    act.wait_ge(S["sneg"], 4 * i + u + 1)
                    for r in range(R):
                        nc.scalar.activation(sm[:, u % 2, r], ps[:, 2 + u % 2, r * P:(r + 1) * P], ACT.Exp, bias=s1neg[:, u % 2, r:r + 1],
                                             scale=SCALE, accum_out=s1sum[:, u % 2, r:r + 1]).then_inc(S["s_p"], 1)
                return fn

            def probsT(u):
                def fn(i):
                    high("p1_hi", 4 * i + u + 1, pT[0][:, u % 2], ps[:, 2 + u % 2, :], "p1_ps")
                return fn

            def heads_out(t):
                def fn(i):
                    act.wait_ge(S["o_ps"], 4 * i + G * (t + 1))
                    for r in range(R):
                        q = slice(DH * r, DH * (r + 1))
                        nc.scalar.activation(oT[0][q, t].rearrange("p (g n) -> p g n", g=G), ps[q, 2:2 + G, r * P:(r + 1) * P],
                                             ACT.Identity, bias=colsb[q, BV, t:t + 1]).then_inc(S["o_hi"], 1)
                return fn

            def normed(n, name, dst, rs, shift):
                def fn(i):
                    act.wait_ge(S[n + "_rs"], 4 * (i + 1))
                    for b in range(G):
                        nc.scalar.activation(dst[:, b], dst[:, b], ACT.Identity, bias=shift[:, b:b + 1], scale=rs[:, b:b + 1]) \
                          .then_inc(S[name], 1)
                return fn

            def x2T(i):
                act.wait_ge(S["x2"], G * (i + 1))
                nc.scalar.activation(x2[0][:], x2n[:], ACT.Identity).then_inc(S["x2_hi"], 1)
                high("x2T_hi", i + 1, bT[0][:].rearrange("p c n -> p (c n)"), ps[:, 4, :], "x2T_ps")

            def g2b(i):
                for b in range(G):
                    scaled(i, "g2", lambda j: b_small[:, j, b], m2[:, b], t2[:, b], SLOPE2, H2, b, G)

            def g2c(i):
                for b in range(G):
                    exps(i, "g2", lambda j: b_small[:, j, b], m2[:, b], t2[:, b], H2, b, G)

            def g2d(i):
                for b in range(G):
                    high("p2_hi", G * i + b + 1, p2[0][:, b], ps[:, 4 + b, :], "p2_ps")

            def gx(b):
                def fn(i):
                    for c in range(C):
                        high("g_hi", C * (G * i + b) + c + 1, hT[0][:, :, c, node(b)],
                             ps[:, 4 + c, :].rearrange("p (h n) -> p h n", h=H2), "g_ps")
                return fn

            def hT_(h):
                def fn(i):
                    if h >= 2:
                        act.wait_ge(S["h_lo"], H2 * i + h - 1)
                    high("h_e", H2 * i + h + 1, he[:, h % 2], ps[:, 4 + h % 2, :], "h_ps", ACT.Exp)
                return fn

            def h_high(h):
                def fn(i):
                    act.wait_ge(S["h_f"], H2 * i + h + 1)
                    nc.scalar.activation(hT[0][:, h].rearrange("p c n -> p (c n)"), he[:, h % 2], ACT.Identity) \
                      .then_inc(S["h_hi"], 1)
                return fn

            def wh3_(b):
                def fn(i):
                    whh(i, "wh3", wh3, 4, [b])
                return fn

            def g3b(i):
                scaled(i, "g3", s3, m3, t3, SLOPE2, G)

            def g3c(i):
                exps(i, "g3", s3, m3, t3, G)

            def pt3(i):
                high("p3_hi", i + 1, p3[0], ps[:, 7, 0:G * P].rearrange("p (g n) -> p g n", g=G), "p3_ps")

            def av3(i):
                act.wait_ge(S["out"], 16 * (i + 1))
                act.wait_ge(S["g3_r"], i + 1)
                for b in range(G):
                    high("o3_e", G * (i + 1), ob[:, b], ps[:, 6, b * D:(b + 1) * D], "av3_ps", ACT.Exp,
                         scale=c_small[:, 7, b:b + 1])

            def oT_(i):
                high("oT_hi", i + 1, cT[0][:].rearrange("p c n -> p (c n)"), ps[:, 7, :], "oT_ps")

            def f1(i):
                for t in range(C):
                    high("hid_hi", C * (i + 1), hid[0][:, t], ps[:, 6, t * G * P:(t + 1) * G * P], "f1_ps", ACT.Relu,
                         bias=colsb[:, B1, t:t + 1])

            def x3T(i):
                high("x3T_hi", i + 1, cT[0][:].rearrange("p c n -> p (c n)"), ps[:, 6, :], "x3T_ps")

            def mm(i):
                for b in range(G):
                    high("mj_hi", G * i + b + 1, mj[0][:, b], ps[:, 6 + b, D:2 * D], "mm_ps")

            rounds(act, {
                "wh": wh_, "g0b": g0b, "g0c": g0c, "pt0": pt0, "x1T": x1T, "qk": qk, "v": v,
                "eA": probs(0), "eB": probs(1), "eC": probs(2), "eD": probs(3),
                "pA": probsT(0), "pB": probsT(1), "pC": probsT(2), "pD": probsT(3),
                "oA": heads_out(0), "oB": heads_out(1),
                "n0b": normed("n0", "x1", xn, f_rs[:, 0], f_sh[:, 0]), "n1b": normed("n1", "x2", x2n, f_rs[:, 1], f_sh[:, 1]),
                "n2b": normed("n2", "n2", ob, b_rs[:, 0], b_sh[:, 0]), "n3b": normed("n3", "x3", ob, b_rs[:, 1], b_sh[:, 1]),
                "n4b": normed("n4", "x4", ob, b_rs[:, 2], b_sh[:, 2]),
                "x2T": x2T, "g2b": g2b, "g2c": g2c, "g2d": g2d, "gx0": gx(0), "gx1": gx(1), "hT0": hT_(0), "hT1": hT_(1),
                "hT2": hT_(2), "hT3": hT_(3), "hh0": h_high(0), "hh1": h_high(1), "hh2": h_high(2), "hh3": h_high(3),
                "wh3_0": wh3_(0), "wh3_1": wh3_(1), "g3b": g3b, "g3c": g3c, "pt3": pt3, "av3": av3,
                "oT": oT_, "f1": f1, "x3T": x3T, "mm": mm})

        @block.vector
        def _(dve):
            V = nc.vector
            dve.wait_ge(S["prep_dma"], 16 * 8)
            chain = [0]

            def link(ins):
                chain[0] += 1
                ins.then_inc(S["prep_w"], 1)
                dve.wait_ge(S["prep_w"], chain[0])

            rows0 = m2[:].rearrange("p g h n -> p (g h n)"), t2[:].rearrange("p g h n -> p (g h n)"), he[:].rearrange("p g n -> p (g n)")

            def att(k):
                per = G * H2 * P // D
                return rows0[k // per][:, (k % per) * D:(k % per + 1) * D]

            scr = sm[:, 0].rearrange("p r n -> p (r n)")[:, 0:D]
            raw0, rawo = view(w_raw, "W0", C, D + 2), view(w_raw, "Wout", H2 * C, D + 2)
            rawh, rawa = view(w_raw, "Wh", H2, C, D), view(w_raw, "Wa", C, P)

            def product(weight, k, dst):
                link(V.tensor_tensor_reduce(out=scr, in0=weight, in1=att(k), scale=1.0, scalar=0.0, op0=ALU.mult,
                                            op1=ALU.add, accum_out=dst))

            for s in range(2):
                for c in range(C):
                    product(raw0[:, c, 0:D], s, raw0[:, c, D + s:D + s + 1])
                for c in range(H2 * C):
                    product(rawo[:, c, 0:D], 2 + s, rawo[:, c, D + s:D + s + 1])
                for h in range(H2):
                    for c in range(C):
                        product(rawh[:, h, c], 4 + 2 * h + s, rawa[:, c, s * H2 + h:s * H2 + h + 1])
            link(V.tensor_copy(view(w_raw, "adjT"), adjt_i[:]))
            link(V.tensor_copy(adj_f[:], adj_i[:]))
            link(V.tensor_scalar(mask[:], adj_f[:], 0.0, MASK, ALU.is_equal, ALU.mult))
            link(V.tensor_scalar(mask2[:], adj_f[:], 0.0, MASK, ALU.is_le, ALU.mult))
            link(V.reduce_sum(deg[:], adj_f[:], axis=AX))
            link(V.tensor_reduce(valid[:, 0:1], mask[:], AX, ALU.max))
            link(V.tensor_scalar(valid[:, 1:2], valid[:, 0:1], 0.0, None, ALU.is_equal))
            link(V.reciprocal(valid[:, 0:1], valid[:, 1:2]))
            link(V.tensor_tensor(valid[:, 2:3], valid[:, 0:1], valid[:, 1:2], ALU.mult))
            link(V.tensor_scalar(rowsb[:, 4], rowsb[:, 4], deg[:], None, ALU.mult))
            link(V.tensor_copy(w_hi[:], w_raw[:]))
            link(V.tensor_tensor(w_lo[:], w_raw[:], f(w_hi[:]), ALU.subtract))
            dve.wait_ge(S["prep_id"], 5)
            link(V.tensor_copy(ident_b[:], ident[:]))
            V.tensor_copy(mask_r[:], mask[:].unsqueeze(1).to_broadcast([P, R, P])).then_inc(S["prep"], 1)

            def low(name, count, dst, src, high_, ready, hi_count=None):
                dve.wait_ge(S[ready], count if hi_count is None else hi_count)
                V.tensor_tensor(dst, src, f(high_), ALU.subtract).then_inc(S[name], 1)

            def edge_columns(i, n, ec, pair, bank0, e_name, graphs=range(G)):
                for b in graphs:
                    dve.wait_ge(S[n + "_hi"], G * i + b + 1)
                    V.tensor_copy(ec[:, b], ps[:, bank0 + b, D:D + 2]).then_inc(S[e_name], 1)
                for b in graphs:
                    low(n + "_lo", G * i + b + 1, pair[1][:, b], ps[:, bank0 + b, 0:D], pair[0][:, b], n + "_hi")

            def front_of_softmax(k, n, small, z, msk, m, es, slope, T):
                V.tensor_tensor(m, z, msk[:].unsqueeze(1).to_broadcast([P, T, P]), ALU.add).then_inc(S[n + "_m"], 1)
                dve.wait_ge(S[n + "_m"], k + 1)
                V.tensor_reduce(small(1), m, AX, ALU.max).then_inc(S[n + "_d"], 1)
                dve.wait_ge(S[n + "_d"], 5 * k + 1)
                V.tensor_tensor(small(2), es, small(1), ALU.add).then_inc(S[n + "_d"], 1)
                dve.wait_ge(S[n + "_d"], 5 * k + 2)
                V.scalar_tensor_tensor(small(3), small(2), slope, small(2), ALU.mult, ALU.max).then_inc(S[n + "_d"], 1)
                dve.wait_ge(S[n + "_d"], 5 * k + 3)
                V.tensor_tensor(small(4), es, small(3), ALU.subtract).then_inc(S[n + "_d"], 1)
                V.scalar_tensor_tensor(small(5), es, slope, small(3), ALU.mult, ALU.subtract).then_inc(S[n + "_d"], 1)

            def larger(k, n, small, m, t, T):
                dve.wait_ge(S[n + "_d"], 5 * k + 5)
                for j in range(T):
                    dve.wait_ge(S[n + "_t"], T * k + j + 1)
                    V.scalar_tensor_tensor(m[:, j], m[:, j], small(4)[:, j:j + 1], t[:, j], ALU.add, ALU.max) \
                     .then_inc(S[n + "_w"], 1)

            def stats(i, n, src, bn, mv):
                for b in range(G):
                    V.bn_stats(bn[:, b], src[:, b]).then_inc(S[n + "_st"], 1)
                dve.wait_ge(S[n + "_st"], G * (i + 1))
                V.memset(tick[:], 0.0)
                for b in range(G):
                    V.bn_aggr(mv[:, b], bn[:, b]).then_inc(S[n + "_mv"], 1)

            s0 = lambda j: f_small[:, j]
            s3 = lambda j: c_small[:, j]

            def x0(i):
                dve.wait_ge(S["xt_in"], 16 * (i + 1))
                if not first(i):
                    dve.wait_ge(S["q_stack"], STACK * i)
                V.tensor_copy(xT[0][:], xt[:]).then_inc(S["xt_hi"], 1)

            def wh_(i):
                edge_columns(i, "wh", ec0, wh, 0, "ec0")

            def g0a(i):
                dve.wait_ge(S["z0_ps"], i + 1)
                dve.wait_ge(S["ec0"], G * (i + 1))
                front_of_softmax(i, "g0", s0, ps[:, 0, 0:G * P].rearrange("p (g n) -> p g n", g=G), mask, m0,
                                 ec0[:, :, 0], SLOPE0, G)

            def g0b(i):
                larger(i, "g0", s0, m0, t0, G)

            def g0c(i):
                dve.wait_ge(S["g0_p"], G * (i + 1))
                V.reciprocal(s0(7), s0(6)).then_inc(S["g0_r"], 1)
                dve.wait_ge(S["g0_r"], 2 * i + 1)
                V.tensor_scalar(s0(7), s0(7), valid[:, 1:2], None, ALU.mult).then_inc(S["g0_r"], 1)

            def pt0(i):
                low("p0_lo", i + 1, p0[1], ps[:, 1, 0:G * P].rearrange("p (g n) -> p g n", g=G), p0[0], "p0_hi")

            def av0(i):
                dve.wait_ge(S["x_in"], 16 * (i + 1))
                dve.wait_ge(S["g0_r"], 2 * (i + 1))
                dve.wait_ge(S["av0_ps"], G * (i + 1))
                for b in range(G):
                    V.scalar_tensor_tensor(xn[:, b], ps[:, 0, b * D:(b + 1) * D], s0(7)[:, b:b + 1], xn[:, b], ALU.mult, ALU.add) \
                     .then_inc(S["y0"], 1)

            def n0(i):
                dve.wait_ge(S["y0"], G * (i + 1))
                stats(i, "n0", xn, f_bn[:, 0], f_mv[:, 0])

            def x1T(i):
                low("x1T_lo", i + 1, x1T_[1], ps[:, 1, :].rearrange("p (c n) -> p c n", c=C), x1T_[0], "x1T_hi")

            def qk(i):
                for n, pair, bank, bias in (("q", qq, 0, BQ), ("k", kk, 1, BK)):
                    dve.wait_ge(S[n + "_hi"], C * (i + 1))
                    for t in range(C):
                        V.scalar_tensor_tensor(pair[1][:, t], ps[:, bank, t * G * P:(t + 1) * G * P],
                                               colsb[:, bias, t:t + 1], f(pair[0][:, t]), ALU.add, ALU.subtract) \
                         .then_inc(S[n + "_lo"], 1)

            def v(i):
                low("v_lo", i + 1, val[1][:].rearrange("p g d -> p (g d)"), ps[:, 0, :],
                    val[0][:].rearrange("p g d -> p (g d)"), "v_hi")

            def scores(u):
                def fn(i):
                    w = u % 2
                    dve.wait_ge(S["s_ps"], 4 * i + u + 1)
                    V.tensor_reduce(s1max[:, w], ps[:, 2 + w, :].rearrange("p (r n) -> p r n", r=R), AX, ALU.max) \
                     .then_inc(S["smax"], 1)
                    dve.wait_ge(S["smax"], 4 * i + u + 1)
                    V.tensor_scalar(s1neg[:, w], s1max[:, w], -SCALE, None, ALU.mult).then_inc(S["sneg"], 1)
                return fn

            def sums(u):
                def fn(i):
                    w = u % 2
                    dve.wait_ge(S["s_p"], R * (4 * i + u + 1))
                    V.reciprocal(s1rec[:, w], s1sum[:, w]).then_inc(S["s_rec0"], 1)
                    dve.wait_ge(S["s_rec0"], 4 * i + u + 1)
                    V.tensor_scalar(s1rec[:, w], s1rec[:, w], valid[:, 2:3], None, ALU.mult).then_inc(S["s_rec"], 1)
                return fn

            def probsT(u):
                def fn(i):
                    w = u % 2
                    low("p1_lo", 4 * i + u + 1, pT[1][:, w], ps[:, 2 + w, :], pT[0][:, w], "p1_hi")
                return fn

            def heads_out(t):
                def fn(i):
                    for r in range(R):
                        q = slice(DH * r, DH * (r + 1))
                        dve.wait_ge(S["o_hi"], C * R * i + R * t + r + 1)
                        V.scalar_tensor_tensor(oT[1][q, t].rearrange("p (g n) -> p g n", g=G), ps[q, 2:2 + G, r * P:(r + 1) * P],
                                               colsb[q, BV, t:t + 1], f(oT[0][q, t].rearrange("p (g n) -> p g n", g=G)),
                                               ALU.add, ALU.subtract).then_inc(S["o_lo"], 1)
                return fn

            def wo(i):
                dve.wait_ge(S["wo_ps"], i + 1)
                dve.wait_ge(S["xr"], i + 1)
                if not first(i):
                    dve.wait_ge(S["xb"], i)
                V.tensor_tensor(x2n[:].rearrange("p g d -> p (g d)"), ps[:, 2, :], xr[:].rearrange("p g d -> p (g d)"), ALU.add) \
                 .then_inc(S["y1"], 1)

            def n1(i):
                dve.wait_ge(S["y1"], i + 1)
                stats(i, "n1", x2n, f_bn[:, 1], f_mv[:, 1])

            def x2T(i):
                low("x2T_lo", i + 1, bT[1][:].rearrange("p c n -> p (c n)"), ps[:, 4, :],
                    bT[0][:].rearrange("p c n -> p (c n)"), "x2T_hi")

            def er(i):
                dve.wait_ge(S["er_ps"], i + 1)
                V.tensor_copy(eT[:], ps[0:2 * H2, 5, 0:G * P]).then_inc(S["eT"], 1)

            def ec(i):
                dve.wait_ge(S["ec_ps"], i + 1)
                V.tensor_copy(ec2[:], ps[:, 4, 0:G * 2 * H2].rearrange("p (g e) -> p g e", g=G)).then_inc(S["ec2"], 1)

            def g2a(i):
                dve.wait_ge(S["ec2"], i + 1)
                for b in range(G):
                    dve.wait_ge(S["z2_ps"], G * i + b + 1)
                    front_of_softmax(G * i + b, "g2", lambda j: b_small[:, j, b],
                                     ps[:, 4 + b, :].rearrange("p (h n) -> p h n", h=H2), mask2, m2[:, b],
                                     ec2[:, b, 0:H2], SLOPE2, H2)

            def g2b(i):
                for b in range(G):
                    larger(G * i + b, "g2", lambda j: b_small[:, j, b], m2[:, b], t2[:, b], H2)

            def g2c(i):
                for b in range(G):
                    dve.wait_ge(S["g2_p"], H2 * (G * i + b + 1))
                    V.reciprocal(b_small[:, 7, b], b_small[:, 6, b]).then_inc(S["g2_r"], 1)

            def g2d(i):
                for b in range(G):
                    low("p2_lo", G * i + b + 1, p2[1][:, b], ps[:, 4 + b, :], p2[0][:, b], "p2_hi")

            def gx(b):
                def fn(i):
                    for c in range(C):
                        low("g_lo", C * (G * i + b) + c + 1, hT[1][:, :, c, node(b)],
                            ps[:, 4 + c, :].rearrange("p (h n) -> p h n", h=H2), hT[0][:, :, c, node(b)], "g_hi")
                return fn

            def hT_(h):
                def fn(i):
                    k = H2 * i + h + 1
                    dve.wait_ge(S["h_e"], k)
                    V.tensor_scalar(he[:, h % 2], he[:, h % 2], 1.0, -1.0, ALU.min, ALU.add).then_inc(S["h_e1"], 1)
                    dve.wait_ge(S["h_e1"], k)
                    V.tensor_tensor(he[:, h % 2], ps[:, 4 + h % 2, :], he[:, h % 2], ALU.max) \
                     .then_inc(S["h_f"], 1)
                return fn

            def wh3_(b):
                def fn(i):
                    edge_columns(i, "wh3", ec3, wh3, 4, "ec3", [b])
                return fn

            def g3a(i):
                dve.wait_ge(S["z3_ps"], i + 1)
                dve.wait_ge(S["ec3"], G * (i + 1))
                front_of_softmax(i, "g3", s3, ps[:, 6, 0:G * P].rearrange("p (g n) -> p g n", g=G), mask2, m3,
                                 ec3[:, :, 0], SLOPE2, G)

            def g3b(i):
                larger(i, "g3", s3, m3, t3, G)

            def g3c(i):
                dve.wait_ge(S["g3_p"], G * (i + 1))
                V.reciprocal(s3(7), s3(6)).then_inc(S["g3_r"], 1)

            def pt3(i):
                low("p3_lo", i + 1, p3[1], ps[:, 7, 0:G * P].rearrange("p (g n) -> p g n", g=G), p3[0], "p3_hi")

            def av3(i):
                dve.wait_ge(S["g3_r"], i + 1)
                dve.wait_ge(S["o3_e"], G * (i + 1))
                V.tensor_scalar(ob[:], ob[:], 1.0, -1.0, ALU.min, ALU.add).then_inc(S["o3_e1"], 1)
                dve.wait_ge(S["o3_e1"], i + 1)
                for b in range(G):
                    V.scalar_tensor_tensor(ob[:, b], ps[:, 6, b * D:(b + 1) * D], s3(7)[:, b:b + 1], ob[:, b], ALU.mult, ALU.max) \
                     .then_inc(S["o3"], 1)

            def oT_(i):
                low("oT_lo", i + 1, cT[1][:].rearrange("p c n -> p (c n)"), ps[:, 7, :],
                    cT[0][:].rearrange("p c n -> p (c n)"), "oT_hi")

            def f1(i):
                dve.wait_ge(S["hid_hi"], C * (i + 1))
                for t in range(C):
                    V.tensor_scalar(hidf[:, t], ps[:, 6, t * G * P:(t + 1) * G * P], colsb[:, B1, t:t + 1], 0.0,
                                    ALU.add, ALU.max).then_inc(S["hid_f"], 1)
                for t in range(C):
                    dve.wait_ge(S["hid_f"], C * i + t + 1)
                    low("hid_lo", C * i + t + 1, hid[1][:, t], hidf[:, t], hid[0][:, t], "hid_hi")

            def f2(i):
                dve.wait_ge(S["f2_ps"], i + 1)
                dve.wait_ge(S["ob"], i + 1)
                V.tensor_tensor(ob[:].rearrange("p g d -> p (g d)"), ps[:, 7, :], ob[:].rearrange("p g d -> p (g d)"), ALU.add) \
                 .then_inc(S["y2"], 1)

            def n2(i):
                dve.wait_ge(S["y2"], i + 1)
                stats(i, "n2", ob, b_bn[:, 0], b_mv[:, 0])

            def n3(i):
                dve.wait_ge(S["y3"], i + 1)
                stats(i, "n3", ob, b_bn[:, 1], b_mv[:, 1])

            def x3T(i):
                low("x3T_lo", i + 1, cT[1][:].rearrange("p c n -> p (c n)"), ps[:, 6, :],
                    cT[0][:].rearrange("p c n -> p (c n)"), "x3T_hi")

            def mm(i):
                dve.wait_ge(S["x3d"], i + 1)
                for b in range(G):
                    dve.wait_ge(S["mj_hi"], G * i + b + 1)
                    V.scalar_tensor_tensor(x3d[:, b], ps[:, 6 + b, 0:D], deg[:], x3d[:, b], ALU.mult, ALU.add) \
                     .then_inc(S["x3m"], 1)
                    low("mj_lo", G * i + b + 1, mj[1][:, b], ps[:, 6 + b, D:2 * D], mj[0][:, b], "mj_hi")

            def am(i):
                dve.wait_ge(S["x3m"], G * (i + 1))
                dve.wait_ge(S["am_ps"], i + 1)
                V.tensor_tensor(ob[:].rearrange("p g d -> p (g d)"), ps[:, 6, :], x3d[:].rearrange("p g d -> p (g d)"), ALU.add) \
                 .then_inc(S["y4"], 1)

            def n4(i):
                dve.wait_ge(S["y4"], i + 1)
                stats(i, "n4", ob, b_bn[:, 2], b_mv[:, 2])

            rounds(dve, {
                "x0": x0, "wh": wh_, "g0a": g0a, "g0b": g0b, "g0c": g0c, "pt0": pt0, "av0": av0, "n0": n0, "x1T": x1T,
                "qk": qk, "v": v, "sA": scores(0), "sB": scores(1), "sC": scores(2), "sD": scores(3),
                "eA": sums(0), "eB": sums(1), "eC": sums(2), "eD": sums(3),
                "pA": probsT(0), "pB": probsT(1), "pC": probsT(2), "pD": probsT(3), "oA": heads_out(0), "oB": heads_out(1),
                "wo": wo, "n1": n1,
                "x2T": x2T, "er": er, "ec": ec, "g2a": g2a, "g2b": g2b, "g2c": g2c, "g2d": g2d, "gx0": gx(0), "gx1": gx(1),
                "hT0": hT_(0), "hT1": hT_(1), "hT2": hT_(2), "hT3": hT_(3), "wh3_0": wh3_(0), "wh3_1": wh3_(1),
                "g3a": g3a, "g3b": g3b, "g3c": g3c, "pt3": pt3, "av3": av3, "oT": oT_, "f1": f1, "f2": f2,
                "n2": n2, "n3": n3, "x3T": x3T, "mm": mm, "am": am, "n4": n4})

        @block.tensor
        def _(pe):
            T_ = nc.tensor
            pe.wait_ge(S["prep"], 1)

            def transposes(src, bank):
                for b in range(G):
                    for c in range(C):
                        last = T_.transpose(ps[:, bank, (c * G + b) * P:(c * G + b + 1) * P], src[:, b, c * P:(c + 1) * P], ident[:])
                return last

            def natural(bank, off, width, xt_, b, w, stop_chunks=C):
                for c in range(C):
                    last = three(pe, ps[:, bank, off:off + width], part(xt_, ALL, c, node(b)), part(w, ALL, c, slice(0, width)),
                                 c == 0, c == C - 1)
                return last

            def transposed(bank, t, w, xt_):
                for c in range(C):
                    last = three(pe, ps[:, bank, t * G * P:(t + 1) * G * P], part(w, ALL, c, slice(t * P, (t + 1) * P)),
                                 part(xt_, ALL, c), c == 0, c == C - 1)
                return last

            def spread(bank, off, col):
                return T_.transpose(ps[:, bank, off:off + P], col.to_broadcast([P, P]), ident[:])

            def wh_(i):
                pe.wait_ge(S["xt_lo"], i + 1)
                for b in range(G):
                    natural(b, 0, D + 2, xT, b, W0).then_inc(S["wh_ps"], 1)

            def g0a(i):
                pe.wait_ge(S["wh_lo"], G * (i + 1))
                for b in range(G):
                    last = spread(0, b * P, ec0[:, b, 1:2])
                last.then_inc(S["z0_ps"], 1)

            def pt0(i):
                pe.wait_ge(S["g0_p"], G * (i + 1))
                for b in range(G):
                    last = T_.transpose(ps[:, 1, b * P:(b + 1) * P], t0[:, b], ident[:])
                last.then_inc(S["p0_ps"], 1)

            def av0(i):
                pe.wait_ge(S["p0_lo"], i + 1)
                pe.wait_ge(S["wh_lo"], G * (i + 1))
                for b in range(G):
                    three(pe, ps[:, 0, b * D:(b + 1) * D], part(p0, ALL, b), part(wh, ALL, b), True, True).then_inc(S["av0_ps"], 1)

            def x1T(i):
                pe.wait_ge(S["x1"], G * (i + 1))
                transposes(xn, 1).then_inc(S["x1T_ps"], 1)

            def qk(i):
                pe.wait_ge(S["x1T_lo"], i + 1)
                for n, w, bank in (("q", Wq, 0), ("k", Wk, 1)):
                    for t in range(C):
                        transposed(bank, t, w, x1T_).then_inc(S[n + "_ps"], 1)

            def v(i):
                pe.wait_ge(S["q_lo"], C * (i + 1))
                for b in range(G):
                    natural(0, b * D, D, x1T_, b, Wv).then_inc(S["v_ps"], 1)

            def scores(u):
                t, b = divmod(u, G)

                def fn(i):
                    if u == 0:
                        if not first(i):
                            pe.wait_ge(S["y1"], i)
                        pe.wait_ge(S["q_stack"], STACK * (i + 1))
                        pe.wait_ge(S["k_stack"], STACK * (i + 1))
                    elif u >= 2:
                        pe.wait_ge(S["o_lo"], C * R * i + R)
                    T_.matmul(ps[:, 2 + u % 2, :], ident_b[:], mask_r[:].rearrange("p r n -> p (r n)"), start=True, stop=False)
                    for r in range(R):
                        last = T_.matmul(ps[:, 2 + u % 2, r * P:(r + 1) * P], qs[:, r, t, node(b)], ks[:, r, t, node(b)],
                                         start=False, stop=r == R - 1)
                    last.then_inc(S["s_ps"], 1)
                return fn

            def probsT(u):
                t, b = divmod(u, G)

                def fn(i):
                    pe.wait_ge(S["s_pn"], 4 * i + u + 1)
                    for r in range(R):
                        last = T_.transpose(ps[:, 2 + b, r * P:(r + 1) * P], sm[:, u % 2, r], ident[:])
                    last.then_inc(S["p1_ps"], 1)
                return fn

            def heads(t):
                def fn(i):
                    pe.wait_ge(S["v_lo"], i + 1)
                    for b in range(G):
                        u = G * t + b
                        pe.wait_ge(S["p1_lo"], 4 * i + u + 1)
                        three(pe, ps[:, 2 + b, :], part(val, ALL, b, slice(t * P, (t + 1) * P)), part(pT, ALL, u % 2), True, True) \
                            .then_inc(S["o_ps"], 1)
                return fn

            def wo(i):
                pe.wait_ge(S["o_lo"], C * R * (i + 1))
                for b in range(G):
                    last = natural(2, b * D, D, oT, b, Wo)
                last.then_inc(S["wo_ps"], 1)

            def x2T(i):
                pe.wait_ge(S["x2"], G * (i + 1))
                if not first(i):
                    pe.wait_ge(S["wh3_lo"], G * i)
                transposes(x2n, 4).then_inc(S["x2T_ps"], 1)

            def er(i):
                pe.wait_ge(S["x2T_lo"], i + 1)
                for c in range(C):
                    last = three(pe, ps[:, 5, 0:G * P], part(WA, ALL, c), part(bT, ALL, c), c == 0, c == C - 1)
                last.then_inc(S["er_ps"], 1)

            def ec(i):
                count = value(pe, i + 1)
                pe.wait_ge(S["prep"], 1)
                pe.wait_ge(S["eT"], count)
                for b in range(G):
                    last = T_.transpose(ps[:, 4, b * 2 * H2:(b + 1) * 2 * H2], eT[:, node(b)], ident[0:2 * H2, 0:2 * H2])
                last.then_inc(S["ec_ps"], 1)

            def g2a(i):
                pe.wait_ge(S["ec2"], i + 1)
                for b in range(G):
                    for h in range(H2):
                        last = spread(4 + b, h * P, ec2[:, b, H2 + h:H2 + h + 1])
                    last.then_inc(S["z2_ps"], 1)

            def g2d(i):
                for b in range(G):
                    pe.wait_ge(S["g2_pn"], G * i + b + 1)
                    for h in range(H2):
                        last = T_.transpose(ps[:, 4 + b, h * P:(h + 1) * P], t2[:, b, h], ident[:])
                    last.then_inc(S["p2_ps"], 1)

            def gx(b):
                def fn(i):
                    pe.wait_ge(S["x2_lo"], i + 1)
                    pe.wait_ge(S["p2_lo"], G * (i + 1))
                    for c in range(C):
                        if b:
                            pe.wait_ge(S["g_lo"], C * (G * i + b - 1) + c + 1)
                        three(pe, ps[:, 4 + c, :], part(x2, ALL, b, slice(c * P, (c + 1) * P)), part(p2, ALL, b), True, True) \
                            .then_inc(S["g_ps"], 1)
                return fn

            def hT_(h):
                def fn(i):
                    if h == 0:
                        pe.wait_ge(S["g_lo"], G * C * (i + 1))
                    if h >= 2:
                        pe.wait_ge(S["h_f"], H2 * i + h - 1)
                    for t in range(C):
                        for c in range(C):
                            last = three(pe, ps[:, 4 + h % 2, t * G * P:(t + 1) * G * P], part(WH, ALL, h, c, slice(t * P, (t + 1) * P)),
                                         part(hT, ALL, h, c), c == 0, c == C - 1)
                    last.then_inc(S["h_ps"], 1)
                return fn

            def wh3_(b):
                def fn(i):
                    pe.wait_ge(S["h_lo"], H2 * (i + 1))
                    for k in range(H2 * C):
                        last = three(pe, ps[:, 4 + b, 0:D + 2], part(hT, ALL, k // C, k % C, node(b)), part(WOUT, ALL, k), k == 0,
                                     k == H2 * C - 1)
                    last.then_inc(S["wh3_ps"], 1)
                return fn

            def g3a(i):
                pe.wait_ge(S["ec3"], G * (i + 1))
                if not first(i):
                    pe.wait_ge(S["y4"], i)
                for b in range(G):
                    last = spread(6, b * P, ec3[:, b, 1:2])
                last.then_inc(S["z3_ps"], 1)

            def pt3(i):
                pe.wait_ge(S["g3_p"], G * (i + 1))
                for b in range(G):
                    last = T_.transpose(ps[:, 7, b * P:(b + 1) * P], t3[:, b], ident[:])
                last.then_inc(S["p3_ps"], 1)

            def av3(i):
                pe.wait_ge(S["p3_lo"], i + 1)
                pe.wait_ge(S["wh3_lo"], G * (i + 1))
                for b in range(G):
                    three(pe, ps[:, 6, b * D:(b + 1) * D], part(p3, ALL, b), part(wh3, ALL, b), True, True).then_inc(S["av3_ps"], 1)

            def oT_(i):
                pe.wait_ge(S["o3"], G * (i + 1))
                transposes(ob, 7).then_inc(S["oT_ps"], 1)

            def f1(i):
                pe.wait_ge(S["oT_lo"], i + 1)
                for t in range(C):
                    transposed(6, t, W1, cT).then_inc(S["f1_ps"], 1)

            def f2(i):
                pe.wait_ge(S["hid_lo"], C * (i + 1))
                for b in range(G):
                    last = natural(7, b * D, D, hid, b, W2)
                last.then_inc(S["f2_ps"], 1)

            def x3T(i):
                pe.wait_ge(S["x3"], G * (i + 1))
                transposes(ob, 6).then_inc(S["x3T_ps"], 1)

            def mm(i):
                pe.wait_ge(S["x3T_lo"], i + 1)
                for b in range(G):
                    natural(6 + b, 0, 2 * D, cT, b, W3).then_inc(S["mm_ps"], 1)

            def am(i):
                pe.wait_ge(S["mj_lo"], G * (i + 1))
                for b in range(G):
                    T_.matmul(ps[:, 6, b * D:(b + 1) * D], ADJT, mj[1][:, b], start=True, stop=False)
                    last = T_.matmul(ps[:, 6, b * D:(b + 1) * D], ADJT, mj[0][:, b], start=False, stop=True)
                last.then_inc(S["am_ps"], 1)

            rounds(pe, {
                "wh": wh_, "g0a": g0a, "pt0": pt0, "av0": av0, "x1T": x1T, "qk": qk, "v": v,
                "sA": scores(0), "sB": scores(1), "sC": scores(2), "sD": scores(3),
                "pA": probsT(0), "pB": probsT(1), "pC": probsT(2), "pD": probsT(3), "oA": heads(0), "oB": heads(1), "wo": wo,
                "x2T": x2T, "er": er, "ec": ec, "g2a": g2a, "g2d": g2d, "gx0": gx(0), "gx1": gx(1), "hT0": hT_(0), "hT1": hT_(1), "hT2": hT_(2),
                "hT3": hT_(3), "wh3_0": wh3_(0), "wh3_1": wh3_(1), "g3a": g3a, "pt3": pt3, "av3": av3, "oT": oT_, "f1": f1, "f2": f2,
                "x3T": x3T, "mm": mm, "am": am})


def kernel(**inputs):
    import concourse.bacc as bacc
    from concourse.bass_utils import run_bass_kernel_spmd

    a = {k: np.asarray(v) for k, v in inputs.items()}
    x = a["x"]
    B = x.shape[0]
    NG = B // G

    def chunks(w):
        return w.reshape(-1, P, w.shape[1]).transpose(1, 0, 2)

    def padded(w):
        v = np.zeros((P, w.shape[0] // P, D + 2), np.float32)
        v[:, :, 0:D] = chunks(w)
        return v

    heads = a["L2_gnn_W_heads"]
    w3 = np.concatenate([a["L3_gnn_W"][:, :D].T, a["L3_gnn_W"][:, D:].T], axis=1)
    parts = {"W0": padded(a["L0_gnn_W"]), "Wq": chunks(a["L1_gnn_Wq"].T), "Wk": chunks(a["L1_gnn_Wk"].T),
             "Wv": chunks(a["L1_gnn_Wv"].T), "Wo": chunks(a["L1_gnn_Wo"].T),
             "Wh": chunks(heads.reshape(H2 * D, D)), "Wout": padded(a["L2_gnn_W_out"]), "w1": chunks(a["L2_gnn_w1"]),
             "w2": chunks(a["L2_gnn_w2"]), "W3": chunks(w3), "Wa": np.zeros((P, C * P), np.float32),
             "adjT": np.zeros((P, P), np.float32)}
    weights = np.concatenate([parts[n].reshape(P, -1) for n, _ in _COLS], axis=1)
    att = np.concatenate([a["L0_gnn_a_src"], a["L0_gnn_a_dst"], a["L2_gnn_a_out"], a["L2_gnn_a_heads"].reshape(-1)])
    rows = np.stack([a["L1_gnn_bo"], a["L2_gnn_b2"], a["L2_gnn_ln_gamma"], a["L2_gnn_ln_beta"], a["L3_gnn_b"]])
    cols = np.stack([a[n].reshape(C, P).T for n in ("L1_gnn_bq", "L1_gnn_bk", "L1_gnn_bv", "L2_gnn_b1")], axis=1)
    arrays = {
        "x_n": x,
        "x_t": x.reshape(NG, G, P, C, P).transpose(0, 4, 3, 1, 2).reshape(NG, P, C * G * P),
        "weights": weights, "adj": a["adj"], "adj_t": a["adj"].T,
        "att_rows": np.broadcast_to(att, (P, att.size)), "rows": np.broadcast_to(rows, (P,) + rows.shape), "cols": cols,
    }
    nc = bacc.Bacc("TRN2", target_bir_lowering=False, num_devices=1)
    args, feed = [], {}
    for name, v in arrays.items():
        v = np.ascontiguousarray(v)
        feed[f"in_{name}"] = v
        args.append(nc.dram_tensor(f"in_{name}", v.shape, mybir.dt.from_np(v.dtype), kind="ExternalInput").ap())
    out = nc.dram_tensor("out_x", x.shape, F32, kind="ExternalOutput").ap()
    build(nc, *args, out)
    r = run_bass_kernel_spmd(nc, [feed], core_ids=[0])
    return r.results[0]["out_x"]
```

```python
from contextlib import ExitStack

import numpy as np

import concourse.bass as bass
from concourse import mybir

F32 = mybir.dt.float32
F32R = mybir.dt.float32r
I32 = mybir.dt.int32
BF16 = mybir.dt.bfloat16
ALU = mybir.AluOpType
ACT = mybir.ActivationFunctionType
AX = mybir.AxisListType.X

P = 128
D = 256
C = D // P
G = 2
H1 = 8
DH = D // H1
R = P // DH
H2 = 4
MASK = -1.0e9
EPS = 1e-5
SLOPE0, SLOPE2 = 0.2, 0.01
STACK = 16 * 3 * R
SCALE = 1.0 / float(np.sqrt(DH))

_COLS = [("W0", C * (D + 2)), ("Wq", C * D), ("Wk", C * D), ("Wv", C * D), ("Wo", C * D),
         ("Wh", H2 * C * D), ("Wout", H2 * C * (D + 2)), ("w1", C * D), ("w2", C * D),
         ("W3", C * 2 * D), ("Wa", C * P), ("adjT", P)]
OFF = {}
WTOT = 0
for _n, _w in _COLS:
    OFF[_n] = (WTOT, WTOT + _w)
    WTOT += _w

SPLIT = (OFF["Wq"][0], OFF["Wh"][1]), (OFF["w1"][0], OFF["W3"][1])

ORDER = [tuple(x.split(":")) for x in """
    B2:g3a F2:sA F2:sB B2:g3b F1:x0 B1:g2a0 F2:eA F2:eB
    B1:g2a1 B2:g3c B1:g2b0 F1:wh0 F1:wh1 B2:pt3 B1:g2b1 F2:pA
    F2:pB B1:g2c0 B2:av3 B1:g2c1 F1:g0a F2:oA B2:oT B1:g2d0
    F1:g0b B1:g2d1 F2:sC F1:g0c B2:f1 F1:pt0 B1:gx0 F1:av0
    B2:f1h F2:oAh F2:sD F2:eC F1:n0 B1:gx1 B2:f2 F2:eD
    B2:n2 F1:n0b E:n4 B1:hT0 F1:x1T F2:pC B2:n2b B2:n2c
    F2:pD B1:hh0 B1:hT1 E:n4b B2:n3 F1:q F2:oB B1:hh1
    B1:hT2 B2:n3b B1:hT3 F2:oBh F1:k B2:x3T B1:hh2 F1:v
    B1:hh3 F2:wo M:n1 B2:mm0 B1:xb B2:mm1 M:n1b F1:xr
    B1:wh3_0 M:x2 B2:am M:x2T B1:wh3_1 M:er M:ec""".split()]
PARTS = {"F1": 0, "F2": 1, "M": 1, "B1": 2, "B2": 3, "E": 4}
_ROWS = ["bo", "b2", "gamma", "beta", "b3"]


def build(nc, x_n, x_t, weights, adj, adj_t, att_rows, rows, cols, out):
    B = x_n.shape[0]
    NG = B // G
    xn_v = x_n.rearrange("(g b) n d -> g n b d", b=G)
    out_v = out.rearrange("(g b) n d -> g n b d", b=G)

    with ExitStack() as ctx:
        def sb(name, shape, dt=F32):
            return ctx.enter_context(nc.sbuf_tensor(name, shape, dt))

        def sem(name):
            return ctx.enter_context(nc.semaphore(name))

        ps = ctx.enter_context(nc.psum_tensor("ps", [P, 8, 512], F32))

        w_hi = sb("w_hi", [P, WTOT], F32R)
        w_lo = sb("w_lo", [P, WTOT], F32R)
        rowsb = sb("rowsb", [P, len(_ROWS), D])
        colsb = sb("colsb", [P, 4, C])
        ident = sb("ident", [P, P])
        mask = sb("mask", [P, P])
        mask2 = sb("mask2", [P, P])
        mask_r = sb("mask_r", [P, R, P], BF16)
        tick = sb("tick", [P, 1])
        ident_b = sb("ident_b", [P, P], BF16)
        adj_i = sb("adj_i", [P, P], I32)
        adjt_i = sb("adjt_i", [P, P], I32)
        adj_f = sb("adj_f", [P, P])
        deg = sb("deg", [P, 1])
        valid = sb("valid", [P, 3])
        eps_t = sb("eps_t", [P, G])
        pow_t = sb("pow_t", [P, G])
        neg_t = sb("neg_t", [P, G])

        def view(t, name, *dims):
            a, b = OFF[name]
            v = t[:, a:b]
            if len(dims) == 2:
                return v.rearrange("p (a b) -> p a b", a=dims[0])
            if len(dims) == 3:
                return v.rearrange("p (a b c) -> p a b c", a=dims[0], b=dims[1])
            return v

        def both(name, *dims):
            return view(w_hi, name, *dims), view(w_lo, name, *dims)

        W0, Wq, Wk, Wv, Wo = both("W0", C, D + 2), both("Wq", C, D), both("Wk", C, D), both("Wv", C, D), both("Wo", C, D)
        WH, WOUT = both("Wh", H2, C, D), both("Wout", H2 * C, D + 2)
        W1, W2, W3, WA = both("w1", C, D), both("w2", C, D), both("W3", C, 2 * D), both("Wa", C, P)
        ADJT = view(w_hi, "adjT")
        row = {n: rowsb[:, k, :].unsqueeze(1).to_broadcast([P, G, D]) for k, n in enumerate(_ROWS)}
        BQ, BK, BV, B1 = range(4)

        xn = sb("xn", [P, G, D])
        xt = sb("xt", [P, C, G * P])
        m2, t2 = sb("m2", [P, G, H2, P]), sb("t2", [P, G, H2, P])
        he = sb("he", [P, 2, C * G * P])
        sm = sb("sm", [P, 2, R, P])
        f_small, b_small, c_small = sb("f_small", [P, 8, G]), sb("b_small", [P, 8, G, H2]), sb("c_small", [P, 8, G])

        with nc.sbuf_tensor("w_raw", [P, WTOT], F32) as w_raw:
            pass

        xr = sb("xr", [P, G, D])
        xT = sb("xT_hi", [P, C, G * P], F32R), sb("xT_lo", [P, C, G * P], F32R)
        wh = sb("wh_hi", [P, G, D], F32R), sb("wh_lo", [P, G, D], F32R)
        val = sb("val_hi", [P, G, D], F32R), sb("val_lo", [P, G, D], F32R)
        x1T_ = tuple(t[:].rearrange("p g d -> p (g d)").rearrange("p (c n) -> p c n", c=C) for t in wh)
        qq = xT
        kk = sb("k_hi", [P, C, G * P], F32R), sb("k_lo", [P, C, G * P], F32R)
        x2n = sb("x2n", [P, G, D])
        qs = sb("q_stack", [3 * DH, R, C, G * P], F32R)
        ks = sb("k_stack", [3 * DH, R, C, G * P], F32R)
        oT = sb("oT_hi", [P, C, G * P], F32R), sb("oT_lo", [P, C, G * P], F32R)
        oTf = sb("oT", [P, C, G * P])
        pT = sb("pT_hi", [P, 2, R * P], F32R), sb("pT_lo", [P, 2, R * P], F32R)
        m0, t0 = (xt[:, k].rearrange("p (g n) -> p g n", g=G) for k in range(C))
        p0 = tuple(t[:, 0].rearrange("p (g n) -> p g n", g=G) for t in kk)
        ec0 = sb("ec0", [P, G, 2])
        s1max, s1neg, s1sum, s1rec = (sb("s1" + n, [P, 2, R]) for n in ("max", "neg", "sum", "rec"))
        f_bn, f_mv, f_rs = sb("f_bn", [P, 2, G, 6]), sb("f_mv", [P, 2, G, 2]), sb("f_rs", [P, 2, G])
        f_ve, f_sh = sb("f_ve", [P, 2, G]), sb("f_sh", [P, 2, G])

        xb = sb("xb", [P, G, D])
        x2 = sb("x2_hi", [P, G, D], F32R), sb("x2_lo", [P, G, D], F32R)
        bT = sb("bT_hi", [P, C, G * P], F32R), sb("bT_lo", [P, C, G * P], F32R)
        eT = sb("eT", [2 * H2, G * P])
        ec2 = sb("ec2", [P, G, 2 * H2])
        p2 = sb("p2_hi", [P, G, H2 * P], F32R), sb("p2_lo", [P, G, H2 * P], F32R)
        hT = sb("hT_hi", [P, H2, C, G * P], F32R), sb("hT_lo", [P, H2, C, G * P], F32R)
        wh3 = sb("wh3_hi", [P, G, D], F32R), sb("wh3_lo", [P, G, D], F32R)
        cT = sb("cT_hi", [P, C, G * P], F32R), sb("cT_lo", [P, C, G * P], F32R)
        ec3 = sb("ec3", [P, G, 2])
        ob = sb("ob", [P, G, D])
        xo = sb("xo", [P, G, D])
        hid = sb("hid_hi", [P, C, G * P], F32R), sb("hid_lo", [P, C, G * P], F32R)
        x3d = sb("x3d", [P, G, D])
        m3, t3 = x3d[:, :, 0:P], x3d[:, :, P:D]
        hidf = x3d[:].rearrange("p g d -> p (g d)").rearrange("p (c n) -> p c n", c=C)
        p3 = tuple(t[:, 0].rearrange("p (g n) -> p g n", g=G) for t in hid)
        mj = tuple(t[:].rearrange("p c n -> p (c n)").rearrange("p (g d) -> p g d", g=G) for t in hid)
        b_bn, b_mv, b_rs = sb("b_bn", [P, 3, G, 6]), sb("b_mv", [P, 3, G, 2]), sb("b_rs", [P, 3, G])
        b_ve, b_sh = sb("b_ve", [P, 3, G]), sb("b_sh", [P, 3, G])

        names = """prep_dma prep prep_w prep_split prep_id x_in xt_in xt_hi xt_lo wh_ps wh_hi wh_lo ec0
            z0_ps g0_m g0_f g0_s g0_top g0_d g0_t g0_w g0_p g0_r p0_ps p0_hi p0_lo av0_ps
            y0 n0_st n0_mv n0_rs x1 x1T_ps x1T_hi x1T_lo xr q_ps q_hi q_lo k_ps k_hi k_lo v_ps v_hi v_lo
            q_stack k_stack s_ps s_end smax sneg s_p s_rec s_pn p1_ps p1_hi p1_lo o_ps o_f o_hi o_lo wo_ps
            y1 n1_st n1_mv n1_rs x2
            x2T_ps x2T_hi x2T_lo x2_hi x2_lo xb er_ps eT ec_ps ec2 z2_ps g2_m g2_f g2_s g2_top g2_d g2_t g2_w g2_p g2_r g2_pn
            p2_ps p2_hi p2_lo g_ps g_hi g_lo h_ps h_e h_e1 h_f h_hi h_lo wh3_ps wh3_hi wh3_lo ec3
            z3_ps g3_m g3_f g3_s g3_top g3_d g3_t g3_w g3_p g3_r p3_ps p3_hi p3_lo av3_ps o3_e o3_e1 o3
            oT_ps oT_hi oT_lo ob f1_ps hid_hi hid_f hid_lo f2_ps y2 n2_st n2_mv n2_rs n2 n2g y3
            n3_st n3_mv n3_rs x3 x3T_ps x3T_hi x3T_lo x3d mm_ps x3m mj_hi mj_lo am_ps
            y4 n4_st n4_mv n4_rs x4 out""".split()
        S = {n: sem("s_" + n) for n in names}

        def three(pe, dst, a, b, start, stop):
            nc.tensor.matmul(dst, a[0], b[1], start=start, stop=False)
            nc.tensor.matmul(dst, a[1], b[0], start=False, stop=False)
            return nc.tensor.matmul(dst, a[0], b[0], start=False, stop=stop)

        def part(pair, *idx):
            return pair[0][idx], pair[1][idx]

        def f(ap):
            return ap.bitcast(F32)

        ALL = slice(None)

        class Turn:

            def __init__(self, i, back=0, eng=None, kept=None):
                self.i, self.back, self.eng, self.kept = i, back, eng, kept
                self.first = eng is None and i == back

            def _at(self, unit, more):
                if self.eng is None:
                    return unit * (self.i - self.back) + more
                key = unit, more - unit * self.back
                if key not in self.kept:
                    if (unit, 0) not in self.kept:
                        self.kept[unit, 0] = self.eng.snap(self.i * unit) if unit > 1 else self.i
                    if key[1]:
                        self.kept[key] = self.eng.snap(self.kept[unit, 0] + key[1])
                return self.kept[key]

            def __call__(self, k, of):
                return self._at(of, k)

            @property
            def all(self):
                return self._at(1, 1)

            @property
            def before(self):
                return self._at(1, 0)

            @property
            def loaded(self):
                return self._at(16, 16)

            @property
            def stacked(self):
                return self._at(STACK, STACK)

            @property
            def stacked_before(self):
                return self._at(STACK, 0)

        def node(b):
            return slice(b * P, (b + 1) * P)

        def run(table, i, parts, eng=None):
            kept = {}
            for part_, stage in ORDER:
                if part_ in parts and stage in table:
                    table[stage](Turn(i, PARTS[part_], eng, kept))

        def rounds(eng, table):
            n = max(PARTS.values()) + 1
            for i in range(n):
                run(table, i, [p for p in PARTS if PARTS[p] <= i])
            with eng.Fori(n, NG) as i:
                run(table, i, PARTS, eng)
            for k in range(1, n):
                run(table, NG - 1 + k, [p for p in PARTS if PARTS[p] >= k])

        block = ctx.enter_context(nc.Block())

        @block.sync
        def _(sp):
            for src, dst in ((weights, w_raw), (rows, rowsb), (cols, colsb), (adj, adj_i), (adj_t, adjt_i)):
                sp.dma_start(dst[:], src).then_inc(S["prep_dma"], 16)
            sp.dma_start(m2[:].rearrange("p g h n -> p (g h n)"), att_rows[:, 0:G * H2 * P]).then_inc(S["prep_dma"], 16)
            sp.dma_start(t2[:].rearrange("p g h n -> p (g h n)"), att_rows[:, G * H2 * P:2 * G * H2 * P]).then_inc(S["prep_dma"], 16)
            sp.dma_start(he[:].rearrange("p g n -> p (g n)"), att_rows[:, 2 * G * H2 * P:]).then_inc(S["prep_dma"], 16)

            def load_xt(i):
                if type(i) is not int or i > 0:
                    sp.wait_ge(S["p0_ps"], i)
                sp.dma_start(xt[:].rearrange("p c n -> p (c n)"), x_t[i]).then_inc(S["xt_in"], 16)

            def load_x(i):
                if type(i) is not int or i > 0:
                    sp.wait_ge(S["xr"], i)
                    sp.wait_ge(S["x1T_ps"], i)
                sp.dma_start(xn[:], xn_v[i]).then_inc(S["x_in"], 16)

            def stack(i):
                for name, pair, dst, order in (("q", qq, qs, (0, 0, 1)), ("k", kk, ks, (0, 1, 0))):
                    sp.wait_ge(S[name + "_hi"], i + 1)
                    sp.wait_ge(S[name + "_lo"], i + 1)
                    if name == "q" and (type(i) is not int or i > 0):
                        sp.wait_ge(S["s_end"], i)
                    for j, which in enumerate(order):
                        for r in range(R):
                            sp.dma_start(f(dst[DH * j:DH * (j + 1), r]), f(pair[which][DH * r:DH * (r + 1)])) \
                              .then_inc(S[name + "_stack"], 16)

            def store(i):
                sp.wait_ge(S["x4"], i + 1)
                sp.dma_start(out_v[i], xo[:]).then_inc(S["out"], 16)

            sp.sem_inc(S["out"], 16)
            late = max(PARTS.values())
            for i in range(late):
                load_xt(i)
                load_x(i)
                stack(i)
            with sp.Fori(late, NG) as i:
                load_xt(i)
                load_x(i)
                store(i - late)
                stack(i)
            for i in range(NG - late, NG):
                store(i)
            sp.wait_ge(S["out"], 16 * (NG + 1))

        @block.gpsimd
        def _(pool):
            nc.gpsimd.memset(ident[:], 0.0).then_inc(S["prep_id"], 1)
            nc.gpsimd.memset(eps_t[:], EPS).then_inc(S["prep_id"], 1)
            nc.gpsimd.memset(pow_t[:], -0.5).then_inc(S["prep_id"], 1)
            nc.gpsimd.memset(neg_t[:], -1.0).then_inc(S["prep_id"], 1)
            pool.wait_ge(S["prep_id"], 4)
            nc.gpsimd.affine_select(out=ident[:], in_=ident[:], compare_op=ALU.not_equal, fill=1.0, base=0,
                                    pattern=[[-1, P]], channel_multiplier=1).then_inc(S["prep_id"], 1)
            pool.wait_ge(S["prep_split"], len(SPLIT))
            for a, b in SPLIT:
                nc.gpsimd.tensor_tensor(w_lo[:, a:b], w_raw[:, a:b], f(w_hi[:, a:b]), ALU.subtract).then_inc(S["prep_split"], 1)
            pool.wait_ge(S["prep"], 1)

            def rsqrt(g, n, mv, ve, rs, sh):
                pool.wait_ge(S[n + "_mv"], g.all)
                nc.gpsimd.tensor_tensor(sh, mv[:, :, 0], neg_t[:], ALU.mult)
                nc.gpsimd.tensor_tensor(ve, mv[:, :, 1], eps_t[:], ALU.add).then_inc(S[n + "_rs"], 1)
                pool.wait_ge(S[n + "_rs"], g(1, 3))
                nc.gpsimd.tensor_tensor(rs, ve, pow_t[:], ALU.pow).then_inc(S[n + "_rs"], 1)
                pool.wait_ge(S[n + "_rs"], g(2, 3))
                nc.gpsimd.tensor_tensor(sh, sh, rs, ALU.mult).then_inc(S[n + "_rs"], 1)

            def x0(g):
                pool.wait_ge(S["xt_hi"], g.all)
                nc.gpsimd.tensor_tensor(xT[1][:], xt[:], f(xT[0][:]), ALU.subtract).then_inc(S["xt_lo"], 1)

            def n0(g):
                rsqrt(g, "n0", f_mv[:, 0], f_ve[:, 0], f_rs[:, 0], f_sh[:, 0])

            def x1_plus(g):
                pool.wait_ge(S["x1"], g.all)
                if not g.first:
                    pool.wait_ge(S["y1"], g.before)
                nc.gpsimd.tensor_tensor(xr[:], xn[:], row["bo"], ALU.add).then_inc(S["xr"], 1)

            def norm_probs(u):
                def fn(g):
                    pool.wait_ge(S["s_p"], g(u + 1, 4))
                    pool.wait_ge(S["s_rec"], g(u + 1, 4))
                    nc.gpsimd.tensor_tensor(sm[:, u % 2], sm[:, u % 2], s1rec[:, u % 2].unsqueeze(2).to_broadcast([P, R, P]),
                                            ALU.mult).then_inc(S["s_pn"], 1)
                return fn

            def heads_low(t):
                def fn(g):
                    pool.wait_ge(S["o_hi"], g(t + 1, C))
                    nc.gpsimd.tensor_tensor(oT[1][:, t], oTf[:, t], f(oT[0][:, t]), ALU.subtract).then_inc(S["o_lo"], 1)
                return fn

            def n1(g):
                rsqrt(g, "n1", f_mv[:, 1], f_ve[:, 1], f_rs[:, 1], f_sh[:, 1])

            def x2_plus(g):
                pool.wait_ge(S["x2_lo"], g.all)
                if not g.first:
                    pool.wait_ge(S["y3"], g.before)
                nc.gpsimd.tensor_tensor(xb[:], f(x2[0][:]), f(x2[1][:]), ALU.add).then_inc(S["xb"], 1)
                pool.wait_ge(S["xb"], g(1, 2))
                nc.gpsimd.tensor_tensor(xb[:], xb[:], row["beta"], ALU.add).then_inc(S["xb"], 1)

            def x2_low(g):
                pool.wait_ge(S["x2_hi"], g.all)
                nc.gpsimd.tensor_tensor(x2[1][:], x2n[:], f(x2[0][:]), ALU.subtract).then_inc(S["x2_lo"], 1)

            def g2c(b):
                def fn(g):
                    pool.wait_ge(S["g2_p"], g(b + 1, G))
                    pool.wait_ge(S["g2_r"], g(b + 1, G))
                    nc.gpsimd.tensor_tensor(t2[:, b], t2[:, b], b_small[:, 7, b].unsqueeze(2).to_broadcast([P, H2, P]),
                                            ALU.mult).then_inc(S["g2_pn"], 1)
                return fn

            def h_low(h):
                def fn(g):
                    pool.wait_ge(S["h_hi"], g(h + 1, H2))
                    nc.gpsimd.tensor_tensor(hT[1][:, h], he[:, h % 2].rearrange("p (c n) -> p c n", c=C), f(hT[0][:, h]),
                                            ALU.subtract).then_inc(S["h_lo"], 1)
                return fn

            def oT_(g):
                pool.wait_ge(S["oT_ps"], g.all)
                nc.gpsimd.tensor_tensor(ob[:], ob[:], row["b2"], ALU.add).then_inc(S["ob"], 1)

            def f1h(g):
                pool.wait_ge(S["hid_hi"], g.all)
                nc.gpsimd.tensor_tensor(hid[1][:], hidf, f(hid[0][:]), ALU.subtract).then_inc(S["hid_lo"], 1)

            def n2(g):
                rsqrt(g, "n2", b_mv[:, 0], b_ve[:, 0], b_rs[:, 0], b_sh[:, 0])

            def n2c(g):
                pool.wait_ge(S["n2"], g.all)
                nc.gpsimd.tensor_tensor(ob[:], ob[:], row["gamma"], ALU.mult).then_inc(S["n2g"], 1)
                pool.wait_ge(S["n2g"], g.all)
                nc.gpsimd.tensor_tensor(ob[:], ob[:], xb[:], ALU.add).then_inc(S["y3"], 1)

            def n3(g):
                rsqrt(g, "n3", b_mv[:, 1], b_ve[:, 1], b_rs[:, 1], b_sh[:, 1])

            def x3T(g):
                pool.wait_ge(S["x3"], g.all)
                nc.gpsimd.tensor_tensor(x3d[:], ob[:], row["b3"], ALU.add).then_inc(S["x3d"], 1)

            def n4(g):
                rsqrt(g, "n4", b_mv[:, 2], b_ve[:, 2], b_rs[:, 2], b_sh[:, 2])

            rounds(pool, {
                "x0": x0, "n0": n0, "xr": x1_plus, "xb": x2_plus, "eA": norm_probs(0), "eB": norm_probs(1), "eC": norm_probs(2),
                "eD": norm_probs(3), "oAh": heads_low(0), "oBh": heads_low(1), "n1": n1, "x2": x2_low, "g2c0": g2c(0), "g2c1": g2c(1), "hh0": h_low(0), "hh1": h_low(1),
                "hh2": h_low(2), "hh3": h_low(3), "oT": oT_, "f1h": f1h, "n2": n2, "n2c": n2c, "n3": n3, "x3T": x3T, "n4": n4})

        @block.scalar
        def _(act):
            act.wait_ge(S["prep_dma"], 16 * 8)
            for a, b in SPLIT:
                nc.scalar.activation(w_hi[:, a:b], w_raw[:, a:b], ACT.Identity).then_inc(S["prep_split"], 1)
            act.wait_ge(S["prep"], 1)

            def high(name, count, dst, src, ready, func=ACT.Identity, **kw):
                act.wait_ge(S[ready], count)
                ins = nc.scalar.activation(dst, src, func, **kw)
                if name:
                    ins.then_inc(S[name], 1)

            def whh(g, n, pair, bank0, graphs=range(G)):
                for b in graphs:
                    high(n + "_hi", g(b + 1, G), pair[0][:, b], ps[:, bank0 + b, 0:D], n + "_ps")

            def scaled(g, n, small, m, t, slope, T, b=0, of=1):
                act.wait_ge(S[n + "_d"], g(b + 1, of))
                for k in range(T):
                    ins = nc.scalar.activation(t[:, k], m[:, k], ACT.Identity, bias=small(5)[:, k:k + 1], scale=slope)
                    if k % (T // 2) == T // 2 - 1:
                        ins.then_inc(S[n + "_t"], 1)

            def exps(g, n, small, m, t, T, b=0, of=1):
                for k in range(T):
                    if k % (T // 2) == 0:
                        act.wait_ge(S[n + "_w"], g(2 * b + k // (T // 2) + 1, 2 * of))
                    last = nc.scalar.activation(t[:, k], m[:, k], ACT.Exp, accum_out=small(6)[:, k:k + 1])
                last.then_inc(S[n + "_p"], 1)

            s0 = lambda j: f_small[:, j]
            s3 = lambda j: c_small[:, j]

            def x0(g):
                act.wait_ge(S["xt_in"], g.loaded)
                if not g.first:
                    act.wait_ge(S["q_stack"], g.stacked_before)
                nc.scalar.activation(xT[0][:], xt[:], ACT.Identity).then_inc(S["xt_hi"], 1)

            def wh_(b):
                def fn(g):
                    whh(g, "wh", wh, 0, [b])
                return fn

            def g0b(g):
                scaled(g, "g0", s0, m0, t0, SLOPE0, G)

            def g0c(g):
                exps(g, "g0", s0, m0, t0, G)

            def pt0(g):
                if not g.first:
                    act.wait_ge(S["k_stack"], g.stacked_before)
                high("p0_hi", g.all, p0[0], ps[:, 1, 0:G * P].rearrange("p (g n) -> p g n", g=G), "p0_ps")

            def x1T(g):
                high("x1T_hi", g.all, x1T_[0], ps[:, 1, :].rearrange("p (c n) -> p c n", c=C), "x1T_ps")

            def proj(n, pair, bank, bias):
                def fn(g):
                    for t in range(C):
                        high(n + "_hi" if t == C - 1 else None, g.all, pair[0][:, t], ps[:, bank, t * G * P:(t + 1) * G * P], n + "_ps",
                             bias=colsb[:, bias, t:t + 1])
                return fn

            def v(g):
                high("v_hi", g.all, val[0][:].rearrange("p g d -> p (g d)"), ps[:, 0, :], "v_ps")

            def probs(u):
                def fn(g):
                    act.wait_ge(S["sneg"], g(u + 1, 4))
                    for r in range(R):
                        last = nc.scalar.activation(sm[:, u % 2, r], ps[:, 2 + u % 2, r * P:(r + 1) * P], ACT.Exp, bias=s1neg[:, u % 2, r:r + 1],
                                             scale=SCALE, accum_out=s1sum[:, u % 2, r:r + 1])
                    last.then_inc(S["s_p"], 1)
                return fn

            def probsT(u):
                def fn(g):
                    high("p1_hi", g(u + 1, 4), pT[0][:, u % 2], ps[:, 2 + u % 2, :], "p1_ps")
                return fn

            def heads_out(t):
                def fn(g):
                    act.wait_ge(S["o_ps"], g(t + 1, C))
                    for r in range(R):
                        q = slice(DH * r, DH * (r + 1))
                        last = nc.scalar.activation(oTf[q, t].rearrange("p (g n) -> p g n", g=G), ps[q, 2:2 + G, r * P:(r + 1) * P],
                                                    ACT.Identity, bias=colsb[q, BV, t:t + 1])
                    last.then_inc(S["o_f"], 1)
                return fn

            def heads_high(t):
                def fn(g):
                    act.wait_ge(S["o_f"], g(t + 1, C))
                    nc.scalar.activation(oT[0][:, t], oTf[:, t], ACT.Identity).then_inc(S["o_hi"], 1)
                return fn

            def normed(n, name, dst, rs, shift):
                def fn(g):
                    act.wait_ge(S[n + "_rs"], g(3, 3))
                    for b in range(G):
                        last = nc.scalar.activation(dst[:, b], dst[:, b], ACT.Identity, bias=shift[:, b:b + 1], scale=rs[:, b:b + 1])
                    last.then_inc(S[name], 1)
                return fn

            def x2_high(g):
                if not g.first:
                    act.wait_ge(S["g_ps"], g(0, G * C))
                    act.wait_ge(S["xb"], g(0, 2))
                act.wait_ge(S["x2"], g.all)
                nc.scalar.activation(x2[0][:], x2n[:], ACT.Identity).then_inc(S["x2_hi"], 1)

            def x2T(g):
                high("x2T_hi", g.all, bT[0][:].rearrange("p c n -> p (c n)"), ps[:, 2, :], "x2T_ps")

            def g2b(b):
                def fn(g):
                    scaled(g, "g2", lambda j: b_small[:, j, b], m2[:, b], t2[:, b], SLOPE2, H2, b, of=G)
                return fn

            def g2c(b):
                def fn(g):
                    exps(g, "g2", lambda j: b_small[:, j, b], m2[:, b], t2[:, b], H2, b, of=G)
                return fn

            def g2d(b):
                def fn(g):
                    high("p2_hi", g(b + 1, G), p2[0][:, b], ps[:, 4 + b, :], "p2_ps")
                return fn

            def gx(b):
                def fn(g):
                    for c in range(C):
                        high("g_hi", g(C * b + c + 1, G * C), hT[0][:, :, c, node(b)],
                             ps[:, 4 + c, :].rearrange("p (h n) -> p h n", h=H2), "g_ps")
                return fn

            def hT_(h):
                def fn(g):
                    if h >= 2:
                        act.wait_ge(S["h_lo"], g(h - 1, H2))
                    high("h_e", g(h + 1, H2), he[:, h % 2], ps[:, 4 + h % 2, :], "h_ps", ACT.Exp)
                return fn

            def h_high(h):
                def fn(g):
                    act.wait_ge(S["h_f"], g(h + 1, H2))
                    nc.scalar.activation(hT[0][:, h].rearrange("p c n -> p (c n)"), he[:, h % 2], ACT.Identity) \
                      .then_inc(S["h_hi"], 1)
                return fn

            def wh3_(b):
                def fn(g):
                    whh(g, "wh3", wh3, 4, [b])
                return fn

            def g3b(g):
                scaled(g, "g3", s3, m3, t3, SLOPE2, G)

            def g3c(g):
                exps(g, "g3", s3, m3, t3, G)

            def pt3(g):
                high("p3_hi", g.all, p3[0], ps[:, 7, 0:G * P].rearrange("p (g n) -> p g n", g=G), "p3_ps")

            def av3(g):
                act.wait_ge(S["g3_r"], g.all)
                for b in range(G):
                    high("o3_e" if b == G - 1 else None, g.all, ob[:, b], ps[:, 6, b * D:(b + 1) * D], "av3_ps", ACT.Exp,
                         scale=c_small[:, 7, b:b + 1])

            def oT_(g):
                high("oT_hi", g.all, cT[0][:].rearrange("p c n -> p (c n)"), ps[:, 7, :], "oT_ps")

            def f1(g):
                for t in range(C):
                    high("hid_f" if t == C - 1 else None, g.all, hidf[:, t], ps[:, 6, t * G * P:(t + 1) * G * P], "f1_ps", ACT.Relu,
                         bias=colsb[:, B1, t:t + 1])

            def f1h(g):
                act.wait_ge(S["hid_f"], g.all)
                nc.scalar.activation(hid[0][:], hidf, ACT.Identity).then_inc(S["hid_hi"], 1)

            def x3T(g):
                high("x3T_hi", g.all, cT[0][:].rearrange("p c n -> p (c n)"), ps[:, 6, :], "x3T_ps")

            def mm(b):
                def fn(g):
                    high("mj_hi", g(b + 1, G), mj[0][:, b], ps[:, 6 + b, D:2 * D], "mm_ps")
                return fn

            rounds(act, {
                "x0": x0, "wh0": wh_(0), "wh1": wh_(1), "g0b": g0b, "g0c": g0c, "pt0": pt0, "x1T": x1T, "q": proj("q", qq, 0, BQ), "k": proj("k", kk, 1, BK), "v": v,
                "eA": probs(0), "eB": probs(1), "eC": probs(2), "eD": probs(3),
                "pA": probsT(0), "pB": probsT(1), "pC": probsT(2), "pD": probsT(3),
                "oA": heads_out(0), "oB": heads_out(1), "oAh": heads_high(0), "oBh": heads_high(1),
                "n0b": normed("n0", "x1", xn, f_rs[:, 0], f_sh[:, 0]), "n1b": normed("n1", "x2", x2n, f_rs[:, 1], f_sh[:, 1]),
                "n2b": normed("n2", "n2", ob, b_rs[:, 0], b_sh[:, 0]), "n3b": normed("n3", "x3", ob, b_rs[:, 1], b_sh[:, 1]),
                "n4b": normed("n4", "x4", xo, b_rs[:, 2], b_sh[:, 2]),
                "x2T": x2T, "x2": x2_high, "g2b0": g2b(0), "g2b1": g2b(1), "g2c0": g2c(0), "g2c1": g2c(1), "g2d0": g2d(0), "g2d1": g2d(1), "gx0": gx(0), "gx1": gx(1), "hT0": hT_(0), "hT1": hT_(1),
                "hT2": hT_(2), "hT3": hT_(3), "hh0": h_high(0), "hh1": h_high(1), "hh2": h_high(2), "hh3": h_high(3),
                "wh3_0": wh3_(0), "wh3_1": wh3_(1), "g3b": g3b, "g3c": g3c, "pt3": pt3, "av3": av3,
                "oT": oT_, "f1": f1, "f1h": f1h, "x3T": x3T, "mm0": mm(0), "mm1": mm(1)})

        @block.vector
        def _(dve):
            V = nc.vector
            dve.wait_ge(S["prep_dma"], 16 * 8)
            chain = [0]

            def link(ins):
                chain[0] += 1
                ins.then_inc(S["prep_w"], 1)
                dve.wait_ge(S["prep_w"], chain[0])

            rows0 = m2[:].rearrange("p g h n -> p (g h n)"), t2[:].rearrange("p g h n -> p (g h n)"), he[:].rearrange("p g n -> p (g n)")

            def att(k):
                per = G * H2 * P // D
                return rows0[k // per][:, (k % per) * D:(k % per + 1) * D]

            scr = sm[:, 0].rearrange("p r n -> p (r n)")[:, 0:D]
            raw0, rawo = view(w_raw, "W0", C, D + 2), view(w_raw, "Wout", H2 * C, D + 2)
            rawh, rawa = view(w_raw, "Wh", H2, C, D), view(w_raw, "Wa", C, P)

            def product(weight, k, dst):
                link(V.tensor_tensor_reduce(out=scr, in0=weight, in1=att(k), scale=1.0, scalar=0.0, op0=ALU.mult,
                                            op1=ALU.add, accum_out=dst))

            for s in range(2):
                for c in range(C):
                    product(raw0[:, c, 0:D], s, raw0[:, c, D + s:D + s + 1])
                for c in range(H2 * C):
                    product(rawo[:, c, 0:D], 2 + s, rawo[:, c, D + s:D + s + 1])
                for h in range(H2):
                    for c in range(C):
                        product(rawh[:, h, c], 4 + 2 * h + s, rawa[:, c, s * H2 + h:s * H2 + h + 1])
            link(V.tensor_copy(view(w_raw, "adjT"), adjt_i[:]))
            link(V.tensor_copy(adj_f[:], adj_i[:]))
            link(V.tensor_scalar(mask[:], adj_f[:], 0.0, MASK, ALU.is_equal, ALU.mult))
            link(V.tensor_scalar(mask2[:], adj_f[:], 0.0, MASK, ALU.is_le, ALU.mult))
            link(V.reduce_sum(deg[:], adj_f[:], axis=AX))
            link(V.tensor_reduce(valid[:, 0:1], mask[:], AX, ALU.max))
            link(V.tensor_scalar(valid[:, 1:2], valid[:, 0:1], 0.0, None, ALU.is_equal))
            link(V.reciprocal(valid[:, 0:1], valid[:, 1:2]))
            link(V.tensor_tensor(valid[:, 2:3], valid[:, 0:1], valid[:, 1:2], ALU.mult))
            link(V.tensor_scalar(valid[:, 2:3], valid[:, 2:3], -1.0, None, ALU.add))
            link(V.tensor_scalar(rowsb[:, 4], rowsb[:, 4], deg[:], None, ALU.mult))
            for a, b in (OFF["W0"], OFF["Wout"], (OFF["Wa"][0], WTOT)):
                link(V.tensor_copy(w_hi[:, a:b], w_raw[:, a:b]))
                link(V.tensor_tensor(w_lo[:, a:b], w_raw[:, a:b], f(w_hi[:, a:b]), ALU.subtract))
            dve.wait_ge(S["prep_id"], 5)
            dve.wait_ge(S["prep_split"], 2 * len(SPLIT))
            link(V.tensor_copy(ident_b[:], ident[:]))
            V.tensor_copy(mask_r[:], mask[:].unsqueeze(1).to_broadcast([P, R, P])).then_inc(S["prep"], 1)

            def low(name, count, dst, src, high_, ready):
                dve.wait_ge(S[ready], count)
                V.tensor_tensor(dst, src, f(high_), ALU.subtract).then_inc(S[name], 1)

            def edge_columns(g, n, ec, pair, bank0, e_name, graphs=range(G)):
                for b in graphs:
                    dve.wait_ge(S[n + "_hi"], g(b + 1, G))
                    V.tensor_copy(ec[:, b], ps[:, bank0 + b, D:D + 2]).then_inc(S[e_name], 1)
                for b in graphs:
                    low(n + "_lo", g(b + 1, G), pair[1][:, b], ps[:, bank0 + b, 0:D], pair[0][:, b], n + "_hi")

            def front_of_softmax(g, n, small, z, msk, m, es, slope, T, b=0, of=1):
                here = g(b + 1, of)
                V.tensor_tensor(m, z, msk[:].unsqueeze(1).to_broadcast([P, T, P]), ALU.add).then_inc(S[n + "_m"], 1)
                dve.wait_ge(S[n + "_m"], here)
                V.tensor_reduce(small(1), m, AX, ALU.max).then_inc(S[n + "_f"], 1)
                dve.wait_ge(S[n + "_f"], here)
                V.tensor_tensor(small(2), es, small(1), ALU.add).then_inc(S[n + "_s"], 1)
                dve.wait_ge(S[n + "_s"], here)
                V.scalar_tensor_tensor(small(3), small(2), slope, small(2), ALU.mult, ALU.max).then_inc(S[n + "_top"], 1)
                dve.wait_ge(S[n + "_top"], here)
                V.tensor_tensor(small(4), es, small(3), ALU.subtract)
                V.scalar_tensor_tensor(small(5), es, slope, small(3), ALU.mult, ALU.subtract).then_inc(S[n + "_d"], 1)

            def larger(g, n, small, m, t, T, b=0, of=1):
                dve.wait_ge(S[n + "_d"], g(b + 1, of))
                for j in range(T):
                    if j % (T // 2) == 0:
                        dve.wait_ge(S[n + "_t"], g(2 * b + j // (T // 2) + 1, 2 * of))
                    ins = V.scalar_tensor_tensor(m[:, j], m[:, j], small(4)[:, j:j + 1], t[:, j], ALU.add, ALU.max)
                    if j % (T // 2) == T // 2 - 1:
                        ins.then_inc(S[n + "_w"], 1)

            def stats(g, n, src, bn, mv):
                for b in range(G):
                    last = V.bn_stats(bn[:, b], src[:, b])
                last.then_inc(S[n + "_st"], 1)
                dve.wait_ge(S[n + "_st"], g.all)
                V.memset(tick[:], 0.0)
                for b in range(G):
                    last = V.bn_aggr(mv[:, b], bn[:, b])
                last.then_inc(S[n + "_mv"], 1)

            s0 = lambda j: f_small[:, j]
            s3 = lambda j: c_small[:, j]

            def wh_(b):
                def fn(g):
                    edge_columns(g, "wh", ec0, wh, 0, "ec0", [b])
                return fn

            def g0a(g):
                dve.wait_ge(S["z0_ps"], g.all)
                dve.wait_ge(S["ec0"], g(G, G))
                front_of_softmax(g, "g0", s0, ps[:, 0, 0:G * P].rearrange("p (g n) -> p g n", g=G), mask, m0,
                                 ec0[:, :, 0], SLOPE0, G)

            def g0b(g):
                larger(g, "g0", s0, m0, t0, G)

            def g0c(g):
                dve.wait_ge(S["g0_p"], g.all)
                V.reciprocal(s0(7), s0(6)).then_inc(S["g0_r"], 1)
                dve.wait_ge(S["g0_r"], g(1, 2))
                V.tensor_scalar(s0(7), s0(7), valid[:, 1:2], None, ALU.mult).then_inc(S["g0_r"], 1)

            def pt0(g):
                low("p0_lo", g.all, p0[1], ps[:, 1, 0:G * P].rearrange("p (g n) -> p g n", g=G), p0[0], "p0_hi")

            def av0(g):
                dve.wait_ge(S["x_in"], g.loaded)
                dve.wait_ge(S["g0_r"], g(2, 2))
                dve.wait_ge(S["av0_ps"], g.all)
                for b in range(G):
                    last = V.scalar_tensor_tensor(xn[:, b], ps[:, 0, b * D:(b + 1) * D], s0(7)[:, b:b + 1], xn[:, b], ALU.mult, ALU.add)
                last.then_inc(S["y0"], 1)

            def n0(g):
                dve.wait_ge(S["y0"], g.all)
                stats(g, "n0", xn, f_bn[:, 0], f_mv[:, 0])

            def x1T(g):
                low("x1T_lo", g.all, x1T_[1], ps[:, 1, :].rearrange("p (c n) -> p c n", c=C), x1T_[0], "x1T_hi")

            def proj(n, pair, bank, bias):
                def fn(g):
                    dve.wait_ge(S[n + "_hi"], g.all)
                    for t in range(C):
                        last = V.scalar_tensor_tensor(pair[1][:, t], ps[:, bank, t * G * P:(t + 1) * G * P],
                                                      colsb[:, bias, t:t + 1], f(pair[0][:, t]), ALU.add, ALU.subtract)
                    last.then_inc(S[n + "_lo"], 1)
                return fn

            def v(g):
                low("v_lo", g.all, val[1][:].rearrange("p g d -> p (g d)"), ps[:, 0, :],
                    val[0][:].rearrange("p g d -> p (g d)"), "v_hi")

            def scores(u):
                def fn(g):
                    w = u % 2
                    dve.wait_ge(S["s_ps" if u < 3 else "s_end"], g(u + 1, 3) if u < 3 else g.all)
                    V.tensor_reduce(s1max[:, w], ps[:, 2 + w, :].rearrange("p (r n) -> p r n", r=R), AX, ALU.max) \
                     .then_inc(S["smax"], 1)
                    dve.wait_ge(S["smax"], g(u + 1, 4))
                    V.tensor_scalar(s1neg[:, w], s1max[:, w], -SCALE, valid[:, 2:3], ALU.mult, ALU.add).then_inc(S["sneg"], 1)
                return fn

            def sums(u):
                def fn(g):
                    dve.wait_ge(S["s_p"], g(u + 1, 4))
                    V.reciprocal(s1rec[:, u % 2], s1sum[:, u % 2]).then_inc(S["s_rec"], 1)
                return fn

            def probsT(u):
                def fn(g):
                    w = u % 2
                    low("p1_lo", g(u + 1, 4), pT[1][:, w], ps[:, 2 + w, :], pT[0][:, w], "p1_hi")
                return fn

            def wo(g):
                dve.wait_ge(S["wo_ps"], g.all)
                dve.wait_ge(S["xr"], g.all)
                if not g.first:
                    dve.wait_ge(S["x2T_ps"], g.before)
                    dve.wait_ge(S["x2_lo"], g.before)
                V.tensor_tensor(x2n[:].rearrange("p g d -> p (g d)"), ps[:, 2, :], xr[:].rearrange("p g d -> p (g d)"), ALU.add) \
                 .then_inc(S["y1"], 1)

            def n1(g):
                dve.wait_ge(S["y1"], g.all)
                stats(g, "n1", x2n, f_bn[:, 1], f_mv[:, 1])

            def x2T(g):
                low("x2T_lo", g.all, bT[1][:].rearrange("p c n -> p (c n)"), ps[:, 2, :],
                    bT[0][:].rearrange("p c n -> p (c n)"), "x2T_hi")

            def er(g):
                dve.wait_ge(S["er_ps"], g.all)
                V.tensor_copy(eT[:], ps[0:2 * H2, 3, 0:G * P]).then_inc(S["eT"], 1)

            def ec(g):
                dve.wait_ge(S["ec_ps"], g.all)
                V.tensor_copy(ec2[:], ps[:, 2, 0:G * 2 * H2].rearrange("p (g e) -> p g e", g=G)).then_inc(S["ec2"], 1)

            def g2a(b):
                def fn(g):
                    dve.wait_ge(S["ec2"], g.all)
                    dve.wait_ge(S["z2_ps"], g(b + 1, G))
                    front_of_softmax(g, "g2", lambda j: b_small[:, j, b],
                                     ps[:, 4 + b, :].rearrange("p (h n) -> p h n", h=H2), mask2, m2[:, b],
                                     ec2[:, b, 0:H2], SLOPE2, H2, b, of=G)
                return fn

            def g2b(b):
                def fn(g):
                    larger(g, "g2", lambda j: b_small[:, j, b], m2[:, b], t2[:, b], H2, b, of=G)
                return fn

            def g2c(b):
                def fn(g):
                    dve.wait_ge(S["g2_p"], g(b + 1, G))
                    V.reciprocal(b_small[:, 7, b], b_small[:, 6, b]).then_inc(S["g2_r"], 1)
                return fn

            def g2d(b):
                def fn(g):
                    low("p2_lo", g(b + 1, G), p2[1][:, b], ps[:, 4 + b, :], p2[0][:, b], "p2_hi")
                return fn

            def gx(b):
                def fn(g):
                    for c in range(C):
                        low("g_lo", g(C * b + c + 1, G * C), hT[1][:, :, c, node(b)],
                            ps[:, 4 + c, :].rearrange("p (h n) -> p h n", h=H2), hT[0][:, :, c, node(b)], "g_hi")
                return fn

            def hT_(h):
                def fn(g):
                    k = g(h + 1, H2)
                    dve.wait_ge(S["h_e"], k)
                    V.tensor_scalar(he[:, h % 2], he[:, h % 2], 1.0, -1.0, ALU.min, ALU.add).then_inc(S["h_e1"], 1)
                    dve.wait_ge(S["h_e1"], k)
                    V.tensor_tensor(he[:, h % 2], ps[:, 4 + h % 2, :], he[:, h % 2], ALU.max) \
                     .then_inc(S["h_f"], 1)
                return fn

            def wh3_(b):
                def fn(g):
                    edge_columns(g, "wh3", ec3, wh3, 4, "ec3", [b])
                return fn

            def g3a(g):
                dve.wait_ge(S["z3_ps"], g.all)
                dve.wait_ge(S["ec3"], g(G, G))
                front_of_softmax(g, "g3", s3, ps[:, 6, 0:G * P].rearrange("p (g n) -> p g n", g=G), mask2, m3,
                                 ec3[:, :, 0], SLOPE2, G)

            def g3b(g):
                larger(g, "g3", s3, m3, t3, G)

            def g3c(g):
                dve.wait_ge(S["g3_p"], g.all)
                V.reciprocal(s3(7), s3(6)).then_inc(S["g3_r"], 1)

            def pt3(g):
                low("p3_lo", g.all, p3[1], ps[:, 7, 0:G * P].rearrange("p (g n) -> p g n", g=G), p3[0], "p3_hi")

            def av3(g):
                dve.wait_ge(S["g3_r"], g.all)
                dve.wait_ge(S["o3_e"], g.all)
                V.tensor_scalar(ob[:], ob[:], 1.0, -1.0, ALU.min, ALU.add).then_inc(S["o3_e1"], 1)
                dve.wait_ge(S["o3_e1"], g.all)
                for b in range(G):
                    last = V.scalar_tensor_tensor(ob[:, b], ps[:, 6, b * D:(b + 1) * D], s3(7)[:, b:b + 1], ob[:, b], ALU.mult, ALU.max)
                last.then_inc(S["o3"], 1)

            def oT_(g):
                low("oT_lo", g.all, cT[1][:].rearrange("p c n -> p (c n)"), ps[:, 7, :],
                    cT[0][:].rearrange("p c n -> p (c n)"), "oT_hi")

            def f2(g):
                dve.wait_ge(S["f2_ps"], g.all)
                dve.wait_ge(S["ob"], g.all)
                V.tensor_tensor(ob[:].rearrange("p g d -> p (g d)"), ps[:, 7, :], ob[:].rearrange("p g d -> p (g d)"), ALU.add) \
                 .then_inc(S["y2"], 1)

            def n2(g):
                dve.wait_ge(S["y2"], g.all)
                stats(g, "n2", ob, b_bn[:, 0], b_mv[:, 0])

            def n3(g):
                dve.wait_ge(S["y3"], g.all)
                stats(g, "n3", ob, b_bn[:, 1], b_mv[:, 1])

            def x3T(g):
                low("x3T_lo", g.all, cT[1][:].rearrange("p c n -> p (c n)"), ps[:, 6, :],
                    cT[0][:].rearrange("p c n -> p (c n)"), "x3T_hi")

            def mm(b):
                def fn(g):
                    dve.wait_ge(S["x3d"], g.all)
                    dve.wait_ge(S["mj_hi"], g(b + 1, G))
                    V.scalar_tensor_tensor(x3d[:, b], ps[:, 6 + b, 0:D], deg[:], x3d[:, b], ALU.mult, ALU.add) \
                     .then_inc(S["x3m"], 1)
                    low("mj_lo", g(b + 1, G), mj[1][:, b], ps[:, 6 + b, D:2 * D], mj[0][:, b], "mj_hi")
                return fn

            def am(g):
                dve.wait_ge(S["x3m"], g(G, G))
                dve.wait_ge(S["am_ps"], g.all)
                dve.wait_ge(S["out"], g.loaded)
                V.tensor_tensor(xo[:].rearrange("p g d -> p (g d)"), ps[:, 6, :], x3d[:].rearrange("p g d -> p (g d)"), ALU.add) \
                 .then_inc(S["y4"], 1)

            def n4(g):
                dve.wait_ge(S["y4"], g.all)
                stats(g, "n4", xo, b_bn[:, 2], b_mv[:, 2])

            rounds(dve, {
                "wh0": wh_(0), "wh1": wh_(1), "g0a": g0a, "g0b": g0b, "g0c": g0c, "pt0": pt0, "av0": av0, "n0": n0, "x1T": x1T,
                "q": proj("q", qq, 0, BQ), "k": proj("k", kk, 1, BK), "v": v, "sA": scores(0), "sB": scores(1), "sC": scores(2), "sD": scores(3),
                "eA": sums(0), "eB": sums(1), "eC": sums(2), "eD": sums(3), "pA": probsT(0), "pB": probsT(1), "pC": probsT(2), "pD": probsT(3), "wo": wo, "n1": n1,
                "x2T": x2T, "er": er, "ec": ec, "g2a0": g2a(0), "g2a1": g2a(1), "g2b0": g2b(0), "g2b1": g2b(1), "g2c0": g2c(0), "g2c1": g2c(1), "g2d0": g2d(0), "g2d1": g2d(1), "gx0": gx(0), "gx1": gx(1),
                "hT0": hT_(0), "hT1": hT_(1), "hT2": hT_(2), "hT3": hT_(3), "wh3_0": wh3_(0), "wh3_1": wh3_(1),
                "g3a": g3a, "g3b": g3b, "g3c": g3c, "pt3": pt3, "av3": av3, "oT": oT_, "f2": f2,
                "n2": n2, "n3": n3, "x3T": x3T, "mm0": mm(0), "mm1": mm(1), "am": am, "n4": n4})

        @block.tensor
        def _(pe):
            T_ = nc.tensor
            pe.wait_ge(S["prep"], 1)

            def transposes(src, bank):
                for b in range(G):
                    for c in range(C):
                        last = T_.transpose(ps[:, bank, (c * G + b) * P:(c * G + b + 1) * P], src[:, b, c * P:(c + 1) * P], ident[:])
                return last

            def natural(bank, off, width, xt_, b, w):
                for c in range(C):
                    last = three(pe, ps[:, bank, off:off + width], part(xt_, ALL, c, node(b)), part(w, ALL, c, slice(0, width)),
                                 c == 0, c == C - 1)
                return last

            def transposed(bank, t, w, xt_):
                for c in range(C):
                    last = three(pe, ps[:, bank, t * G * P:(t + 1) * G * P], part(w, ALL, c, slice(t * P, (t + 1) * P)),
                                 part(xt_, ALL, c), c == 0, c == C - 1)
                return last

            def spread(bank, off, col):
                return T_.transpose(ps[:, bank, off:off + P], col.to_broadcast([P, P]), ident[:])

            def wh_(b):
                def fn(g):
                    pe.wait_ge(S["xt_lo"], g.all)
                    if not g.first:
                        pe.wait_ge(S["v_lo" if b == 0 else "k_lo"], g.before)
                    natural(b, 0, D + 2, xT, b, W0).then_inc(S["wh_ps"], 1)
                return fn

            def g0a(g):
                pe.wait_ge(S["wh_lo"], g(G, G))
                for b in range(G):
                    last = spread(0, b * P, ec0[:, b, 1:2])
                last.then_inc(S["z0_ps"], 1)

            def pt0(g):
                pe.wait_ge(S["g0_p"], g.all)
                for b in range(G):
                    last = T_.transpose(ps[:, 1, b * P:(b + 1) * P], t0[:, b], ident[:])
                last.then_inc(S["p0_ps"], 1)

            def av0(g):
                pe.wait_ge(S["p0_lo"], g.all)
                pe.wait_ge(S["wh_lo"], g(G, G))
                for b in range(G):
                    last = three(pe, ps[:, 0, b * D:(b + 1) * D], part(p0, ALL, b), part(wh, ALL, b), True, True)
                last.then_inc(S["av0_ps"], 1)

            def x1T(g):
                pe.wait_ge(S["x1"], g.all)
                transposes(xn, 1).then_inc(S["x1T_ps"], 1)

            def proj(n, w, bank):
                def fn(g):
                    pe.wait_ge(S["x1T_lo"], g.all)
                    for t in range(C):
                        last = transposed(bank, t, w, x1T_)
                    last.then_inc(S[n + "_ps"], 1)
                return fn

            def v(g):
                pe.wait_ge(S["q_lo"], g.all)
                for b in range(G):
                    last = natural(0, b * D, D, x1T_, b, Wv)
                last.then_inc(S["v_ps"], 1)

            def scores(u):
                t, b = divmod(u, G)

                def fn(g):
                    if u == 0:
                        if not g.first:
                            pe.wait_ge(S["ec2"], g.before)
                        pe.wait_ge(S["q_stack"], g.stacked)
                        pe.wait_ge(S["k_stack"], g.stacked)
                    elif u >= 2:
                        pe.wait_ge(S["o_f"], g(1, C))
                    T_.matmul(ps[:, 2 + u % 2, :], ident_b[:], mask_r[:].rearrange("p r n -> p (r n)"), start=True, stop=False)
                    for r in range(R):
                        last = T_.matmul(ps[:, 2 + u % 2, r * P:(r + 1) * P], qs[:, r, t, node(b)], ks[:, r, t, node(b)],
                                         start=False, stop=r == R - 1)
                    last.then_inc(S["s_ps" if u < 3 else "s_end"], 1)
                return fn

            def probsT(u):
                t, b = divmod(u, G)

                def fn(g):
                    pe.wait_ge(S["s_pn"], g(u + 1, 4))
                    for r in range(R):
                        last = T_.transpose(ps[:, 2 + b, r * P:(r + 1) * P], sm[:, u % 2, r], ident[:])
                    last.then_inc(S["p1_ps"], 1)
                return fn

            def heads(t):
                def fn(g):
                    pe.wait_ge(S["v_lo"], g.all)
                    for b in range(G):
                        u = G * t + b
                        pe.wait_ge(S["p1_lo"], g(u + 1, 4))
                        last = three(pe, ps[:, 2 + b, :], part(val, ALL, b, slice(t * P, (t + 1) * P)), part(pT, ALL, u % 2), True, True)
                    last.then_inc(S["o_ps"], 1)
                return fn

            def wo(g):
                pe.wait_ge(S["o_lo"], g(C, C))
                for b in range(G):
                    last = natural(2, b * D, D, oT, b, Wo)
                last.then_inc(S["wo_ps"], 1)

            def x2T(g):
                pe.wait_ge(S["x2"], g.all)
                transposes(x2n, 2).then_inc(S["x2T_ps"], 1)

            def er(g):
                pe.wait_ge(S["x2T_lo"], g.all)
                for c in range(C):
                    last = three(pe, ps[:, 3, 0:G * P], part(WA, ALL, c), part(bT, ALL, c), c == 0, c == C - 1)
                last.then_inc(S["er_ps"], 1)

            def ec(g):
                pe.wait_ge(S["prep"], 1)
                pe.wait_ge(S["eT"], g.all)
                for b in range(G):
                    last = T_.transpose(ps[:, 2, b * 2 * H2:(b + 1) * 2 * H2], eT[:, node(b)], ident[0:2 * H2, 0:2 * H2])
                last.then_inc(S["ec_ps"], 1)

            def g2a(b):
                def fn(g):
                    pe.wait_ge(S["ec2"], g.all)
                    if not g.first:
                        pe.wait_ge(S["wh3_lo"], g(0, G))
                    for h in range(H2):
                        last = spread(4 + b, h * P, ec2[:, b, H2 + h:H2 + h + 1])
                    last.then_inc(S["z2_ps"], 1)
                return fn

            def g2d(b):
                def fn(g):
                    pe.wait_ge(S["g2_pn"], g(b + 1, G))
                    for h in range(H2):
                        last = T_.transpose(ps[:, 4 + b, h * P:(h + 1) * P], t2[:, b, h], ident[:])
                    last.then_inc(S["p2_ps"], 1)
                return fn

            def gx(b):
                def fn(g):
                    pe.wait_ge(S["x2_lo"], g.all)
                    pe.wait_ge(S["p2_lo"], g(G, G))
                    for c in range(C):
                        if b:
                            pe.wait_ge(S["g_lo"], g(c + 1, G * C))
                        three(pe, ps[:, 4 + c, :], part(x2, ALL, b, slice(c * P, (c + 1) * P)), part(p2, ALL, b), True, True) \
                            .then_inc(S["g_ps"], 1)
                return fn

            def hT_(h):
                def fn(g):
                    if h == 0:
                        pe.wait_ge(S["g_lo"], g(G * C, G * C))
                    if h >= 2:
                        pe.wait_ge(S["h_f"], g(h - 1, H2))
                    for t in range(C):
                        for c in range(C):
                            last = three(pe, ps[:, 4 + h % 2, t * G * P:(t + 1) * G * P], part(WH, ALL, h, c, slice(t * P, (t + 1) * P)),
                                         part(hT, ALL, h, c), c == 0, c == C - 1)
                    last.then_inc(S["h_ps"], 1)
                return fn

            def wh3_(b):
                def fn(g):
                    pe.wait_ge(S["h_lo"], g(H2, H2))
                    for k in range(H2 * C):
                        last = three(pe, ps[:, 4 + b, 0:D + 2], part(hT, ALL, k // C, k % C, node(b)), part(WOUT, ALL, k), k == 0,
                                     k == H2 * C - 1)
                    last.then_inc(S["wh3_ps"], 1)
                return fn

            def g3a(g):
                pe.wait_ge(S["ec3"], g(G, G))
                if not g.first:
                    pe.wait_ge(S["y4"], g.before)
                for b in range(G):
                    last = spread(6, b * P, ec3[:, b, 1:2])
                last.then_inc(S["z3_ps"], 1)

            def pt3(g):
                pe.wait_ge(S["g3_p"], g.all)
                for b in range(G):
                    last = T_.transpose(ps[:, 7, b * P:(b + 1) * P], t3[:, b], ident[:])
                last.then_inc(S["p3_ps"], 1)

            def av3(g):
                pe.wait_ge(S["p3_lo"], g.all)
                pe.wait_ge(S["wh3_lo"], g(G, G))
                for b in range(G):
                    last = three(pe, ps[:, 6, b * D:(b + 1) * D], part(p3, ALL, b), part(wh3, ALL, b), True, True)
                last.then_inc(S["av3_ps"], 1)

            def oT_(g):
                pe.wait_ge(S["o3"], g.all)
                transposes(ob, 7).then_inc(S["oT_ps"], 1)

            def f1(g):
                pe.wait_ge(S["oT_lo"], g.all)
                for t in range(C):
                    last = transposed(6, t, W1, cT)
                last.then_inc(S["f1_ps"], 1)

            def f2(g):
                pe.wait_ge(S["hid_lo"], g.all)
                for b in range(G):
                    last = natural(7, b * D, D, hid, b, W2)
                last.then_inc(S["f2_ps"], 1)

            def x3T(g):
                pe.wait_ge(S["x3"], g.all)
                transposes(ob, 6).then_inc(S["x3T_ps"], 1)

            def mm(b):
                def fn(g):
                    pe.wait_ge(S["x3T_lo"], g.all)
                    natural(6 + b, 0, 2 * D, cT, b, W3).then_inc(S["mm_ps"], 1)
                return fn

            def am(g):
                pe.wait_ge(S["mj_lo"], g(G, G))
                for b in range(G):
                    T_.matmul(ps[:, 6, b * D:(b + 1) * D], ADJT, mj[1][:, b], start=True, stop=False)
                    last = T_.matmul(ps[:, 6, b * D:(b + 1) * D], ADJT, mj[0][:, b], start=False, stop=True)
                last.then_inc(S["am_ps"], 1)

            rounds(pe, {
                "wh0": wh_(0), "wh1": wh_(1), "g0a": g0a, "pt0": pt0, "av0": av0, "x1T": x1T, "q": proj("q", Wq, 0), "k": proj("k", Wk, 1), "v": v,
                "sA": scores(0), "sB": scores(1), "sC": scores(2), "sD": scores(3),
                "pA": probsT(0), "pB": probsT(1), "pC": probsT(2), "pD": probsT(3), "oA": heads(0), "oB": heads(1), "wo": wo,
                "x2T": x2T, "er": er, "ec": ec, "g2a0": g2a(0), "g2a1": g2a(1), "g2d0": g2d(0), "g2d1": g2d(1), "gx0": gx(0), "gx1": gx(1), "hT0": hT_(0), "hT1": hT_(1), "hT2": hT_(2),
                "hT3": hT_(3), "wh3_0": wh3_(0), "wh3_1": wh3_(1), "g3a": g3a, "pt3": pt3, "av3": av3, "oT": oT_, "f1": f1, "f2": f2,
                "x3T": x3T, "mm0": mm(0), "mm1": mm(1), "am": am})


def kernel(**inputs):
    import concourse.bacc as bacc
    from concourse.bass_utils import run_bass_kernel_spmd

    a = {k: np.asarray(v) for k, v in inputs.items()}
    x = a["x"]
    B = x.shape[0]
    NG = B // G

    def chunks(w):
        return w.reshape(-1, P, w.shape[1]).transpose(1, 0, 2)

    def padded(w):
        v = np.zeros((P, w.shape[0] // P, D + 2), np.float32)
        v[:, :, 0:D] = chunks(w)
        return v

    heads = a["L2_gnn_W_heads"]
    w3 = np.concatenate([a["L3_gnn_W"][:, :D].T, a["L3_gnn_W"][:, D:].T], axis=1)
    parts = {"W0": padded(a["L0_gnn_W"]), "Wq": chunks(a["L1_gnn_Wq"].T), "Wk": chunks(a["L1_gnn_Wk"].T),
             "Wv": chunks(a["L1_gnn_Wv"].T), "Wo": chunks(a["L1_gnn_Wo"].T),
             "Wh": chunks(heads.reshape(H2 * D, D)), "Wout": padded(a["L2_gnn_W_out"]), "w1": chunks(a["L2_gnn_w1"]),
             "w2": chunks(a["L2_gnn_w2"]), "W3": chunks(w3), "Wa": np.zeros((P, C * P), np.float32),
             "adjT": np.zeros((P, P), np.float32)}
    weights = np.concatenate([parts[n].reshape(P, -1) for n, _ in _COLS], axis=1)
    att = np.concatenate([a["L0_gnn_a_src"], a["L0_gnn_a_dst"], a["L2_gnn_a_out"], a["L2_gnn_a_heads"].reshape(-1)])
    rows = np.stack([a["L1_gnn_bo"], a["L2_gnn_b2"], a["L2_gnn_ln_gamma"], a["L2_gnn_ln_beta"], a["L3_gnn_b"]])
    cols = np.stack([a[n].reshape(C, P).T for n in ("L1_gnn_bq", "L1_gnn_bk", "L1_gnn_bv", "L2_gnn_b1")], axis=1)
    arrays = {
        "x_n": x,
        "x_t": x.reshape(NG, G, P, C, P).transpose(0, 4, 3, 1, 2).reshape(NG, P, C * G * P),
        "weights": weights, "adj": a["adj"], "adj_t": a["adj"].T,
        "att_rows": np.broadcast_to(att, (P, att.size)), "rows": np.broadcast_to(rows, (P,) + rows.shape), "cols": cols,
    }
    nc = bacc.Bacc("TRN2", target_bir_lowering=False, num_devices=1)
    args, feed = [], {}
    for name, v in arrays.items():
        v = np.ascontiguousarray(v)
        feed[f"in_{name}"] = v
        args.append(nc.dram_tensor(f"in_{name}", v.shape, mybir.dt.from_np(v.dtype), kind="ExternalInput").ap())
    out = nc.dram_tensor("out_x", x.shape, F32, kind="ExternalOutput").ap()
    build(nc, *args, out)
    r = run_bass_kernel_spmd(nc, [feed], core_ids=[0])
    return r.results[0]["out_x"]
```
